# Optimizing a Trainium2 kernel written in Bass

```python
import numpy as np
import jax
import jax.numpy as jnp

def _softmax(x, axis=-1):
    return jax.nn.softmax(x, axis=axis)

def _gelu(x):
    return jax.nn.gelu(x, approximate=True)

def _silu(x):
    return jax.nn.silu(x)

def _sigmoid(x):
    return jax.nn.sigmoid(x)

def _layernorm(x, axis=-1, eps=1e-05):
    m = jnp.mean(x, axis=axis, keepdims=True)
    v = jnp.var(x, axis=axis, keepdims=True)
    return (x - m) / jnp.sqrt(v + eps)

def _scatter_add(tgt, idx, src, axis=0):
    return tgt.at[idx].add(src)

def _segment_sum(src, seg, n):
    return jax.ops.segment_sum(src, seg, n)
kernel_name = 'mk_decoder_preln_d1_seqx_r4_9d57a5'

def setup_inputs(seed: int=0):
    np.random.seed(seed)
    _w = jnp.asarray

    def _rec_inputs():
        import jax
        import jax.numpy as jnp
        _rk = jax.random.key(seed)
        x = -0.000125 + 0.9999 * jax.random.normal(jax.random.fold_in(_rk, 1), (8, 256, 1024), jnp.float32)
        _lenS = 256 - jax.random.randint(jax.random.fold_in(_rk, 7), (8,), 0, max(1, 256 // 4) + 1, jnp.int32)
        _lenS2 = 256 - jax.random.randint(jax.random.fold_in(_rk, 8), (8,), 0, max(1, 256 // 4) + 1, jnp.int32)
        _ctx_4096P = jax.random.normal(jax.random.fold_in(_rk, 11), (8, 16, 1024), jnp.float32)
        _ctx_4096c = jax.random.dirichlet(jax.random.fold_in(_rk, 511), 0.3 * jnp.ones((16,), jnp.float32), (8, 256))
        _ctx_4096t = jnp.einsum('bsk,bkd->bsd', _ctx_4096c, _ctx_4096P)
        _ctx_4096t = _ctx_4096t * jax.lax.rsqrt(jnp.mean(jnp.square(_ctx_4096t)) + 1e-12) * 0.953939
        ctx_4096 = -1.52775e-05 + 0.999936 * (_ctx_4096t + 0.3 * jax.random.normal(jax.random.fold_in(_rk, 611), (8, 256, 1024), jnp.float32))
        return (x, ctx_4096)
    x, ctx_4096 = _rec_inputs()

    def _L0_attn_setup():
        import jax, jax.numpy as jnp
        import numpy as np
        DEPTH, DIM, DFF, VOCAB = (4, 128, 512, 1024)
        EPS = 1e-05

        def layernorm(x, w, b):
            mu = jnp.mean(x, axis=-1, keepdims=True)
            var = jnp.mean((x - mu) ** 2, axis=-1, keepdims=True)
            return (x - mu) * jax.lax.rsqrt(var + EPS) * w + b

        def sconv(x, phazor_c, last_conv_c):
            B, L, D = x.shape
            r = jnp.abs(phazor_c)
            p = jnp.tanh(r) * jnp.exp(1j * jnp.angle(phazor_c))
            prog = p[None, :] ** jnp.arange(L, dtype=jnp.float32)[:, None]
            filt_fft = jnp.fft.fft(prog, n=2 * L, axis=0)
            x_fft = jnp.fft.fft(x.astype(jnp.complex64), n=2 * L, axis=1)
            conv = jnp.fft.ifft(filt_fft[None] * x_fft, axis=1)[:, :L]
            conv = conv + last_conv_c[None, None, :] * prog[None] * p[None, None, :]
            return conv.real.astype(x.dtype)

        def _forward(x, Win, bin, ln1_w, ln1_b, phz_re, phz_im, lc_re, lc_im, sc_lin, ln2_w, ln2_b, W1, b1, W2, b2, lnl_w, lnl_b, Wout, bout):
            h = jnp.einsum('blv,dv->bld', x, Win) + bin

            def body(h, p):
                l1w, l1b, pr, pi, lr, li, scl, l2w, l2b, w1, b1_, w2, b2_ = p
                y = jax.nn.silu(layernorm(h, l1w, l1b))
                y = sconv(y, pr + 1j * pi, lr + 1j * li)
                h = h + y * scl
                y = layernorm(h, l2w, l2b)
                y = jax.nn.silu(jnp.einsum('bld,fd->blf', y, w1) + b1_)
                y = jnp.einsum('blf,df->bld', y, w2) + b2_
                return (h + y, None)
            xs = (ln1_w, ln1_b, phz_re, phz_im, lc_re, lc_im, sc_lin, ln2_w, ln2_b, W1, b1, W2, b2)
            h, _ = jax.lax.scan(body, h, xs)
            h = layernorm(h, lnl_w, lnl_b)
            return jnp.einsum('bld,vd->blv', h, Wout) + bout
        key = jax.random.key(seed)
        ks = jax.random.split(key, 20)
        f32 = jnp.float32
        inp = {}
        inp['x'] = jax.random.normal(ks[0], (2, 1024, VOCAB), dtype=f32)
        inp['Win'] = jax.random.normal(ks[1], (DIM, VOCAB), dtype=f32) * VOCAB ** (-0.5)
        inp['bin'] = jnp.zeros((DIM,), f32)
        inp['ln1_w'] = jnp.ones((DEPTH, DIM), f32)
        inp['ln1_b'] = jnp.zeros((DEPTH, DIM), f32)
        ang = 2 * np.pi * jnp.arange(DIM, dtype=f32) / DIM
        mag = jnp.abs(jax.random.normal(ks[2], (DEPTH, DIM), dtype=f32))
        inp['phz_re'] = mag * jnp.cos(ang)[None]
        inp['phz_im'] = mag * jnp.sin(ang)[None]
        inp['lc_re'] = jax.random.normal(ks[3], (DEPTH, DIM), dtype=f32)
        inp['lc_im'] = jax.random.normal(ks[4], (DEPTH, DIM), dtype=f32)
        inp['sc_lin'] = jnp.ones((DEPTH, DIM), f32)
        inp['ln2_w'] = jnp.ones((DEPTH, DIM), f32)
        inp['ln2_b'] = jnp.zeros((DEPTH, DIM), f32)
        inp['W1'] = jax.random.normal(ks[5], (DEPTH, DFF, DIM), dtype=f32) * DIM ** (-0.5)
        inp['b1'] = jnp.zeros((DEPTH, DFF), f32)
        inp['W2'] = jax.random.normal(ks[6], (DEPTH, DIM, DFF), dtype=f32) * DFF ** (-0.5)
        inp['b2'] = jnp.zeros((DEPTH, DIM), f32)
        inp['lnl_w'] = jnp.ones((DIM,), f32)
        inp['lnl_b'] = jnp.zeros((DIM,), f32)
        inp['Wout'] = jax.random.normal(ks[7], (VOCAB, DIM), dtype=f32) * DIM ** (-0.5)
        inp['bout'] = jnp.zeros((VOCAB,), f32)
        return inp
    _L0_attn_all = _L0_attn_setup()
    _L0_attn_in = {k: v for k, v in _L0_attn_all.items() if k in ('Win', 'bin', 'ln1_w', 'ln1_b', 'phz_re', 'phz_im', 'lc_re', 'lc_im', 'sc_lin', 'ln2_w', 'ln2_b', 'W1', 'b1', 'W2', 'b2', 'lnl_w', 'lnl_b', 'Wout', 'bout')}
    del _L0_attn_all

    def _L0_xattn_setup():
        import jax, jax.numpy as jnp
        import numpy as np
        import math
        EPS = 1e-05
        LAMBDA = 0.6

        def _crucial_k(C):
            f = math.floor(LAMBDA * C)
            return f + f % 2

        def _conv1d(y, w):
            return jax.lax.conv_general_dilated(y, w, window_strides=(1,), padding=((3, 3),), dimension_numbers=('NCH', 'OIH', 'NCH'))

        def _norm_active(z, gamma, beta):
            mu = jnp.mean(z, axis=(0, 2), keepdims=True)
            var = jnp.mean((z - mu) ** 2, axis=(0, 2), keepdims=True)
            zn = (z - mu) * jax.lax.rsqrt(var + EPS)
            zn = zn * gamma.reshape(1, -1, 1) + beta.reshape(1, -1, 1)
            return jax.nn.sigmoid(jax.nn.relu(zn))
        key = jax.random.key(seed)
        k1, k2, k3 = jax.random.split(key, 3)
        B, C, L = (32, 64, 1024)
        x = jax.random.normal(k1, (B, C, L), dtype=jnp.float32)
        channel_map = jax.random.normal(k2, (B, C, L), dtype=jnp.float32)
        fan_in = 2 * 7
        bound = 1.0 / math.sqrt(fan_in)
        conv_w = jax.random.uniform(k3, (1, 2, 7), jnp.float32, -bound, bound)
        bn_gamma = jnp.ones((1,), jnp.float32)
        bn_beta = jnp.zeros((1,), jnp.float32)
        return {'x': x, 'channel_map': channel_map, 'conv_w': conv_w, 'bn_gamma': bn_gamma, 'bn_beta': bn_beta}
    _L0_xattn_all = _L0_xattn_setup()
    _L0_xattn_in = {k: v for k, v in _L0_xattn_all.items() if k in ('conv_w', 'bn_gamma', 'bn_beta')}
    del _L0_xattn_all

    def _L0_ffn_setup():
        import jax, jax.numpy as jnp
        import numpy as np
        TOP_K = 2
        key = jax.random.key(seed)
        k1, k2, k3 = jax.random.split(key, 3)
        B, S, H, O, E = (32, 1, 1024, 1024, 8)
        x = jax.random.normal(k1, (B, S, H), dtype=jnp.float32)
        gate_w = jax.random.normal(k2, (H, E), dtype=jnp.float32) * 0.02
        expert_w = jax.random.normal(k3, (E, H, O), dtype=jnp.float32) * 0.02
        return {'x': x, 'gate_w': gate_w, 'expert_w': expert_w}
    _L0_ffn_all = _L0_ffn_setup()
    _L0_ffn_in = {k: v for k, v in _L0_ffn_all.items() if k in ('gate_w', 'expert_w')}
    del _L0_ffn_all
    return {'x': x, 'ctx_4096': ctx_4096, 'L0_attn_Win': _L0_attn_in['Win'], 'L0_attn_bin': _L0_attn_in['bin'], 'L0_attn_ln1_w': _L0_attn_in['ln1_w'], 'L0_attn_ln1_b': _L0_attn_in['ln1_b'], 'L0_attn_phz_re': _L0_attn_in['phz_re'], 'L0_attn_phz_im': _L0_attn_in['phz_im'], 'L0_attn_lc_re': _L0_attn_in['lc_re'], 'L0_attn_lc_im': _L0_attn_in['lc_im'], 'L0_attn_sc_lin': _L0_attn_in['sc_lin'], 'L0_attn_ln2_w': _L0_attn_in['ln2_w'], 'L0_attn_ln2_b': _L0_attn_in['ln2_b'], 'L0_attn_W1': _L0_attn_in['W1'], 'L0_attn_b1': _L0_attn_in['b1'], 'L0_attn_W2': _L0_attn_in['W2'], 'L0_attn_b2': _L0_attn_in['b2'], 'L0_attn_lnl_w': _L0_attn_in['lnl_w'], 'L0_attn_lnl_b': _L0_attn_in['lnl_b'], 'L0_attn_Wout': _L0_attn_in['Wout'], 'L0_attn_bout': _L0_attn_in['bout'], 'L0_xattn_conv_w': _L0_xattn_in['conv_w'], 'L0_xattn_bn_gamma': _L0_xattn_in['bn_gamma'], 'L0_xattn_bn_beta': _L0_xattn_in['bn_beta'], 'L0_ffn_gate_w': _L0_ffn_in['gate_w'], 'L0_ffn_expert_w': _L0_ffn_in['expert_w']}

def reference(x, ctx_4096, L0_attn_Win, L0_attn_bin, L0_attn_ln1_w, L0_attn_ln1_b, L0_attn_phz_re, L0_attn_phz_im, L0_attn_lc_re, L0_attn_lc_im, L0_attn_sc_lin, L0_attn_ln2_w, L0_attn_ln2_b, L0_attn_W1, L0_attn_b1, L0_attn_W2, L0_attn_b2, L0_attn_lnl_w, L0_attn_lnl_b, L0_attn_Wout, L0_attn_bout, L0_xattn_conv_w, L0_xattn_bn_gamma, L0_xattn_bn_beta, L0_ffn_gate_w, L0_ffn_expert_w):
    import jax
    import jax.numpy as jnp

    def _L0_attn_ref(x, Win, bin, ln1_w, ln1_b, phz_re, phz_im, lc_re, lc_im, sc_lin, ln2_w, ln2_b, W1, b1, W2, b2, lnl_w, lnl_b, Wout, bout):
        import jax, jax.numpy as jnp
        import numpy as np
        DEPTH, DIM, DFF, VOCAB = (4, 128, 512, 1024)
        EPS = 1e-05

        def layernorm(x, w, b):
            mu = jnp.mean(x, axis=-1, keepdims=True)
            var = jnp.mean((x - mu) ** 2, axis=-1, keepdims=True)
            return (x - mu) * jax.lax.rsqrt(var + EPS) * w + b

        def sconv(x, phazor_c, last_conv_c):
            B, L, D = x.shape
            r = jnp.abs(phazor_c)
            p = jnp.tanh(r) * jnp.exp(1j * jnp.angle(phazor_c))
            prog = p[None, :] ** jnp.arange(L, dtype=jnp.float32)[:, None]
            filt_fft = jnp.fft.fft(prog, n=2 * L, axis=0)
            x_fft = jnp.fft.fft(x.astype(jnp.complex64), n=2 * L, axis=1)
            conv = jnp.fft.ifft(filt_fft[None] * x_fft, axis=1)[:, :L]
            conv = conv + last_conv_c[None, None, :] * prog[None] * p[None, None, :]
            return conv.real.astype(x.dtype)

        def _forward(x, Win, bin, ln1_w, ln1_b, phz_re, phz_im, lc_re, lc_im, sc_lin, ln2_w, ln2_b, W1, b1, W2, b2, lnl_w, lnl_b, Wout, bout):
            h = jnp.einsum('blv,dv->bld', x, Win) + bin

            def body(h, p):
                l1w, l1b, pr, pi, lr, li, scl, l2w, l2b, w1, b1_, w2, b2_ = p
                y = jax.nn.silu(layernorm(h, l1w, l1b))
                y = sconv(y, pr + 1j * pi, lr + 1j * li)
                h = h + y * scl
                y = layernorm(h, l2w, l2b)
                y = jax.nn.silu(jnp.einsum('bld,fd->blf', y, w1) + b1_)
                y = jnp.einsum('blf,df->bld', y, w2) + b2_
                return (h + y, None)
            xs = (ln1_w, ln1_b, phz_re, phz_im, lc_re, lc_im, sc_lin, ln2_w, ln2_b, W1, b1, W2, b2)
            h, _ = jax.lax.scan(body, h, xs)
            h = layernorm(h, lnl_w, lnl_b)
            return jnp.einsum('bld,vd->blv', h, Wout) + bout
        return _forward(x, Win, bin, ln1_w, ln1_b, phz_re, phz_im, lc_re, lc_im, sc_lin, ln2_w, ln2_b, W1, b1, W2, b2, lnl_w, lnl_b, Wout, bout)

    def _L0_xattn_ref(x, channel_map, conv_w, bn_gamma, bn_beta):
        import jax, jax.numpy as jnp
        import numpy as np
        import math
        EPS = 1e-05
        LAMBDA = 0.6

        def _crucial_k(C):
            f = math.floor(LAMBDA * C)
            return f + f % 2

        def _conv1d(y, w):
            return jax.lax.conv_general_dilated(y, w, window_strides=(1,), padding=((3, 3),), dimension_numbers=('NCH', 'OIH', 'NCH'))

        def _norm_active(z, gamma, beta):
            mu = jnp.mean(z, axis=(0, 2), keepdims=True)
            var = jnp.mean((z - mu) ** 2, axis=(0, 2), keepdims=True)
            zn = (z - mu) * jax.lax.rsqrt(var + EPS)
            zn = zn * gamma.reshape(1, -1, 1) + beta.reshape(1, -1, 1)
            return jax.nn.sigmoid(jax.nn.relu(zn))
        B, C, L = x.shape
        k = _crucial_k(C)
        cm = jnp.moveaxis(channel_map, 1, 2)
        _, topk_idx = jax.lax.top_k(cm, k)
        b_idx = jnp.arange(B)[:, None, None]
        l_idx = jnp.arange(L)[None, :, None]
        mask = jnp.zeros((B, L, C), x.dtype).at[b_idx, l_idx, topk_idx].set(1.0)
        crucial_channels = jnp.moveaxis(mask, 2, 1)
        subcrucial_channels = 1.0 - crucial_channels
        crucial_features = crucial_channels * x
        subcrucial_features = subcrucial_channels * x
        c_max = jnp.max(crucial_features, axis=1, keepdims=True)
        c_avg = jnp.mean(crucial_features, axis=1, keepdims=True) * (C / k)
        s_max = jnp.max(subcrucial_features, axis=1, keepdims=True)
        s_avg = jnp.mean(subcrucial_features, axis=1, keepdims=True) * (C / (C - k))
        crucial_x = jnp.concatenate([c_max, c_avg], axis=1)
        subcrucial_x = jnp.concatenate([s_max, s_avg], axis=1)
        A_S1 = _norm_active(_conv1d(crucial_x, conv_w), bn_gamma, bn_beta)
        A_S2 = _norm_active(_conv1d(subcrucial_x, conv_w), bn_gamma, bn_beta)
        return crucial_features * A_S1 + subcrucial_features * A_S2

    def _L0_ffn_ref(x, gate_w, expert_w):
        import jax, jax.numpy as jnp
        import numpy as np
        TOP_K = 2
        E = expert_w.shape[0]
        gate_logits = jnp.einsum('bsh,he->bse', x, gate_w)
        top_vals, top_idx = jax.lax.top_k(gate_logits, TOP_K)
        probs = jax.nn.softmax(top_vals, axis=-1)
        onehot = jax.nn.one_hot(top_idx, E, dtype=x.dtype)
        w_e = jnp.einsum('bsk,bske->bse', probs, onehot)
        expert_out = jnp.einsum('bsh,eho->bseo', x, expert_w)
        out = jnp.einsum('bseo,bse->bso', expert_out, w_e)
        return out
    x = x + _L0_attn_ref(_layernorm(x, axis=-1), L0_attn_Win, L0_attn_bin, L0_attn_ln1_w, L0_attn_ln1_b, L0_attn_phz_re, L0_attn_phz_im, L0_attn_lc_re, L0_attn_lc_im, L0_attn_sc_lin, L0_attn_ln2_w, L0_attn_ln2_b, L0_attn_W1, L0_attn_b1, L0_attn_W2, L0_attn_b2, L0_attn_lnl_w, L0_attn_lnl_b, L0_attn_Wout, L0_attn_bout)
    x = x + _L0_xattn_ref(_layernorm(x, axis=-1), ctx_4096, L0_xattn_conv_w, L0_xattn_bn_gamma, L0_xattn_bn_beta)
    x = x + _L0_ffn_ref(_layernorm(x, axis=-1), L0_ffn_gate_w, L0_ffn_expert_w)
    return x

_drawn_inputs = setup_inputs


def setup_inputs(seed=0):
    import zlib

    import numpy as np

    out = dict(_drawn_inputs(seed))
    spreads = {'L0_attn_bin': (0.0, 0.1),
     'L0_attn_ln1_w': (1.0, 0.2),
     'L0_attn_ln1_b': (0.0, 0.1),
     'L0_attn_sc_lin': (1.0, 0.2),
     'L0_attn_ln2_w': (1.0, 0.2),
     'L0_attn_ln2_b': (0.0, 0.1),
     'L0_attn_b1': (0.0, 0.1),
     'L0_attn_b2': (0.0, 0.1),
     'L0_attn_lnl_w': (1.0, 0.2),
     'L0_attn_lnl_b': (0.0, 0.1),
     'L0_attn_bout': (0.0, 0.1)}
    factors = {}
    for name, (base, spread) in spreads.items():
        noise = np.random.default_rng([zlib.crc32(name.encode()), seed]).standard_normal(out[name].shape)
        drawn = base * np.exp(spread * noise) if base else spread * noise
        out[name] = jnp.asarray(drawn.astype(out[name].dtype))
    for name, factor in factors.items():
        out[name] = (out[name] * factor).astype(out[name].dtype)
    return out
```

```python
from contextlib import ExitStack

import concourse.bass as bass
from concourse import mybir

F32 = mybir.dt.float32
I32 = mybir.dt.int32
U32 = mybir.dt.uint32
BF16 = mybir.dt.bfloat16

ALU = mybir.AluOpType
ACT = mybir.ActivationFunctionType
AX = mybir.AxisListType
ds = bass.ds

P = 128
BANK = 512
EPS = 1e-5
FLT_MAX = 3.4028234663852886e38
LAMBDA = 0.6


def crucial_count(c):
    f = int(LAMBDA * c // 1)
    return f + f % 2


def decoder_kernel(nc, x, ctx_map, w_in, b_in, ln1_w, ln1_b, phz_re, phz_im, lc_re, lc_im, sc_lin, ln2_w, ln2_b,
                   w1, b1, w2, b2, lnl_w, lnl_b, w_out, b_out, conv_w, bn_gamma, bn_beta, gate_w, expert_w, out):
    B, S, D = x.shape
    DM = w_in.shape[0]
    NL = ln1_w.shape[0]
    FF = w1.shape[1]
    E = gate_w.shape[1]
    N = B * S
    NT = N // P
    KD = D // P
    FT = FF // P
    CW = BANK
    CH = N // CW
    TPC = CW // P
    BPC = CW // S
    CT = S // P
    KC = crucial_count(S)
    KS = S - KC
    ROUNDS = -(-KS // 8)
    PADS = ROUNDS * 8 - KS
    SLOTS = 2 * N // P + E - 1
    UNR = 3
    TAPS = conv_w.shape[2]
    HALF = TAPS // 2
    assert DM == P and SLOTS % UNR == 0 and D == 2 * BANK

    x2d = x.rearrange("b s d -> (b s) d")
    x_nrm = nc.dram_tensor("x_nrm", [N, D], F32, kind="Internal").ap()

    ctx = ExitStack()
    with ctx:
        def sb(name, shape, dt=F32):
            return ctx.enter_context(nc.sbuf_tensor(name, shape, dt))

        def sem(name):
            return ctx.enter_context(nc.semaphore(name))

        X = sb("X", [P, NT, D])
        Xf = X[:, :, :].rearrange("p t d -> p (t d)")
        T = sb("T", [P, KD, N])
        Tf = T[:, :, :].rearrange("p k n -> p (k n)")
        M = sb("M", [P, KD, N], mybir.dt.bfloat16)
        H = sb("H", [P, N])
        nat = sb("nat", [P, TPC, D])
        natf = nat[:, :, :].rearrange("p u d -> p (u d)")
        fin = sb("fin", [P, 2, CW])
        bank = [ctx.enter_context(nc.psum_tensor(f"bank{i}", [P, BANK], F32)) for i in range(8)]

        ident = sb("ident", [P, P])
        ones = sb("ones", [P, P])
        utri = sb("utri", [P, P])
        center = sb("center", [P, P])
        inv_col = sb("inv_col", [P, 1])
        neg_half = sb("neg_half", [P, NT])
        pos_half = sb("pos_half", [P, NT])
        late = sb("late", [P, 2 * D])
        wout_t, bout_b = late[:, 0:D], late[:, D:2 * D]
        gate = sb("gate", [P, KD, E])
        convw = sb("convw", [P, 2 * TAPS])
        bn_gb = sb("bn_gb", [P, 2])
        ewide = sb("ewide", [P, 3 * P + TAPS - 1])
        band = sb("band", [P, 2, 3 * P])
        layer_par = sb("layer_par", [P, NL, 13])
        block_par = sb("block_par", [P, 4])
        cur = sb("cur", [P, 13])
        st6 = sb("st6", [P, TPC, 12])
        mv = sb("mv", [P, TPC, 2])
        ve = sb("ve", [P, TPC, 4])
        rs = sb("rs", [P, TPC, 4])

        o = 8192

        def in_t(n):
            nonlocal o
            o += n
            return Tf[:, o - n:o]

        cos_t = in_t(NL * S).rearrange("p (l s) -> p l s", l=NL)
        sin_t = in_t(NL * S).rearrange("p (l s) -> p l s", l=NL)
        win_t = in_t(D).rearrange("p (k m) -> p k m", k=KD)
        w1raw = in_t(FF).rearrange("p (t m) -> p t m", t=FT)
        w2raw = in_t(FF)
        w1u = in_t(FF)
        w1s = in_t(FF)
        w2c = in_t(FF).rearrange("p (t m) -> p t m", t=FT)
        cs = in_t(P)
        b1f = in_t(FT)
        rows = in_t(P)
        ph = in_t(4 * NL).rearrange("p (k l) -> p k l", k=4)
        tmp = in_t(16 * NL).rearrange("p (k l) -> p k l", k=16)
        tab = in_t(4 * NL * S // 2).rearrange("p (k l s) -> p k l s", k=4, l=NL)
        assert o <= KD * N

        LN1W, LN1B, SCL, LN2W, LN2B, B2, B1, RHO, UR0, UI0 = 0, 1, 2, 3, 4, 5, 6, 10, 11, 12

        iota_lane = sb("iota_lane", [P, P])
        iota_slot = sb("iota_slot", [P, SLOTS])
        rev_e = sb("rev_e", [P, NT, E])
        step_t = sb("step_t", [P, E, NT])
        later_t = sb("later_t", [P, E * NT])
        tok1 = sb("tok1", [P, NT])
        spare = sb("spare", [P, 1])

        ld_rows = sem("ld_rows")
        ld_win = sem("ld_win")
        ld_wout = sem("ld_wout")
        ld_misc = sem("ld_misc")
        const_ready = sem("const_ready")
        set_pe = sem("set_pe")
        set_act = sem("set_act")
        set_dve = sem("set_dve")
        set_pool = sem("set_pool")
        NCONST = 9
        NIOTA = 6
        io = Xf[:, 0:1024].bitcast(I32)
        io_lane, io_slot = io[:, 0:P], io[:, 128:128 + SLOTS]
        io_rev = io[:, 256:384].rearrange("p (t e) -> p t e", e=E)
        io_step = io[:, 384:512].rearrange("p (e t) -> p e t", e=E)
        io_tok, io_spare = io[:, 512:528], io[:, 528:529]

        with nc.Block() as block:
            @block.sync
            def _(sp):
                for k, par in enumerate([ln1_w, ln1_b, sc_lin, ln2_w, ln2_b, b2, phz_re, phz_im, lc_re, lc_im]):
                    sp.dma_start(rows[k * NL:(k + 1) * NL, :], par[:, :]).then_inc(ld_rows, 16)
                sp.dma_start(rows[40:56, :], b1.rearrange("l (t p) -> (l t) p", p=P)).then_inc(ld_rows, 16)
                for k, par in enumerate([b_in, lnl_w, lnl_b]):
                    sp.dma_start(rows[56 + k:57 + k, :], par.rearrange("(a d) -> a d", a=1)).then_inc(ld_rows, 16)
                sp.dma_start(nat[:, 0, :], w_in[:, :]).then_inc(ld_win, 16)
                sp.dma_start(nat[:, 1, :].rearrange("p (t d) -> p t d", t=KD),
                             w_out.rearrange("(t p) d -> p t d", p=P)).then_inc(ld_wout, 16)
                sp.dma_start(bout_b, b_out.rearrange("(a d) -> a d", a=1).to_broadcast([P, D])).then_inc(ld_misc, 16)
                sp.dma_start(convw[:, :], conv_w.rearrange("a c j -> a (c j)").to_broadcast([P, 2 * TAPS])).then_inc(ld_misc, 16)
                sp.dma_start(bn_gb[:, 0:1], bn_gamma.rearrange("(a d) -> a d", a=1).to_broadcast([P, 1])).then_inc(ld_misc, 16)
                sp.dma_start(bn_gb[:, 1:2], bn_beta.rearrange("(a d) -> a d", a=1).to_broadcast([P, 1])).then_inc(ld_misc, 16)
                sp.dma_start(gate[:, :, :], gate_w.rearrange("(k p) e -> p k e", p=P)).then_inc(ld_misc, 16)
                sp.wait_ge(ld_misc, 5 * 16)

            @block.gpsimd
            def _(pool):
                g = nc.gpsimd
                g.memset(ident[:, :], 0.0).then_inc(const_ready, 1)
                g.memset(ones[:, :], 1.0).then_inc(const_ready, 1)
                g.memset(ewide[:, :], 0.0).then_inc(const_ready, 1)
                g.memset(inv_col[:, :], 1.0 / P).then_inc(const_ready, 1)
                g.memset(neg_half[:, :], -0.5).then_inc(const_ready, 1)
                g.memset(pos_half[:, :], 0.5).then_inc(const_ready, 1)
                pool.wait_ge(const_ready, 6)
                g.affine_select(out=ident[:, :], in_=ident[:, :], compare_op=ALU.not_equal, fill=1.0, base=0,
                                pattern=[[-1, P]], channel_multiplier=1).then_inc(const_ready, 1)
                g.affine_select(out=utri[:, :], in_=ones[:, :], compare_op=ALU.is_gt, fill=0.0, base=0,
                                pattern=[[1, P]], channel_multiplier=-1).then_inc(const_ready, 1)
                g.affine_select(out=ewide[:, :], in_=ewide[:, :], compare_op=ALU.not_equal, fill=1.0, base=-(P + HALF),
                                pattern=[[1, 3 * P + TAPS - 1]], channel_multiplier=-1).then_inc(const_ready, 1)
                g.iota(io_lane, [[1, P]], base=0, channel_multiplier=0).then_inc(const_ready, 1)
                g.iota(io_slot, [[1, SLOTS]], base=0, channel_multiplier=0).then_inc(const_ready, 1)
                g.iota(io_rev, [[0, NT], [-1, E]], base=E, channel_multiplier=0).then_inc(const_ready, 1)
                g.iota(io_step, [[0, E], [P, NT]], base=0, channel_multiplier=0).then_inc(const_ready, 1)
                g.iota(io_tok, [[P, NT]], base=1, channel_multiplier=1).then_inc(const_ready, 1)
                g.iota(io_spare, [[0, 1]], base=N + 1, channel_multiplier=1).then_inc(const_ready, 1)
                pool.wait_ge(set_dve, 17)
                g.tensor_tensor(tmp[:, 8, :], tmp[:, 6, :], pos_half[:, 0:NL], ALU.pow).then_inc(set_pool, 1)
                g.tensor_tensor(tmp[:, 9, :], tmp[:, 6, :], neg_half[:, 0:NL], ALU.pow).then_inc(set_pool, 1)

            @block.tensor
            def _(pe):
                pe.wait_ge(const_ready, NCONST)
                pe.wait_ge(ld_rows, 14 * 16)
                nc.tensor.transpose(bank[0][:, 0:59], rows[0:59, :], ident[0:59, 0:59]).then_inc(set_pe, 1)
                pe.wait_ge(ld_wout, 16)
                for t in range(KD):
                    mm = nc.tensor.transpose(bank[2 + t // 4][:, (t % 4) * P:(t % 4 + 1) * P],
                                             nat[:, 1, t * P:(t + 1) * P], ident[:, :])
                mm.then_inc(set_pe, 1)
                pe.wait_ge(set_dve, 4)
                nc.tensor.matmul(bank[1][:, 0:NL], center[:, :], layer_par[:, :, B2], start=True, stop=True)
                nc.tensor.matmul(bank[1][:, NL:NL + 1], center[:, :], block_par[:, 0:1],
                                 start=True, stop=True).then_inc(set_pe, 1)
                pe.wait_ge(ld_win, 16)
                for t in range(KD):
                    mm = nc.tensor.matmul(bank[4 + t // 4][:, (t % 4) * P:(t % 4 + 1) * P],
                                          nat[:, 0, t * P:(t + 1) * P], center[:, :], start=True, stop=True)
                mm.then_inc(set_pe, 1)
                pe.wait_ge(set_act, 2)
                for n in range(2):
                    mm = nc.tensor.matmul(bank[6 + n][:, :], block_par[:, 2:3].to_broadcast([P, P]),
                                          nat[:, 2, n * BANK:(n + 1) * BANK], start=True, stop=True)
                mm.then_inc(set_pe, 1)

            @block.scalar
            def _(act):
                act.wait_ge(set_pe, 2)
                for n in range(2):
                    nc.scalar.copy(nat[:, 2, n * BANK:(n + 1) * BANK], bank[2 + n][:, :]).then_inc(set_act, 1)
                act.wait_ge(set_pe, 4)
                for n in range(2):
                    nc.scalar.copy(win_t[:, 4 * n:4 * n + 4, :].rearrange("p k m -> p (k m)"), bank[4 + n][:, :]).then_inc(set_act, 1)
                act.wait_ge(set_dve, 18)
                nc.scalar.activation(layer_par[:, :, RHO], tmp[:, 10, :], ACT.Tanh).then_inc(set_act, 1)

            @block.vector
            def _(dve):
                v = nc.vector
                n_link = [0]

                def link(ins):
                    n_link[0] += 1
                    ins.then_inc(set_dve, 1)
                    dve.wait_ge(set_dve, n_link[0])

                dve.wait_ge(const_ready, NCONST)
                link(v.tensor_scalar(center[:, :], ident[:, :], -1.0 / P, None, ALU.add))
                dve.wait_ge(set_pe, 1)
                link(v.tensor_copy(layer_par[:, :, 0:6], bank[0][:, 0:24].rearrange("p (k l) -> p l k", k=6)))
                link(v.tensor_copy(layer_par[:, :, B1:B1 + FT], bank[0][:, 40:56].rearrange("p (l t) -> p l t", l=NL)))
                link(v.tensor_copy(block_par[:, 0:3], bank[0][:, 56:59]))
                link(v.tensor_copy(ph[:, :, :], bank[0][:, 24:40].rearrange("p (k l) -> p k l", k=4)))
                re, im, lr, li = (ph[:, k, :] for k in range(4))
                t_re, t_im, t_max, t_inv, t_a, t_b, t_q, t_z, t_sq, t_rsq, t_r, c_m, s_m, t_c, t_s = (tmp[:, k, :] for k in range(15))
                link(v.scalar_tensor_tensor(t_re, re, -1.0, re, ALU.mult, ALU.max))
                link(v.scalar_tensor_tensor(t_im, im, -1.0, im, ALU.mult, ALU.max))
                link(v.tensor_tensor(t_max, t_re, t_im, ALU.max))
                link(v.tensor_scalar(t_inv, t_max, 1e-37, None, ALU.max))
                link(v.reciprocal(t_inv, t_inv))
                link(v.tensor_tensor(t_a, re, t_inv, ALU.mult))
                link(v.tensor_tensor(t_b, im, t_inv, ALU.mult))
                link(v.tensor_scalar(t_z, t_max, 0.0, None, ALU.is_equal))
                link(v.tensor_tensor(t_a, t_a, t_z, ALU.add))
                link(v.tensor_tensor(t_c, t_a, t_a, ALU.mult))
                link(v.tensor_tensor(t_s, t_b, t_b, ALU.mult))
                link(v.tensor_tensor(t_q, t_c, t_s, ALU.add))
                dve.wait_ge(set_pool, 2)
                link(v.tensor_tensor(t_r, t_max, t_sq, ALU.mult))
                assert n_link[0] == 18
                link(v.tensor_tensor(c_m, t_a, t_rsq, ALU.mult))
                link(v.tensor_tensor(s_m, t_b, t_rsq, ALU.mult))
                link(v.tensor_tensor(t_re, lr, c_m, ALU.mult))
                link(v.tensor_tensor(t_im, li, s_m, ALU.mult))
                link(v.tensor_tensor(layer_par[:, :, UR0], t_re, t_im, ALU.subtract))
                link(v.tensor_tensor(t_re, lr, s_m, ALU.mult))
                link(v.tensor_tensor(t_im, li, c_m, ALU.mult))
                link(v.tensor_tensor(t_re, t_re, t_im, ALU.add))
                link(v.tensor_scalar(layer_par[:, :, UI0], t_re, -1.0, None, ALU.mult))
                link(v.memset(cos_t[:, :, 0:1], 1.0))
                link(v.memset(sin_t[:, :, 0:1], 0.0))
                m = 1
                while m < S:
                    cb = c_m.unsqueeze(2).to_broadcast([P, NL, m])
                    sb_ = s_m.unsqueeze(2).to_broadcast([P, NL, m])
                    link(v.tensor_tensor(tab[:, 0, :, 0:m], cos_t[:, :, 0:m], cb, ALU.mult))
                    link(v.tensor_tensor(tab[:, 1, :, 0:m], sin_t[:, :, 0:m], sb_, ALU.mult))
                    link(v.tensor_tensor(tab[:, 2, :, 0:m], sin_t[:, :, 0:m], cb, ALU.mult))
                    link(v.tensor_tensor(tab[:, 3, :, 0:m], cos_t[:, :, 0:m], sb_, ALU.mult))
                    link(v.tensor_tensor(cos_t[:, :, m:2 * m], tab[:, 0, :, 0:m], tab[:, 1, :, 0:m], ALU.subtract))
                    link(v.tensor_tensor(sin_t[:, :, m:2 * m], tab[:, 2, :, 0:m], tab[:, 3, :, 0:m], ALU.add))
                    link(v.tensor_tensor(t_c, c_m, c_m, ALU.mult))
                    link(v.tensor_tensor(t_s, s_m, s_m, ALU.mult))
                    link(v.tensor_tensor(t_q, c_m, s_m, ALU.mult))
                    link(v.tensor_tensor(c_m, t_c, t_s, ALU.subtract))
                    link(v.tensor_scalar(s_m, t_q, 2.0, None, ALU.mult))
                    m *= 2
                dve.wait_ge(set_pe, 3)
                link(v.tensor_copy(layer_par[:, :, B2], bank[1][:, 0:NL]))
                link(v.tensor_copy(block_par[:, 0:1], bank[1][:, NL:NL + 1]))
                dve.wait_ge(set_act, 2)
                for n in range(2):
                    link(v.tensor_scalar(wout_t[:, n * BANK:(n + 1) * BANK], bank[2 + n][:, :], block_par[:, 1:2], None, ALU.mult))
                dve.wait_ge(set_pe, 5)
                dve.wait_ge(ld_misc, 5 * 16)
                for n in range(2):
                    link(v.tensor_tensor(bout_b[:, n * BANK:(n + 1) * BANK], bank[6 + n][:, :],
                                         bout_b[:, n * BANK:(n + 1) * BANK], ALU.add))
                for c in range(2):
                    link(v.tensor_scalar(band[:, c, :], ewide[:, 0:3 * P], convw[:, c * TAPS:c * TAPS + 1], None, ALU.mult))
                    for j in range(1, TAPS):
                        w = convw[:, c * TAPS + j:c * TAPS + j + 1]
                        link(v.scalar_tensor_tensor(band[:, c, :], ewide[:, j:j + 3 * P], w, band[:, c, :], ALU.mult, ALU.add))
                dve.wait_ge(const_ready, NCONST + NIOTA)
                link(v.tensor_copy(iota_lane[:, :], io_lane))
                link(v.tensor_copy(iota_slot[:, :], io_slot))
                link(v.tensor_copy(rev_e[:, :, :], io_rev))
                link(v.tensor_copy(step_t[:, :, :], io_step))
                link(v.tensor_copy(tok1[:, :], io_tok))
                link(v.tensor_copy(spare[:, :], io_spare))
                link(v.tensor_scalar(later_t[:, :], step_t[:, :, :].rearrange("p e t -> p (e t)"), 0.0, None, ALU.is_gt))

        held = sem("held")

        def hold(eng, done, n):
            eng.wait_ge(done, n)
            eng.sem_inc(held, 1)

        GT = 2 * KD
        NG = B // 2
        QUICK = 2
        WINDOW = 8 * QUICK
        WK = WINDOW + S
        LOW, HIGH = -0.5, 0.0
        AIM = KS - WINDOW / 2 + 0.5
        AIM_S = 2 * AIM - S
        cT = Xf.rearrange("p (b k s) -> p b k s", b=B, k=KD)
        cin = nat[:, :, :].rearrange("p (u h) l -> p u h l", u=2)
        w = Tf[:, 0:GT * WK].rearrange("p (i s) -> p i s", i=GT)
        under = Tf[:, GT * WK:GT * WK + GT * S // 2].bitcast(BF16).rearrange("p (i s) -> p i s", i=GT)
        signs = H[:, :].bitcast(BF16).rearrange("p (i s) -> p i s", i=GT)
        so = GT * WK + GT * S // 2

        def in_sel(*shape):
            nonlocal so
            n = 1
            for d in shape:
                n *= d
            so += n
            assert so <= 8192
            names = "abc"[:len(shape)]
            return Tf[:, so - n:so].rearrange(f"p ({' '.join(names)}) -> p {' '.join(names)}", **dict(zip(names, shape)))

        st_c, mv_c = in_sel(GT, 6), in_sel(GT, 2)
        dev, t_lo, t_hi, width, t_1, t_2, s_lo, s_hi, s_1, rise, inv, miss, side, step = (in_sel(GT) for _ in range(14))
        c_low, c_width, c_one, c_aim, c_inv = (in_sel(GT) for _ in range(5))
        m_cnt, off = in_sel(GT), in_sel(GT)
        top8 = in_sel(GT, 8)
        pad01 = w[:, :, 0:WINDOW]
        pad_neg = in_sel(GT, WINDOW)
        off_max, off_any, off_one = in_sel(NG), in_sel(1), in_sel(1)
        off_i = in_sel(1).bitcast(I32)
        ctx_in = [sem(f"ctx_in{u}") for u in range(2)]
        ctx_tp, ctx_set, c_stat, c_mean, sel_pool = (sem(n) for n in ("ctx_tp", "ctx_set", "c_stat", "c_mean", "sel_pool"))
        t0_set, s0_sum, t1_set, s1_sum, t2_set, counted, sel_small, w_set = (sem(n) for n in (
            "t0_set", "s0_sum", "t1_set", "s1_sum", "t2_set", "counted", "sel_small", "w_set"))
        round_max, round_rep, mask_done, off_set, off_mm = (sem(n) for n in ("round_max", "round_rep", "mask_done", "off_set", "off_mm"))

        with nc.Block() as block:
            @block.sync
            def _(sp):
                sp.sem_inc(ctx_tp, 4 * 2)
                with sp.Fori(0, NG) as g:
                    for u in range(2):
                        sp.wait_ge(ctx_tp, g * 8 + 4 * u + 4)
                        sp.dma_start(cin[:, u, :, :], ctx_map[ds(g * 2 + u, 1), :, :].rearrange("a (h p) l -> p (a h) l", p=P)).then_inc(ctx_in[u], 16)

            @block.tensor
            def _(pe):
                with pe.Fori(0, NG) as g:
                    for u in range(2):
                        pe.wait_ge(ctx_in[u], g * 16 + 16)
                        for j in range(4):
                            pe.wait_ge(ctx_set, g * 8 + 4 * u + j + 1)
                            for k in (2 * j, 2 * j + 1):
                                for h in range(CT):
                                    mm = nc.tensor.transpose(bank[4 * u + j][:, (k % 2) * S + h * P:(k % 2) * S + (h + 1) * P],
                                                             cin[:, u, h, k * P:(k + 1) * P], ident[:, :])
                            mm.then_inc(ctx_tp, 1)
                pe.wait_ge(off_set, 1)
                nc.tensor.matmul(bank[0][:, 0:1], ones[:, :], off_any[:, 0:1], start=True, stop=True).then_inc(off_mm, 1)

            @block.scalar
            def _(act):
                a = nc.scalar
                act.sem_inc(ctx_set, 8)
                with act.Fori(0, NG) as g:
                    for u in range(2):
                        for j in range(4):
                            act.wait_ge(ctx_tp, g * 8 + 4 * u + j + 9)
                            a.copy(cT[:, ds(g * 2 + u, 1), 2 * j:2 * j + 2, :].rearrange("p a k s -> p (a k) s"),
                                   bank[4 * u + j][:, :].rearrange("p (k s) -> p k s", k=2)[:, :, ::-1]).then_inc(ctx_set, 1)
                    hold(act, t0_set, g + 1)
                    for n, (thr, sums_) in enumerate(((t_lo, s_lo), (t_hi, s_hi))):
                        if n == 1:
                            hold(act, s0_sum, g * (2 * GT) + GT)
                        for i in range(GT):
                            a.activation(signs[:, i, :], cT[:, ds(g * 2 + i // KD, 1), i % KD, :].rearrange("p a s -> p (a s)"), ACT.Sign,
                                               scale=-1.0, bias=thr[:, i:i + 1], accum_out=sums_[:, i:i + 1]).then_inc(s0_sum, 1)
                    hold(act, t1_set, g + 1)
                    for i in range(GT):
                        a.activation(signs[:, i, :], cT[:, ds(g * 2 + i // KD, 1), i % KD, :].rearrange("p a s -> p (a s)"), ACT.Sign,
                                     scale=-1.0, bias=t_1[:, i:i + 1], accum_out=s_1[:, i:i + 1]).then_inc(s1_sum, 1)

            @block.gpsimd
            def _(pool):
                g_ = nc.gpsimd
                n_chain = 29
                for dst, val in ((c_low, LOW), (c_width, HIGH - LOW), (c_one, 1.0), (c_aim, AIM_S), (c_inv, -1.0)):
                    ins = g_.memset(dst, val)
                ins.then_inc(sel_pool, 1)
                with pool.Fori(0, NG) as g:
                    n_link = [0]

                    def chain(dst, a, b, op, done=None):
                        pool.wait_ge(sel_pool, g * n_chain + n_link[0] + 1)
                        g_.tensor_tensor(dst, a, b, op).then_inc(sel_pool, 1)
                        n_link[0] += 1

                    pool.wait_ge(c_mean, g * GT + GT)
                    chain(dev, mv_c[:, :, 1], pos_half[:, 0:GT], ALU.pow)
                    chain(t_lo, dev, c_low, ALU.mult)
                    chain(t_lo, t_lo, mv_c[:, :, 0], ALU.add)
                    chain(width, dev, c_width, ALU.mult)
                    chain(t_hi, t_lo, width, ALU.add)
                    pool.wait_ge(sel_pool, g * n_chain + n_link[0] + 1)
                    pool.sem_inc(t0_set, 1)
                    pool.wait_ge(s0_sum, g * (2 * GT) + 2 * GT)
                    chain(rise, s_hi, s_lo, ALU.subtract)
                    chain(inv, rise, rise, ALU.mult)
                    chain(inv, inv, c_one, ALU.add)
                    chain(inv, inv, c_inv, ALU.pow)
                    chain(inv, inv, rise, ALU.mult)
                    chain(miss, c_aim, s_lo, ALU.subtract)
                    chain(miss, miss, width, ALU.mult)
                    chain(miss, miss, inv, ALU.mult)
                    chain(t_1, t_lo, miss, ALU.add)
                    pool.wait_ge(sel_pool, g * n_chain + n_link[0] + 1)
                    pool.sem_inc(t1_set, 1)
                    pool.wait_ge(s1_sum, g * GT + GT)
                    hold(pool, sel_pool, g * n_chain + n_link[0] + 1)
                    g_.tensor_scalar(side, s_1, AIM_S, None, ALU.is_le).then_inc(sel_pool, 1)
                    n_link[0] += 1
                    chain(rise, rise, side, ALU.mult)
                    chain(rise, rise, s_lo, ALU.add)
                    chain(rise, rise, s_1, ALU.subtract)
                    chain(width, width, side, ALU.mult)
                    chain(width, width, t_lo, ALU.add)
                    chain(width, width, t_1, ALU.subtract)
                    chain(inv, rise, rise, ALU.mult)
                    chain(inv, inv, c_one, ALU.add)
                    chain(inv, inv, c_inv, ALU.pow)
                    chain(rise, rise, inv, ALU.mult)
                    chain(rise, rise, width, ALU.mult)
                    chain(miss, c_aim, s_1, ALU.subtract)
                    chain(miss, miss, rise, ALU.mult)
                    pool.wait_ge(counted, g * GT + 1)
                    chain(t_2, t_1, miss, ALU.add)
                    pool.wait_ge(sel_pool, g * n_chain + n_link[0] + 1)
                    pool.sem_inc(t2_set, 1)
                    assert n_link[0] == n_chain, n_link

            @block.vector
            def _(dve):
                v = nc.vector

                def stats(g):
                    for i in range(GT):
                        if i % 2 == 0:
                            hold(dve, ctx_set, g * 8 + i // 2 + 9)
                        v.bn_stats(st_c[:, i, :], cT[:, ds(g * 2 + i // KD, 1), i % KD, :].rearrange("p a s -> p (a s)")).then_inc(c_stat, 1)
                    for i in range(GT):
                        hold(dve, c_stat, g * GT + i + 1)
                        v.bn_aggr(mv_c[:, i, :], st_c[:, i, :]).then_inc(c_mean, 1)

                def take(n_before, pads):
                    for done, gate_, go in ((round_max, round_rep, lambda i: v.max(top8[:, i, :], w[:, i, pads:])),
                                            (round_rep, round_max, lambda i: v.match_replace(w[:, i, pads:], top8[:, i, :], w[:, i, pads:], -FLT_MAX))):
                        for i in range(GT):
                            if i % 4 == 0:
                                hold(dve, gate_, n_before + i + 4)
                            go(i).then_inc(done, 1)

                def masks(g):
                    for u in range(2):
                        v.tensor_scalar(M[:, :, ds((g * 2 + u) * S, S)], w[:, u * KD:(u + 1) * KD, WINDOW:WK][:, :, ::-1], -FLT_MAX, None,
                                        ALU.is_gt).then_inc(mask_done, 1)

                def heavy(g):
                    hold(dve, t2_set, g + 1)
                    hold(dve, mask_done, g * 2 + 2)
                    for i in range(GT):
                        v.tensor_scalar(under[:, i, :], cT[:, ds(g * 2 + i // KD, 1), i % KD, :].rearrange("p a s -> p (a s)"),
                                        t_2[:, i:i + 1], 0.0, ALU.is_lt, ALU.add, accum_out=m_cnt[:, i:i + 1]).then_inc(counted, 1)
                    hold(dve, counted, g * GT + GT // 2 + 1)
                    for u in range(2):
                        if u == 1:
                            hold(dve, counted, g * GT + GT + 1)
                        v.scalar_tensor_tensor(w[:, u * KD:(u + 1) * KD, WINDOW:WK], under[:, u * KD:(u + 1) * KD, :], -FLT_MAX,
                                               cT[:, ds(g * 2 + u, 1), :, :].rearrange("p a k s -> p (a k) s"), ALU.mult, ALU.subtract).then_inc(w_set, 1)
                    fill = m_cnt[:, :].unsqueeze(2).to_broadcast([P, GT, WINDOW])
                    v.scalar_tensor_tensor(pad01, iota_lane[:, 0:WINDOW].unsqueeze(1).to_broadcast([P, GT, WINDOW]), float(KS - WINDOW), fill,
                                           ALU.add, ALU.is_lt).then_inc(sel_small, 1)
                    v.tensor_scalar(off[:, :], m_cnt[:, :], -float(KS - WINDOW // 2), None, ALU.add).then_inc(sel_small, 1)
                    hold(dve, sel_small, g * 6 + 1)
                    v.tensor_scalar(pad_neg, pad01, -1.0, FLT_MAX, ALU.add, ALU.mult).then_inc(sel_small, 1)
                    hold(dve, sel_small, g * 6 + 2)
                    v.tensor_tensor(off[:, :], off[:, :], off[:, :], ALU.mult).then_inc(sel_small, 1)
                    hold(dve, sel_small, g * 6 + 3)
                    v.scalar_tensor_tensor(pad01, pad01, FLT_MAX, pad_neg, ALU.mult, ALU.add).then_inc(sel_small, 1)
                    hold(dve, sel_small, g * 6 + 4)
                    v.tensor_reduce(off_max[:, ds(g, 1)], off[:, :], AX.X, ALU.max).then_inc(sel_small, 1)
                    hold(dve, sel_small, g * 6 + 5)
                    hold(dve, w_set, g * 2 + 2)
                    for r in range(QUICK):
                        take((g * QUICK + r) * GT, 0)
                    hold(dve, round_rep, (g + 1) * QUICK * GT + GT)
                    masks(g)

                dve.sem_inc(counted, 1)
                dve.sem_inc(mask_done, 2)
                dve.sem_inc(round_rep, GT)
                stats(0)
                with dve.Fori(0, NG - 1) as g:
                    hold(dve, t0_set, g + 1)
                    stats(g + 1)
                    heavy(g)
                heavy(NG - 1)
                hold(dve, sel_small, NG * 6)
                v.tensor_reduce(off_one, off_max, AX.X, ALU.max).then_inc(sel_small, 1)
                hold(dve, sel_small, NG * 6 + 1)
                v.tensor_scalar(off_any, off_one, float((WINDOW // 2) ** 2), None, ALU.is_gt).then_inc(off_set, 1)
                hold(dve, off_mm, 1)
                v.tensor_copy(off_i, bank[0][:, 0:1]).then_inc(sel_small, 1)
                hold(dve, sel_small, NG * 6 + 2)
                missed = dve.value_load(off_i[0:1, 0:1], min_val=0, max_val=P)
                with dve.If(missed > 0):
                    with dve.Fori(0, NG) as g:
                        hold(dve, mask_done, (g + NG) * 2 + 2)
                        v.memset(w[:, :, WINDOW - PADS:WINDOW], FLT_MAX).then_inc(w_set, 1)
                        for u in range(2):
                            v.tensor_scalar(w[:, u * KD:(u + 1) * KD, WINDOW:WK], cT[:, ds(g * 2 + u, 1), :, :].rearrange("p a k s -> p (a k) s"),
                                            -1.0, None, ALU.mult).then_inc(w_set, 1)
                        hold(dve, w_set, NG * 2 + g * 3 + 3)
                        with dve.Fori(0, ROUNDS) as r:
                            take((g * ROUNDS + r + NG * QUICK) * GT, WINDOW - PADS)
                        hold(dve, round_rep, (g + 1) * (ROUNDS * GT) + (NG * QUICK + 1) * GT)
                        masks(g)

        ln_stat = sem("ln_stat")
        ln_mean = sem("ln_mean")
        ln_var = sem("ln_var")
        ln_rstd = sem("ln_rstd")
        ln_out = sem("ln_out")

        def ln_stats(dve, src, u, n):
            v = nc.vector
            v.bn_stats(st6[:, u, 0:6], src[:, 0:BANK])
            v.bn_stats(st6[:, u, 6:12], src[:, BANK:D]).then_inc(ln_stat, 1)
            hold(dve, ln_stat, n)
            v.bn_aggr(mv[:, u, :], st6[:, u, :]).then_inc(ln_mean, 1)
            dve.wait_ge(ln_mean, n)
            v.tensor_scalar(ve[:, u, 0:1], mv[:, u, 1:2], EPS, None, ALU.add).then_inc(ln_var, 1)

        def ln_pow(pool, u, n):
            pool.wait_ge(ln_var, n)
            nc.gpsimd.tensor_tensor(rs[:, u, 0:1], ve[:, u, 0:1], neg_half[:, 0:1], ALU.pow).then_inc(ln_rstd, 1)

        def ln_apply(dve, dst, src, u, n):
            dve.wait_ge(ln_rstd, n)
            nc.vector.tensor_scalar(dst, src, mv[:, u, 0:1], rs[:, u, 0:1], ALU.subtract, ALU.mult).then_inc(ln_out, 1)

        x_in = [sem(f"x_in{u}") for u in range(TPC)]
        emb_tp = sem("emb_tp")
        emb_tpev = sem("emb_tpev")
        emb_mm = sem("emb_mm")
        emb_ev = sem("emb_ev")
        xn_t = X[:, :, :].rearrange("p t d -> p (t d)").rearrange("p (k n) -> p k n", k=KD)

        with nc.Block() as block:
            @block.sync
            def _(sp):
                with sp.Fori(0, CH) as q:
                    for u in range(TPC):
                        sp.wait_ge(emb_tp, q * 8 + 2 * u + 2)
                        sp.dma_start(nat[:, u, :], x2d[ds(q * CW + u * P, P), :]).then_inc(x_in[u], 16)

            @block.gpsimd
            def _(pool):
                with pool.Fori(0, CH) as q:
                    for u in range(TPC):
                        ln_pow(pool, u, q * TPC + u + 1)

            @block.vector
            def _(dve):
                with dve.Fori(0, CH) as q:
                    for u in range(TPC + 1):
                        if u < TPC:
                            dve.wait_ge(x_in[u], q * 16 + 16)
                            ln_stats(dve, nat[:, u, :], u, q * TPC + u + 1)
                        if u > 0:
                            ln_apply(dve, nat[:, u - 1, :], nat[:, u - 1, :], u - 1, q * TPC + u)

            @block.tensor
            def _(pe):
                pe.sem_inc(emb_tp, 8)
                with pe.Fori(0, CH) as q:
                    for u in range(TPC):
                        pe.wait_ge(ln_out, q * TPC + u + 1)
                        for h in range(2):
                            pe.wait_ge(emb_tpev, q * 8 + 2 * u + h + 1)
                            for j in range(4):
                                k = 4 * h + j
                                mm = nc.tensor.transpose(bank[2 * (u % 2) + h][:, j * P:(j + 1) * P], nat[:, u, k * P:(k + 1) * P], ident[:, :])
                            mm.then_inc(emb_tp, 1)
                    pe.wait_ge(emb_tpev, q * 8 + 12)
                    pe.wait_ge(emb_ev, q + 1)
                    for k in range(KD):
                        mm = nc.tensor.matmul(bank[4][:, :], win_t[:, k, :], xn_t[:, k, ds(q * CW, CW)], start=(k == 0), stop=(k == KD - 1))
                    mm.then_inc(emb_mm, 1)

            @block.scalar
            def _(act):
                act.sem_inc(emb_tpev, 4)
                act.sem_inc(emb_ev, 1)
                with act.Fori(0, CH) as q:
                    for u in range(TPC):
                        for h in range(2):
                            act.wait_ge(emb_tp, q * 8 + 2 * u + h + 9)
                            nc.scalar.copy(xn_t[:, 4 * h:4 * h + 4, ds(q * CW + u * P, P)],
                                           bank[2 * (u % 2) + h][:, :].rearrange("p (k n) -> p k n", k=4)).then_inc(emb_tpev, 1)
                    act.wait_ge(emb_mm, q + 1)
                    nc.scalar.activation(H[:, ds(q * CW, CW)], bank[4][:, :], ACT.Identity, bias=block_par[:, 0:1]).then_inc(emb_ev, 1)

        hid = Xf[:, 0:CH * FT * CW].rearrange("p (q t n) -> p q t n", q=CH, t=FT)
        a_buf = Xf[:, 8192:10240]
        b_buf = Xf[:, 10240:12288]
        sq = Xf[:, 12288:14336]
        yn = Xf[:, 14336:16384]
        BC, ZO, HD, SMALL, PREP = (0, 1), (2, 3), (4, 5), 6, 7
        VAR = (6, 7, 4, 5)
        w1_in, w2_in = sem("w1_in"), sem("w2_in")
        cur_set, cs_set = sem("cur_set"), sem("cs_set")
        w1_tp, w1_u, w1_s, w2_tp, w2_set, b1_mm, b1_set = (sem(n) for n in ("w1_tp", "w1_u", "w1_s", "w2_tp", "w2_set", "b1_mm", "b1_set"))
        sq1, var1, ve1, rt1, bc1, yn1 = (sem(n) for n in ("sq1", "var1", "ve1", "rt1", "bc1", "yn1"))
        sq2, var2, ve2, rt2, bc2, yn2 = (sem(n) for n in ("sq2", "var2", "ve2", "rt2", "bc2", "yn2"))
        act1, ab_in, scanned, ab_out, z_mm, h_mid = (sem(n) for n in ("act1", "ab_in", "scanned", "ab_out", "z_mm", "h_mid"))
        hid_mm, hid_act, o_mm, h_out = (sem(n) for n in ("hid_mm", "hid_act", "o_mm", "h_out"))

        def chunk(buf, q):
            return buf[:, q * CW:(q + 1) * CW]

        def variance(src, q):
            for i in range(TPC):
                mm = nc.tensor.matmul(bank[VAR[q]][:, i:i + 1], src[:, i * P:(i + 1) * P], inv_col[:, :], start=True, stop=True)
            return mm

        def spread(dst, q):
            for i in range(TPC):
                mm = nc.tensor.matmul(dst[:, i * P:(i + 1) * P], rs[:, q, i:i + 1].to_broadcast([P, P]), ident[:, :], start=True, stop=True)
            return mm

        with nc.Block() as block:
            @block.sync
            def _(sp):
                sp.sem_inc(w1_tp, 1)
                sp.sem_inc(w2_tp, 1)
                with sp.Fori(0, NL) as l:
                    sp.wait_ge(w1_tp, l + 1)
                    sp.dma_start(w1raw, w1[ds(l, 1), :, :].rearrange("a (t p) d -> p (a t) d", p=P)).then_inc(w1_in, 16)
                    sp.wait_ge(w2_tp, l + 1)
                    sp.dma_start(w2raw, w2[ds(l, 1), :, :].rearrange("a p f -> p (a f)")).then_inc(w2_in, 16)

            @block.gpsimd
            def _(pool):
                g = nc.gpsimd

                def turn(dst, src, l, q, table):
                    g.tensor_tensor(chunk(dst, q).rearrange("p (b s) -> p b s", b=BPC), chunk(src, q).rearrange("p (b s) -> p b s", b=BPC),
                                    table[:, ds(l, 1), :].to_broadcast([P, BPC, S]), ALU.mult)

                def turn_done(dst, src, l, q, table, done):
                    g.tensor_tensor(chunk(dst, q).rearrange("p (b s) -> p b s", b=BPC), chunk(src, q).rearrange("p (b s) -> p b s", b=BPC),
                                    table[:, ds(l, 1), :].to_broadcast([P, BPC, S]), ALU.mult).then_inc(done, 1)

                with pool.Fori(0, NL) as l:
                    for q in range(CH):
                        pool.wait_ge(ve1, l * CH + q + 1)
                        g.tensor_tensor(rs[:, q, :], ve[:, q, :], neg_half[:, 0:TPC], ALU.pow).then_inc(rt1, 1)
                    for q in range(CH):
                        hold(pool, act1, l * CH + q + 1)
                        turn(a_buf, yn, l, q, cos_t)
                        turn_done(b_buf, yn, l, q, sin_t, ab_in)
                    for q in range(CH):
                        hold(pool, scanned, l * CH + q + 1)
                        turn(a_buf, a_buf, l, q, cos_t)
                        turn_done(b_buf, b_buf, l, q, sin_t, ab_out)
                    for q in range(CH):
                        pool.wait_ge(ve2, l * CH + q + 1)
                        g.tensor_tensor(rs[:, q, :], ve[:, q, :], neg_half[:, 0:TPC], ALU.pow).then_inc(rt2, 1)

            @block.tensor
            def _(pe):
                with pe.Fori(0, NL) as l:
                    pe.wait_ge(w1_in, l * 16 + 16)
                    for t in range(FT):
                        mm = nc.tensor.transpose(bank[PREP][:, t * P:(t + 1) * P], w1raw[:, t, :], ident[:, :])
                    mm.then_inc(w1_tp, 1)
                    pe.wait_ge(w1_u, l + 1)
                    pe.wait_ge(w1_s, l + 1)
                    pe.wait_ge(w2_in, l * 16 + 16)
                    for t in range(FT):
                        mm = nc.tensor.matmul(bank[PREP][:, t * P:(t + 1) * P], w2raw[:, t * P:(t + 1) * P], center[:, :], start=True, stop=True)
                    mm.then_inc(w2_tp, 1)
                    pe.wait_ge(cur_set, l + 1)
                    for t in range(FT):
                        mm = nc.tensor.matmul(bank[SMALL][:, 32 + t:33 + t], w1u[:, t * P:(t + 1) * P], cur[:, LN2B:LN2B + 1], start=True, stop=True)
                    mm.then_inc(b1_mm, 1)
                    pe.wait_ge(b1_set, l + 1)
                    pe.wait_ge(w2_set, l + 1)
                    pe.wait_ge(hid_act, l * (CH * FT) + 2)
                    for q in range(CH):
                        pe.wait_ge(sq1, l * CH + q + 1)
                        variance(chunk(sq, q), q).then_inc(var1, 1)
                    for q in range(CH):
                        pe.wait_ge(rt1, l * CH + q + 1)
                        if q >= 2:
                            pe.wait_ge(yn1, l * CH + q - 1)
                        spread(bank[BC[q % 2]], q).then_inc(bc1, 1)
                    pe.wait_ge(cs_set, l + 1)
                    for q in range(CH):
                        pe.wait_ge(ab_out, l * CH + q + 1)
                        if q >= 2:
                            pe.wait_ge(h_mid, l * CH + q - 1)
                        nc.tensor.matmul(bank[ZO[q % 2]][:, :], cs, chunk(a_buf, q), start=True, stop=False)
                        nc.tensor.matmul(bank[ZO[q % 2]][:, :], cs, chunk(b_buf, q), start=False, stop=True).then_inc(z_mm, 1)
                    for q in range(CH):
                        pe.wait_ge(sq2, l * CH + q + 1)
                        variance(chunk(sq, q), q).then_inc(var2, 1)
                    for q in range(CH):
                        pe.wait_ge(rt2, l * CH + q + 1)
                        if q >= 2:
                            pe.wait_ge(yn2, l * CH + q - 1)
                        spread(bank[BC[q % 2]], q).then_inc(bc2, 1)
                    for q in range(CH):
                        pe.wait_ge(yn2, l * CH + q + 1)
                        for t in range(FT):
                            pe.wait_ge(hid_act, l * (CH * FT) + q * FT + t + 1)
                            nc.tensor.matmul(bank[HD[t % 2]][:, :], w1s[:, t * P:(t + 1) * P], chunk(yn, q), start=True, stop=True).then_inc(hid_mm, 1)
                        if q >= 2:
                            pe.wait_ge(h_out, l * CH + q + 3)
                        for t in range(FT):
                            pe.wait_ge(hid_act, l * (CH * FT) + q * FT + t + 3)
                            mm = nc.tensor.matmul(bank[ZO[q % 2]][:, :], w2c[:, t, :], hid[:, q, t, :], start=(t == 0), stop=(t == FT - 1))
                        mm.then_inc(o_mm, 1)

            @block.scalar
            def _(act):
                a = nc.scalar
                act.sem_inc(hid_act, 2)
                with act.Fori(0, NL) as l:
                    act.wait_ge(w1_tp, l + 2)
                    a.copy(w1u, bank[PREP][:, :]).then_inc(w1_u, 1)
                    act.wait_ge(w2_tp, l + 2)
                    a.copy(w2c.rearrange("p t m -> p (t m)"), bank[PREP][:, :]).then_inc(w2_set, 1)
                    for q in range(CH):
                        act.wait_ge(h_out, l * CH + q + 1)
                        a.activation(chunk(sq, q), chunk(H, q), ACT.Square).then_inc(sq1, 1)
                    act.wait_ge(cur_set, l + 1)
                    for q in range(CH):
                        act.wait_ge(yn1, l * CH + q + 1)
                        a.activation(chunk(yn, q), chunk(yn, q), ACT.Silu, scale=cur[:, LN1W:LN1W + 1], bias=cur[:, LN1B:LN1B + 1]).then_inc(act1, 1)
                    for q in range(CH):
                        act.wait_ge(h_mid, l * CH + q + 1)
                        a.activation(chunk(sq, q), chunk(H, q), ACT.Square).then_inc(sq2, 1)
                    act.wait_ge(b1_set, l + 1)
                    for q in range(CH):
                        for t in range(FT):
                            act.wait_ge(hid_mm, l * (CH * FT) + q * FT + t + 1)
                            a.activation(hid[:, q, t, :], bank[HD[t % 2]][:, :], ACT.Silu, bias=b1f[:, t:t + 1]).then_inc(hid_act, 1)

            @block.vector
            def _(dve):
                v = nc.vector
                dve.sem_inc(h_out, 4)
                with dve.Fori(0, NL) as l:
                    dve.wait_ge(h_out, l * CH + 4)
                    v.tensor_copy(cur[:, :], layer_par[:, ds(l, 1), :].rearrange("p a k -> p (a k)")).then_inc(cur_set, 1)
                    dve.wait_ge(cur_set, l + 1)
                    v.tensor_scalar(cs, center[:, :], cur[:, SCL:SCL + 1], None, ALU.mult).then_inc(cs_set, 1)
                    dve.wait_ge(w1_u, l + 1)
                    v.tensor_scalar(w1s, bank[PREP][:, :], cur[:, LN2W:LN2W + 1], None, ALU.mult).then_inc(w1_s, 1)
                    dve.wait_ge(b1_mm, l + 1)
                    v.tensor_tensor(b1f, bank[SMALL][:, 32:32 + FT], cur[:, B1:B1 + FT], ALU.add).then_inc(b1_set, 1)
                    for q in range(CH):
                        dve.wait_ge(var1, l * CH + q + 1)
                        v.tensor_scalar(ve[:, q, :], bank[VAR[q]][:, 0:TPC], EPS, None, ALU.add).then_inc(ve1, 1)
                    for q in range(CH):
                        dve.wait_ge(bc1, l * CH + q + 1)
                        v.tensor_tensor(chunk(yn, q), chunk(H, q), bank[BC[q % 2]][:, :], ALU.mult).then_inc(yn1, 1)
                    rho = cur[:, RHO:RHO + 1].to_broadcast([P, S])
                    for q in range(CH):
                        dve.wait_ge(ab_in, l * CH + q + 1)
                        for b in range(BPC):
                            for buf, first in ((a_buf, UR0), (b_buf, UI0)):
                                part = buf[:, q * CW + b * S:q * CW + (b + 1) * S]
                                sc = v.tensor_tensor_scan(part, rho, part, cur[:, first:first + 1], ALU.mult, ALU.add)
                        sc.then_inc(scanned, 1)
                    for q in range(CH):
                        dve.wait_ge(z_mm, l * CH + q + 1)
                        v.tensor_tensor(chunk(H, q), chunk(H, q), bank[ZO[q % 2]][:, :], ALU.add).then_inc(h_mid, 1)
                    for q in range(CH):
                        dve.wait_ge(var2, l * CH + q + 1)
                        v.tensor_scalar(ve[:, q, :], bank[VAR[q]][:, 0:TPC], EPS, None, ALU.add).then_inc(ve2, 1)
                    for q in range(CH):
                        dve.wait_ge(bc2, l * CH + q + 1)
                        v.tensor_tensor(chunk(yn, q), chunk(H, q), bank[BC[q % 2]][:, :], ALU.mult).then_inc(yn2, 1)
                    for q in range(CH):
                        dve.wait_ge(o_mm, l * CH + q + 1)
                        v.scalar_tensor_tensor(chunk(H, q), bank[ZO[q % 2]][:, :], cur[:, B2:B2 + 1], chunk(H, q), ALU.add, ALU.add).then_inc(h_out, 1)

        sq_f, yn_f = fin[:, 0, :], fin[:, 1, :]
        f_sq, f_var, f_ve, f_rt, f_bc, f_yn = (sem(n) for n in ("f_sq", "f_var", "f_ve", "f_rt", "f_bc", "f_yn"))
        r_in = [sem(f"r_in{u}") for u in range(TPC)]
        r_bias, o2_mm, x1_done, x1_tp, x1_tpev = (sem(n) for n in ("r_bias", "o2_mm", "x1_done", "x1_tp", "x1_tpev"))

        with nc.Block() as block:
            @block.sync
            def _(sp):
                sp.sem_inc(x1_tp, 8)
                with sp.Fori(0, CH) as q:
                    for u in range(TPC):
                        sp.wait_ge(x1_tp, q * 8 + 2 * u + 2)
                        sp.dma_start(nat[:, u, :], x2d[ds(q * CW + u * P, P), :]).then_inc(r_in[u], 16)

            @block.gpsimd
            def _(pool):
                g = nc.gpsimd
                with pool.Fori(0, CH) as q:
                    pool.wait_ge(f_ve, q + 1)
                    g.tensor_tensor(rs[:, 0, :], ve[:, 0, :], neg_half[:, 0:TPC], ALU.pow).then_inc(f_rt, 1)
                    for u in range(TPC):
                        pool.wait_ge(r_in[u], q * 16 + 16)
                        g.tensor_tensor(nat[:, u, :], nat[:, u, :], bout_b, ALU.add).then_inc(r_bias, 1)
                    for u in range(TPC):
                        ln_pow(pool, u, q * TPC + u + NT + 1)

            @block.scalar
            def _(act):
                act.sem_inc(x1_tpev, 2)
                with act.Fori(0, CH) as q:
                    nc.scalar.activation(sq_f, H[:, ds(q * CW, CW)], ACT.Square).then_inc(f_sq, 1)
                    for u in range(TPC):
                        for h in range(2):
                            act.wait_ge(x1_tp, q * 8 + 2 * u + h + 9)
                            nc.scalar.copy(T[:, 4 * h:4 * h + 4, ds(q * CW + u * P, P)],
                                           bank[6 + h][:, :].rearrange("p (k n) -> p k n", k=4)).then_inc(x1_tpev, 1)

            @block.tensor
            def _(pe):
                with pe.Fori(0, CH) as q:
                    pe.wait_ge(f_sq, q + 1)
                    for i in range(TPC):
                        mm = nc.tensor.matmul(bank[0][:, i:i + 1], sq_f[:, i * P:(i + 1) * P], inv_col[:, :], start=True, stop=True)
                    mm.then_inc(f_var, 1)
                    pe.wait_ge(f_rt, q + 1)
                    spread(bank[1], 0).then_inc(f_bc, 1)
                    pe.wait_ge(f_yn, q + 1)
                    for u in range(TPC + 1):
                        if u < TPC:
                            for n in range(2):
                                pe.wait_ge(x1_done, q * 8 + 2 * u + n + 1)
                                nc.tensor.matmul(bank[2 + 2 * (u % 2) + n][:, :], yn_f[:, u * P:(u + 1) * P], wout_t[:, n * BANK:(n + 1) * BANK],
                                                 start=True, stop=True).then_inc(o2_mm, 1)
                        if u > 0:
                            pe.wait_ge(ln_out, q * TPC + u + NT)
                            for h in range(2):
                                pe.wait_ge(x1_tpev, q * 8 + 2 * u + h - 1)
                                for j in range(4):
                                    k = 4 * h + j
                                    mm = nc.tensor.transpose(bank[6 + h][:, j * P:(j + 1) * P], nat[:, u - 1, k * P:(k + 1) * P], ident[:, :])
                                mm.then_inc(x1_tp, 1)

            @block.vector
            def _(dve):
                v = nc.vector
                dve.sem_inc(x1_done, 4)
                with dve.Fori(0, CH) as q:
                    dve.wait_ge(f_var, q + 1)
                    v.tensor_scalar(ve[:, 0, :], bank[0][:, 0:TPC], EPS, None, ALU.add).then_inc(f_ve, 1)
                    dve.wait_ge(f_bc, q + 1)
                    v.tensor_tensor(yn_f, H[:, ds(q * CW, CW)], bank[1][:, :], ALU.mult).then_inc(f_yn, 1)
                    for u in range(TPC + 1):
                        if u < TPC:
                            row = X[:, ds(q * TPC + u, 1), :].rearrange("p a d -> p (a d)")
                            dve.wait_ge(r_bias, q * TPC + u + 1)
                            for n in range(2):
                                dve.wait_ge(o2_mm, q * 8 + 2 * u + n + 1)
                                v.tensor_tensor(row[:, n * BANK:(n + 1) * BANK], bank[2 + 2 * (u % 2) + n][:, :],
                                                nat[:, u, n * BANK:(n + 1) * BANK], ALU.add).then_inc(x1_done, 1)
                            hold(dve, x1_done, q * 8 + 2 * u + 6)
                            ln_stats(dve, row, u, q * TPC + u + NT + 1)
                        if u > 0:
                            row = X[:, ds(q * TPC + u - 1, 1), :].rearrange("p a d -> p (a d)")
                            ln_apply(dve, nat[:, u - 1, :], row, u - 1, q * TPC + u + NT)

        crux = natf[:, 0:N]
        rest = natf[:, N:2 * N]
        lo = 0

        def in_late(*shape):
            nonlocal lo
            n = 1
            for s in shape:
                n *= s
            lo += n
            flat = late[:, lo - n:lo]
            names = "abcd"[:len(shape)]
            return flat.rearrange(f"p ({' '.join(names)}) -> p {' '.join(names)}", **dict(zip(names, shape)))

        pooled = in_late(2, 2, KD, B)
        sums = in_late(2, B)
        junk = H[:, :].bitcast(mybir.dt.bfloat16).rearrange("p (i n) -> p i n", i=2)
        cr_mul, cr_max, cr_sum, re_sub, re_max, re_sum, sums_out = (sem(n) for n in ("cr_mul", "cr_max", "cr_sum", "re_sub", "re_max", "re_sum", "sums_out"))

        with nc.Block() as block:
            @block.gpsimd
            def _(pool):
                g = nc.gpsimd
                pool.sem_inc(cr_mul, 1)
                pool.sem_inc(re_sub, 1)
                with pool.Fori(0, KD) as k:
                    xk = T[:, ds(k, 1), :].rearrange("p a n -> p (a n)")
                    mk = M[:, ds(k, 1), :].rearrange("p a n -> p (a n)")
                    pool.wait_ge(cr_max, k + 1)
                    pool.wait_ge(cr_sum, k + 1)
                    hold(pool, re_sub, k + 1)
                    g.tensor_tensor(crux, xk, mk, ALU.mult).then_inc(cr_mul, 1)
                    pool.wait_ge(cr_mul, k + 2)
                    pool.wait_ge(re_max, k + 1)
                    hold(pool, re_sum, k + 1)
                    g.tensor_tensor(rest, xk, crux, ALU.subtract).then_inc(re_sub, 1)

            @block.vector
            def _(dve):
                v = nc.vector
                dve.sem_inc(cr_max, 1)
                dve.sem_inc(re_max, 1)
                dve.sem_inc(sums_out, 1)
                with dve.Fori(0, KD) as k:
                    for i, (src, made, done) in enumerate(((crux, cr_mul, cr_max), (rest, re_sub, re_max))):
                        dve.wait_ge(made, k + 2)
                        v.tensor_reduce(pooled[:, 0, i, ds(k, 1), :].rearrange("p a b -> p (a b)"), src.rearrange("p (b s) -> p b s", b=B),
                                        AX.X, ALU.max).then_inc(done, 1)
                    dve.wait_ge(cr_sum, k + 2)
                    dve.wait_ge(re_sum, k + 2)
                    for i, n in enumerate((KC, KS)):
                        ins = v.tensor_scalar(pooled[:, 1, i, ds(k, 1), :].rearrange("p a b -> p (a b)"), sums[:, i, :], 1.0 / n, None, ALU.mult)
                    ins.then_inc(sums_out, 1)

            @block.scalar
            def _(act):
                act.sem_inc(cr_sum, 1)
                act.sem_inc(re_sum, 1)
                with act.Fori(0, KD) as k:
                    act.wait_ge(sums_out, k + 1)
                    for i, (src, made, done) in enumerate(((crux, cr_mul, cr_sum), (rest, re_sub, re_sum))):
                        act.wait_ge(made, k + 2)
                        for b in range(B):
                            ins = nc.scalar.activation(junk[:, i, b * S:(b + 1) * S], src[:, b * S:(b + 1) * S], ACT.Copy, accum_out=sums[:, i, b:b + 1])
                        ins.then_inc(done, 1)

        z = in_late(2, KD * B)
        zz = in_late(2, KD * B)
        gsum = in_late(2)
        gmean = in_late(2)
        gvar = in_late(2)
        grs = in_late(2)
        g_dve, g_pe, g_pool, g_act = (sem(n) for n in ("g_dve", "g_pe", "g_pool", "g_act"))
        CNT = D * B

        with nc.Block() as block:
            @block.tensor
            def _(pe):
                pin = pooled[:, :, :, :, :].rearrange("p m i k b -> p m i (k b)")
                zb = bank[0][:, 0:2 * KD * B].rearrange("p (i n) -> p i n", i=2)
                edge = B
                for c in range(2):
                    nc.tensor.matmul(zb[:, :, :], band[:, c, P:2 * P], pin[:, c, :, :], start=(c == 0), stop=False, skip_group_check=True)
                for c in range(2):
                    for i in range(2):
                        nc.tensor.matmul(zb[:, i, edge:], band[:, c, 2 * P:3 * P], pin[:, c, i, 0:KD * B - edge], start=False, stop=False, skip_group_check=True)
                        mm = nc.tensor.matmul(zb[:, i, 0:KD * B - edge], band[:, c, 0:P], pin[:, c, i, edge:], start=False, stop=(c == 1 and i == 1),
                                              skip_group_check=True)
                mm.then_inc(g_pe, 1)
                pe.wait_ge(g_dve, 2)
                nc.tensor.matmul(bank[1][:, 0:2], ones[:, :], gsum[:, :], start=True, stop=True).then_inc(g_pe, 1)
                pe.wait_ge(g_dve, 6)
                nc.tensor.matmul(bank[2][:, 0:2], ones[:, :], gsum[:, :], start=True, stop=True).then_inc(g_pe, 1)

            @block.gpsimd
            def _(pool):
                pool.wait_ge(g_dve, 7)
                nc.gpsimd.tensor_tensor(grs[:, :], gvar[:, :], neg_half[:, 0:2], ALU.pow).then_inc(g_pool, 1)

            @block.scalar
            def _(act):
                act.wait_ge(g_dve, 10)
                nc.scalar.activation(z[:, :, :], z[:, :, :], ACT.Sigmoid).then_inc(g_act, 1)

            @block.vector
            def _(dve):
                v = nc.vector
                n_link = [0]

                def link(ins):
                    n_link[0] += 1
                    ins.then_inc(g_dve, 1)
                    dve.wait_ge(g_dve, n_link[0])

                dve.wait_ge(g_pe, 1)
                link(v.tensor_copy(z[:, :, :], bank[0][:, 0:2 * KD * B].rearrange("p (i n) -> p i n", i=2)))
                link(v.tensor_reduce(gsum[:, :], z[:, :, :], AX.X, ALU.add))
                dve.wait_ge(g_pe, 2)
                link(v.tensor_scalar(gmean[:, :], bank[1][:, 0:2], 1.0 / CNT, None, ALU.mult))
                link(v.tensor_tensor(z[:, :, :], z[:, :, :], gmean[:, :].unsqueeze(2).to_broadcast([P, 2, KD * B]), ALU.subtract))
                link(v.tensor_tensor(zz[:, :, :], z[:, :, :], z[:, :, :], ALU.mult))
                link(v.tensor_reduce(gsum[:, :], zz[:, :, :], AX.X, ALU.add))
                dve.wait_ge(g_pe, 3)
                link(v.tensor_scalar(gvar[:, :], bank[2][:, 0:2], 1.0 / CNT, EPS, ALU.mult, ALU.add))
                dve.wait_ge(g_pool, 1)
                link(v.tensor_tensor(z[:, :, :], z[:, :, :], grs[:, :].unsqueeze(2).to_broadcast([P, 2, KD * B]), ALU.mult))
                link(v.tensor_scalar(z[:, :, :], z[:, :, :], bn_gb[:, 0:1], bn_gb[:, 1:2], ALU.mult, ALU.add))
                link(v.tensor_scalar(z[:, :, :], z[:, :, :], 0.0, None, ALU.max))
                dve.wait_ge(g_act, 1)
                link(v.tensor_tensor(z[:, 0, :], z[:, 0, :], z[:, 1, :], ALU.subtract))

        gated = natf[:, 0:N]
        gmul, gm_done, gt_mm, x2_done = (sem(n) for n in ("gmul", "gm_done", "gt_mm", "x2_done"))
        gsel = natf[:, N:2 * N]

        with nc.Block() as block:
            @block.scalar
            def _(act):
                act.sem_inc(gmul, 1)
                with act.Fori(0, KD) as k:
                    act.wait_ge(gm_done, k + 1)
                    for b in range(B):
                        ins = nc.scalar.activation(gsel[:, b * S:(b + 1) * S], M[:, ds(k, 1), b * S:(b + 1) * S].rearrange("p a s -> p (a s)"),
                                                   ACT.Identity, scale=z[:, 0, ds(k * B + b, 1)], bias=z[:, 1, ds(k * B + b, 1)])
                    ins.then_inc(gmul, 1)

            @block.tensor
            def _(pe):
                with pe.Fori(0, KD) as k:
                    pe.wait_ge(gm_done, k + 2)
                    for g in range(CH):
                        pe.wait_ge(x2_done, k * CH + g + 1)
                        for j in range(TPC):
                            t = g * TPC + j
                            mm = nc.tensor.transpose(bank[g][:, j * P:(j + 1) * P], gated[:, t * P:(t + 1) * P], ident[:, :])
                        mm.then_inc(gt_mm, 1)

            @block.vector
            def _(dve):
                v = nc.vector
                dve.sem_inc(gm_done, 1)
                dve.sem_inc(x2_done, 4)
                with dve.Fori(0, KD) as k:
                    dve.wait_ge(gmul, k + 2)
                    v.tensor_tensor(gated, gsel, T[:, ds(k, 1), :].rearrange("p a n -> p (a n)"), ALU.mult).then_inc(gm_done, 1)
                    for g in range(CH):
                        dve.wait_ge(gt_mm, k * CH + g + 1)
                        part = X[:, g * TPC:(g + 1) * TPC, ds(k * P, P)]
                        v.tensor_tensor(part, part, bank[g][:, :].rearrange("p (t n) -> p t n", t=TPC), ALU.add).then_inc(x2_done, 1)

        logits = sb("logits", [P, NT, E])
        xt = H[:, :].rearrange("p (u k n) -> p u k n", u=2, k=KD)
        wslot = Tf.rearrange("p (w k n) -> p w k n", w=2, k=KD)
        out_init = sem("out_init")
        w_in_sem = [sem(f"w_in{w}") for w in range(2)]
        nrm_st = [sem(f"nrm_st{u}") for u in range(TPC)]
        l_tp, l_tpev, l_mm, l_ev = (sem(n) for n in ("l_tp", "l_tpev", "l_mm", "l_ev"))

        def expert_src(e):
            return expert_w[e, :, :].rearrange("(k p) n -> p k n", p=P)

        with nc.Block() as block:
            @block.sync
            def _(sp):
                sp.dma_start(out[0:N, :].rearrange("(t p) d -> p t d", p=P), X[:, :, :]).then_inc(out_init, 16)
                sp.dma_start(out[N:N + P, :], X[:, 0, :]).then_inc(out_init, 16)
                with sp.Fori(0, CH) as q:
                    for u in range(TPC):
                        sp.wait_ge(ln_out, q * TPC + u + 2 * NT + 1)
                        sp.dma_start(x_nrm[ds(q * CW + u * P, P), :], nat[:, u, :]).then_inc(nrm_st[u], 16)
                for w in range(2):
                    sp.dma_start(wslot[:, w, :, :], expert_src(w)).then_inc(w_in_sem[w], 16)
                for u in range(TPC):
                    sp.wait_ge(nrm_st[u], 16 * CH + 16)
                sp.wait_ge(out_init, 32)

            @block.gpsimd
            def _(pool):
                with pool.Fori(0, CH) as q:
                    for u in range(TPC):
                        ln_pow(pool, u, q * TPC + u + 2 * NT + 1)

            @block.vector
            def _(dve):
                v = nc.vector
                for u in range(TPC):
                    dve.sem_inc(nrm_st[u], 16)
                dve.sem_inc(l_tp, 8)
                with dve.Fori(0, CH) as q:
                    for u in range(TPC + 1):
                        if u < TPC:
                            ln_stats(dve, X[:, ds(q * TPC + u, 1), :].rearrange("p a d -> p (a d)"), u, q * TPC + u + 2 * NT + 1)
                        if u > 0:
                            dve.wait_ge(nrm_st[u - 1], q * 16 + 16)
                            dve.wait_ge(l_tp, q * 8 + 2 * u)
                            ln_apply(dve, nat[:, u - 1, :], X[:, ds(q * TPC + u - 1, 1), :].rearrange("p a d -> p (a d)"), u - 1,
                                     q * TPC + u + 2 * NT)
                    for u in range(TPC):
                        dve.wait_ge(l_mm, q * TPC + u + 1)
                        v.tensor_copy(logits[:, ds(q * TPC + u, 1), :].rearrange("p a e -> p (a e)"), bank[4 + u][:, 0:E]).then_inc(l_ev, 1)

            @block.tensor
            def _(pe):
                pe.sem_inc(l_ev, 4)
                with pe.Fori(0, CH) as q:
                    for u in range(TPC + 1):
                        if u < TPC:
                            pe.wait_ge(ln_out, q * TPC + u + 2 * NT + 1)
                            for h in range(2):
                                pe.wait_ge(l_tpev, q * 8 + 2 * u + h + 1)
                                for j in range(4):
                                    k = 4 * h + j
                                    mm = nc.tensor.transpose(bank[2 * (u % 2) + h][:, j * P:(j + 1) * P], nat[:, u, k * P:(k + 1) * P], ident[:, :])
                                mm.then_inc(l_tp, 1)
                        if u > 0:
                            pe.wait_ge(l_tpev, q * 8 + 2 * u + 4)
                            pe.wait_ge(l_ev, q * TPC + u)
                            for k in range(KD):
                                mm = nc.tensor.matmul(bank[4 + u - 1][:, 0:E], xt[:, (u - 1) % 2, k, :], gate[:, k, :], start=(k == 0), stop=(k == KD - 1))
                            mm.then_inc(l_mm, 1)

            @block.scalar
            def _(act):
                act.sem_inc(l_tpev, 4)
                with act.Fori(0, CH) as q:
                    for u in range(TPC):
                        if u >= 2:
                            act.wait_ge(l_mm, q * TPC + u - 1)
                        for h in range(2):
                            act.wait_ge(l_tp, q * 8 + 2 * u + h + 9)
                            nc.scalar.copy(xt[:, u % 2, 4 * h:4 * h + 4, :], bank[2 * (u % 2) + h][:, :].rearrange("p (k n) -> p k n", k=4)).then_inc(l_tpev, 1)

        xo = 9 * D

        def small(*shape, dt=F32):
            nonlocal xo
            n = 1
            for s in shape:
                n *= s
            xo += n
            flat = Xf[:, xo - n:xo]
            names = "abc"[:len(shape)]
            return (flat if dt == F32 else flat.bitcast(dt)).rearrange(f"p ({' '.join(names)}) -> p {' '.join(names)}", **dict(zip(names, shape)))

        best = small(2, NT)
        hot = small(2, NT, E)
        eq = small(NT, E)
        first = small(NT)
        masked = small(NT, E)
        either = small(NT, E)
        e2 = small(NT)
        prob = small(2, NT)
        tot = small(E, NT)
        upto = small(E, NT)
        full = small(E, NT)
        need = small(E)
        end = small(E)
        begin = small(E)
        place = small(NT, E)
        pos = small(2, NT)
        pos_i = small(2, NT, dt=I32)
        lane_i = small(2, NT, dt=I32)
        lane = small(2, NT)
        slot = small(2, NT)
        past = small(E, SLOTS)
        who = small(SLOTS)
        who_i = small(SLOTS, dt=I32)
        odd_i = small(SLOTS, dt=I32)
        ready_i = small(SLOTS, dt=I32)
        end_i = small(E, dt=I32)
        hot_lane = small(2, P)
        hot_slot = small(2, 2, SLOTS)
        zero_l = small(P)
        tokp1 = small(SLOTS)
        pair_p = small(SLOTS)
        unused = small(SLOTS)
        tok_f = small(SLOTS)
        src_i = small(SLOTS, dt=U32)
        dst_i = small(SLOTS, dt=U32)
        r_dve, r_act, r_pe, hot_set, hot_mm = (sem(n) for n in ("r_dve", "r_act", "r_pe", "hot_set", "hot_mm"))

        with nc.Block() as block:
            @block.scalar
            def _(act):
                act.wait_ge(r_dve, 13)
                nc.scalar.activation(e2[:, :], e2[:, :], ACT.Exp).then_inc(r_act, 1)

            @block.tensor
            def _(pe):
                pe.wait_ge(r_dve, 12)
                nc.tensor.matmul(bank[0][:, 0:NT * E], utri[:, :], either[:, :, :].rearrange("p t e -> p (t e)"), start=True, stop=True)
                nc.tensor.matmul(bank[1][:, 0:NT * E], ones[:, :], either[:, :, :].rearrange("p t e -> p (t e)"), start=True, stop=True).then_inc(r_pe, 1)
                pe.wait_ge(r_dve, 17)
                nc.tensor.matmul(bank[2][:, 0:2 * SLOTS], zero_l[:, :], band[:, 0, 0:2 * SLOTS], start=True, stop=False, skip_group_check=True)
                with pe.Fori(0, NT) as t:
                    for k in range(2):
                        pe.wait_ge(hot_set, t * 2 + k + 1)
                        nc.tensor.matmul(bank[2][:, 0:2 * SLOTS], hot_lane[:, k, :], hot_slot[:, k, :, :].rearrange("p a s -> p (a s)"),
                                         start=False, stop=False, skip_group_check=True).then_inc(hot_mm, 1)
                nc.tensor.matmul(bank[2][:, 0:2 * SLOTS], zero_l[:, :], band[:, 0, 0:2 * SLOTS], start=False, stop=True, skip_group_check=True).then_inc(r_pe, 1)

            @block.vector
            def _(dve):
                v = nc.vector
                n_link = [0]

                def link(ins):
                    n_link[0] += 1
                    ins.then_inc(r_dve, 1)
                    dve.wait_ge(r_dve, n_link[0])

                def over_e(ap):
                    return ap.unsqueeze(2).to_broadcast([P, NT, E])

                link(v.tensor_reduce(best[:, 0, :], logits[:, :, :], AX.X, ALU.max))
                link(v.tensor_tensor(eq[:, :, :], logits[:, :, :], over_e(best[:, 0, :]), ALU.is_equal))
                link(v.tensor_tensor(eq[:, :, :], eq[:, :, :], rev_e[:, :, :], ALU.mult))
                link(v.tensor_reduce(first[:, :], eq[:, :, :], AX.X, ALU.max))
                link(v.tensor_tensor(hot[:, 0, :, :], eq[:, :, :], over_e(first[:, :]), ALU.is_equal))
                link(v.scalar_tensor_tensor(masked[:, :, :], hot[:, 0, :, :], -FLT_MAX, logits[:, :, :], ALU.mult, ALU.add))
                link(v.tensor_reduce(best[:, 1, :], masked[:, :, :], AX.X, ALU.max))
                link(v.tensor_tensor(eq[:, :, :], masked[:, :, :], over_e(best[:, 1, :]), ALU.is_equal))
                link(v.tensor_tensor(eq[:, :, :], eq[:, :, :], rev_e[:, :, :], ALU.mult))
                link(v.tensor_reduce(first[:, :], eq[:, :, :], AX.X, ALU.max))
                link(v.tensor_tensor(hot[:, 1, :, :], eq[:, :, :], over_e(first[:, :]), ALU.is_equal))
                link(v.tensor_tensor(either[:, :, :], hot[:, 0, :, :], hot[:, 1, :, :], ALU.add))
                assert n_link[0] == 12
                link(v.tensor_tensor(e2[:, :], best[:, 1, :], best[:, 0, :], ALU.subtract))
                dve.wait_ge(r_act, 1)
                link(v.tensor_scalar(prob[:, 0, :], e2[:, :], 1.0, None, ALU.add))
                link(v.reciprocal(prob[:, 0, :], prob[:, 0, :]))
                link(v.tensor_tensor(prob[:, 1, :], e2[:, :], prob[:, 0, :], ALU.mult))
                link(v.memset(zero_l[:, :], 0.0))
                assert n_link[0] == 17
                dve.wait_ge(r_pe, 1)
                link(v.tensor_copy(tot[:, :, :], bank[1][:, 0:NT * E].rearrange("p (t e) -> p e t", e=E)))
                link(v.tensor_tensor_scan(upto[:, :, :].rearrange("p e t -> p (e t)"), later_t[:, :], tot[:, :, :].rearrange("p e t -> p (e t)"),
                                          0.0, ALU.mult, ALU.add))
                link(v.tensor_tensor(full[:, :, :], step_t[:, :, :], upto[:, :, NT - 1:NT].to_broadcast([P, E, NT]), ALU.is_lt))
                link(v.tensor_reduce(need[:, :], full[:, :, :], AX.X, ALU.add))
                link(v.tensor_tensor_scan(end[:, :], ones[:, 0:E], need[:, :], 0.0, ALU.mult, ALU.add))
                link(v.tensor_tensor(begin[:, :], end[:, :], need[:, :], ALU.subtract))
                link(v.tensor_tensor(upto[:, :, :], upto[:, :, :], tot[:, :, :], ALU.subtract))
                link(v.scalar_tensor_tensor(upto[:, :, :], begin[:, :].unsqueeze(2).to_broadcast([P, E, NT]), float(P), upto[:, :, :], ALU.mult, ALU.add))
                link(v.tensor_tensor(place[:, :, :], bank[0][:, 0:NT * E].rearrange("p (t e) -> p t e", e=E),
                                     upto[:, :, :].rearrange("p e t -> p t e"), ALU.add))
                for k in range(2):
                    link(v.tensor_tensor(eq[:, :, :], hot[:, k, :, :], place[:, :, :], ALU.mult))
                    link(v.tensor_reduce(pos[:, k, :], eq[:, :, :], AX.X, ALU.add))
                link(v.tensor_copy(pos_i[:, :, :], pos[:, :, :]))
                link(v.tensor_scalar(lane_i[:, :, :], pos_i[:, :, :], P - 1, None, ALU.bitwise_and))
                link(v.tensor_copy(lane[:, :, :], lane_i[:, :, :]))
                link(v.tensor_scalar(pos_i[:, :, :], pos_i[:, :, :], 7, None, ALU.logical_shift_right))
                link(v.tensor_copy(slot[:, :, :], pos_i[:, :, :]))
                link(v.tensor_tensor(past[:, :, :], iota_slot[:, :].unsqueeze(1).to_broadcast([P, E, SLOTS]),
                                     end[:, :].unsqueeze(2).to_broadcast([P, E, SLOTS]), ALU.is_ge))
                link(v.tensor_reduce(who[:, :], past[:, :, :].rearrange("p e s -> p s e"), AX.X, ALU.add))
                link(v.tensor_scalar(who[:, :], who[:, :], float(E - 1), None, ALU.min))
                link(v.tensor_copy(who_i[:, :], who[:, :]))
                link(v.tensor_scalar(odd_i[:, :], who_i[:, :], 1, None, ALU.bitwise_and))
                link(v.tensor_scalar(ready_i[:, :], who[:, :], 1.0, None, ALU.add))
                link(v.tensor_scalar(end_i[:, :], end[:, :], 1.0, None, ALU.add))
                dve.sem_inc(hot_mm, 2)
                with dve.Fori(0, NT) as t:
                    for k in range(2):
                        dve.wait_ge(hot_mm, t * 2 + k + 1)
                        v.tensor_scalar(hot_lane[:, k, :], iota_lane[:, :], lane[:, k, ds(t, 1)], None, ALU.is_equal)
                        v.tensor_scalar(hot_slot[:, k, 0, :], iota_slot[:, :], slot[:, k, ds(t, 1)], tok1[:, ds(t, 1)], ALU.is_equal, ALU.mult)
                        v.tensor_scalar(hot_slot[:, k, 1, :], iota_slot[:, :], slot[:, k, ds(t, 1)], prob[:, k, ds(t, 1)],
                                        ALU.is_equal, ALU.mult).then_inc(hot_set, 1)
                dve.wait_ge(r_pe, 2)
                link(v.tensor_copy(tokp1[:, :], bank[2][:, 0:SLOTS]))
                link(v.tensor_copy(pair_p[:, :], bank[2][:, SLOTS:2 * SLOTS]))
                link(v.tensor_scalar(unused[:, :], tokp1[:, :], 0.0, spare[:, 0:1], ALU.is_equal, ALU.mult))
                link(v.tensor_scalar(tok_f[:, :], tokp1[:, :], -1.0, 0.0, ALU.add, ALU.max))
                link(v.tensor_copy(src_i[:, :], tok_f[:, :]))
                link(v.tensor_tensor(tok_f[:, :], tokp1[:, :], unused[:, :], ALU.add))
                link(v.tensor_scalar(dst_i[:, :], tok_f[:, :], -1.0, None, ALU.add))

        xg = [Xf[:, u * D:(u + 1) * D] for u in range(UNR)]
        xgt = [Xf[:, (3 + u) * D:(4 + u) * D].rearrange("p (k n) -> p k n", k=KD) for u in range(UNR)]
        yv = [Xf[:, (6 + u) * D:(7 + u) * D] for u in range(UNR)]
        col_s = [sb(f"col_s{u}", [P, 1], U32) for u in range(UNR)]
        col_d = [sb(f"col_d{u}", [P, 1], U32) for u in range(UNR)]
        col_p = [sb(f"col_p{u}", [P, 1]) for u in range(UNR)]
        xg_in = [sem(f"xg_in{u}") for u in range(UNR)]
        cols_set, xg_tp, xg_tpev, y_mm, y_act, y_dve, y_out, w_ready, tile_mm = (sem(n) for n in (
            "cols_set", "xg_tp", "xg_tpev", "y_mm", "y_act", "y_dve", "y_out", "w_ready", "tile_mm"))

        with nc.Block() as block:
            @block.sync
            def _(sp):
                for w in range(2):
                    sp.wait_ge(w_in_sem[w], 16)
                    sp.sem_inc(w_ready, 1)
                with sp.Fori(0, E // 2 - 1) as i:
                    for w in range(2):
                        used = sp.value_load(end_i[0:1, ds(i * 2 + w, 1)], min_val=1, max_val=SLOTS + 1)
                        sp.wait_ge(tile_mm, used)
                        sp.dma_start(wslot[:, w, :, :], expert_w[ds(i * 2 + w + 2, 1), :, :].rearrange("a (k p) n -> p (a k) n", p=P)).then_inc(w_in_sem[w], 16)
                    for w in range(2):
                        sp.wait_ge(w_in_sem[w], i * 16 + 32)
                        sp.sem_inc(w_ready, 1)

            @block.gpsimd
            def _(pool):
                g = nc.gpsimd

                def gather(j, u):
                    pool.wait_ge(cols_set, j + 1)
                    hold(pool, xg_tp, j * 2 + 2)
                    g.indirect_dma_start(out=xg[u], out_offset=None, in_=x_nrm[:, :],
                                         in_offset=bass.IndirectOffsetOnAxis(ap=col_s[u][:, 0:1], axis=0)).then_inc(xg_in[u], 16)

                def scatter(j, u, first=False):
                    pool.wait_ge(y_act, j + UNR + 1)
                    pool.wait_ge(y_dve, j + UNR + 1)
                    if not first:
                        pool.wait_ge(y_out, j * 16)
                    pool.sem_inc(held, 1)
                    g.indirect_dma_start(out=out[:, :], out_offset=bass.IndirectOffsetOnAxis(ap=col_d[u][:, 0:1], axis=0),
                                         in_=yv[u], in_offset=None, compute_op=ALU.add).then_inc(y_out, 16)

                for u in range(UNR):
                    gather(u, u)
                scatter(0, 0, first=True)
                with pool.Fori(1, SLOTS // UNR) as i:
                    for u in range(UNR):
                        gather(i * UNR + u, u)
                        scatter(i * UNR + u - 2, (u + 1) % UNR)
                for j in range(SLOTS - 2, SLOTS):
                    scatter(j, j % UNR)
                pool.wait_ge(y_out, SLOTS * 16)

            @block.tensor
            def _(pe):
                pe.sem_inc(xg_tp, 6)
                pe.sem_inc(tile_mm, 1)
                with pe.Fori(0, SLOTS // UNR) as i:
                    for u in range(UNR):
                        j = i * UNR + u
                        pe.wait_ge(xg_in[u], i * 16 + 16)
                        for h in range(2):
                            pe.wait_ge(xg_tpev, j * 2 + h + 1)
                            for c in range(4):
                                k = 4 * h + c
                                mm = nc.tensor.transpose(bank[6 + h][:, c * P:(c + 1) * P], xg[u][:, k * P:(k + 1) * P], ident[:, :])
                            mm.then_inc(xg_tp, 1)
                        ready = pe.value_load(ready_i[0:1, ds(j, 1)], min_val=1, max_val=E)
                        odd = pe.value_load(odd_i[0:1, ds(j, 1)], min_val=0, max_val=1)
                        pe.wait_ge(w_ready, ready)
                        pe.wait_ge(xg_tpev, j * 2 + 4)
                        pe.wait_ge(y_act, j + 1)
                        pe.wait_ge(y_dve, j + 1)
                        for n in range(2):
                            for k in range(KD):
                                mm = nc.tensor.matmul(bank[2 * u + n][:, :], xgt[u][:, k, :],
                                                      Tf[:, ds(odd * (KD * D) + (k * D + n * BANK), BANK)], start=(k == 0), stop=(k == KD - 1))
                            mm.then_inc(y_mm if n == 0 else tile_mm, 1)

            @block.scalar
            def _(act):
                act.sem_inc(xg_tpev, 2)
                act.sem_inc(y_act, UNR)
                with act.Fori(0, SLOTS // UNR) as i:
                    for u in range(UNR):
                        j = i * UNR + u
                        for h in range(2):
                            act.wait_ge(xg_tp, j * 2 + h + 7)
                            nc.scalar.copy(xgt[u][:, 4 * h:4 * h + 4, :].rearrange("p k n -> p (k n)"), bank[6 + h][:, :]).then_inc(xg_tpev, 1)
                        act.wait_ge(y_mm, j + 1)
                        act.wait_ge(cols_set, j + 1)
                        nc.scalar.activation(yv[u][:, 0:BANK], bank[2 * u][:, :], ACT.Copy, scale=col_p[u][:, 0:1]).then_inc(y_act, 1)

            @block.vector
            def _(dve):
                v = nc.vector

                def columns(j, u):
                    v.tensor_copy(col_s[u][:, :], src_i[:, ds(j, 1)])
                    v.tensor_copy(col_d[u][:, :], dst_i[:, ds(j, 1)])
                    v.tensor_copy(col_p[u][:, :], pair_p[:, ds(j, 1)]).then_inc(cols_set, 1)

                dve.sem_inc(y_dve, UNR)
                for u in range(UNR):
                    columns(u, u)
                dve.wait_ge(cols_set, UNR)
                with dve.Fori(0, SLOTS // UNR - 1) as i:
                    for u in range(UNR):
                        j = i * UNR + u
                        dve.wait_ge(tile_mm, j + 2)
                        v.tensor_scalar(yv[u][:, BANK:D], bank[2 * u + 1][:, :], col_p[u][:, 0:1], None, ALU.mult).then_inc(y_dve, 1)
                        dve.wait_ge(y_out, j * 16 + 16)
                        columns(j + UNR, u)
                        dve.wait_ge(cols_set, j + UNR + 1)
                for u in range(UNR):
                    dve.wait_ge(tile_mm, SLOTS - UNR + u + 2)
                    v.tensor_scalar(yv[u][:, BANK:D], bank[2 * u + 1][:, :], col_p[u][:, 0:1], None, ALU.mult).then_inc(y_dve, 1)


_INS = ['x', 'ctx_4096', 'L0_attn_Win', 'L0_attn_bin', 'L0_attn_ln1_w', 'L0_attn_ln1_b', 'L0_attn_phz_re', 'L0_attn_phz_im',
        'L0_attn_lc_re', 'L0_attn_lc_im', 'L0_attn_sc_lin', 'L0_attn_ln2_w', 'L0_attn_ln2_b', 'L0_attn_W1', 'L0_attn_b1',
        'L0_attn_W2', 'L0_attn_b2', 'L0_attn_lnl_w', 'L0_attn_lnl_b', 'L0_attn_Wout', 'L0_attn_bout', 'L0_xattn_conv_w',
        'L0_xattn_bn_gamma', 'L0_xattn_bn_beta', 'L0_ffn_gate_w', 'L0_ffn_expert_w']


def kernel(**inputs):
    import numpy as _np
    import concourse.bacc as _bacc
    from concourse import mybir as _mybir
    from concourse.bass_utils import run_bass_kernel_spmd as _run

    nc = _bacc.Bacc("TRN2", target_bir_lowering=False, num_devices=1)
    arrays, args = {}, []
    for name in _INS:
        a = _np.ascontiguousarray(inputs[name])
        arrays[f"in_{name}_dram"] = a
        args.append(nc.dram_tensor(f"in_{name}_dram", a.shape, _mybir.dt.from_np(a.dtype), kind="ExternalInput").ap())
    b, s, d = inputs["x"].shape
    res = nc.dram_tensor("out_0_dram", (b * s + 128, d), _mybir.dt.float32, kind="ExternalOutput").ap()
    decoder_kernel(nc, *args, res)
    r = _run(nc, [arrays], core_ids=[0])
    return r.results[0]["out_0_dram"][:b * s].reshape(b, s, d)
```

```python
from contextlib import ExitStack

import concourse.bass as bass
from concourse import mybir

F32 = mybir.dt.float32
I32 = mybir.dt.int32
U32 = mybir.dt.uint32
BF16 = mybir.dt.bfloat16

ALU = mybir.AluOpType
ACT = mybir.ActivationFunctionType
AX = mybir.AxisListType
ds = bass.ds

P = 128
BANK = 512
EPS = 1e-5
FLT_MAX = 3.4028234663852886e38
LAMBDA = 0.6


def crucial_count(c):
    f = int(LAMBDA * c // 1)
    return f + f % 2


def decoder_kernel(nc, x, ctx_map, w_in, b_in, ln1_w, ln1_b, phz_re, phz_im, lc_re, lc_im, sc_lin, ln2_w, ln2_b,
                   w1, b1, w2, b2, lnl_w, lnl_b, w_out, b_out, conv_w, bn_gamma, bn_beta, gate_w, expert_w, out):
    B, S, D = x.shape
    DM = w_in.shape[0]
    NL = ln1_w.shape[0]
    FF = w1.shape[1]
    E = gate_w.shape[1]
    N = B * S
    NT = N // P
    KD = D // P
    FT = FF // P
    CW = BANK
    CH = N // CW
    TPC = CW // P
    BPC = CW // S
    CT = S // P
    KC = crucial_count(S)
    KS = S - KC
    ROUNDS = -(-KS // 8)
    PADS = ROUNDS * 8 - KS
    SLOTS = 2 * N // P + E - 1
    UNR = 3
    TAPS = conv_w.shape[2]
    HALF = TAPS // 2
    assert DM == P and SLOTS % UNR == 0 and D == 2 * BANK

    x2d = x.rearrange("b s d -> (b s) d")
    x_nrm = nc.dram_tensor("x_nrm", [N, D], F32, kind="Internal").ap()

    ctx = ExitStack()
    with ctx:
        def sb(name, shape, dt=F32):
            return ctx.enter_context(nc.sbuf_tensor(name, shape, dt))

        def sem(name):
            return ctx.enter_context(nc.semaphore(name))

        X = sb("X", [P, NT, D])
        Xf = X[:, :, :].rearrange("p t d -> p (t d)")
        T = sb("T", [P, KD, N])
        Tf = T[:, :, :].rearrange("p k n -> p (k n)")
        M = sb("M", [P, KD, N], mybir.dt.bfloat16)
        H = sb("H", [P, N])
        nat = sb("nat", [P, TPC, D])
        natf = nat[:, :, :].rearrange("p u d -> p (u d)")
        fin = sb("fin", [P, 2, CW])
        bank = [ctx.enter_context(nc.psum_tensor(f"bank{i}", [P, BANK], F32)) for i in range(8)]

        ident = sb("ident", [P, P])
        ones = sb("ones", [P, P])
        utri = sb("utri", [P, P])
        center = sb("center", [P, P])
        inv_col = sb("inv_col", [P, 1])
        neg_half = sb("neg_half", [P, NT])
        pos_half = sb("pos_half", [P, NT])
        late = sb("late", [P, 2 * D])
        wout_t, bout_b = late[:, 0:D], late[:, D:2 * D]
        gate = sb("gate", [P, KD, E])
        convw = sb("convw", [P, 2 * TAPS])
        bn_gb = sb("bn_gb", [P, 2])
        ewide = sb("ewide", [P, 3 * P + TAPS - 1])
        band = sb("band", [P, 2, 3 * P])
        layer_par = sb("layer_par", [P, NL, 13])
        block_par = sb("block_par", [P, 4])
        cur = sb("cur", [P, 13])
        st6 = sb("st6", [P, TPC, 12])
        mv = sb("mv", [P, TPC, 2])
        ve = sb("ve", [P, TPC, 4])
        rs = sb("rs", [P, TPC, 4])

        o = 8192

        def in_t(n):
            nonlocal o
            o += n
            return Tf[:, o - n:o]

        cos_t = in_t(NL * S).rearrange("p (l s) -> p l s", l=NL)
        sin_t = in_t(NL * S).rearrange("p (l s) -> p l s", l=NL)
        win_t = in_t(D).rearrange("p (k m) -> p k m", k=KD)
        w1raw = in_t(FF).rearrange("p (t m) -> p t m", t=FT)
        w2raw = in_t(FF)
        w1u = in_t(FF)
        w1s = in_t(FF)
        w2c = in_t(FF).rearrange("p (t m) -> p t m", t=FT)
        cs = in_t(P)
        b1f = in_t(FT)
        rows = in_t(P)
        ph = in_t(4 * NL).rearrange("p (k l) -> p k l", k=4)
        tmp = in_t(16 * NL).rearrange("p (k l) -> p k l", k=16)
        tab = in_t(4 * NL * S // 2).rearrange("p (k l s) -> p k l s", k=4, l=NL)
        assert o <= KD * N

        LN1W, LN1B, SCL, LN2W, LN2B, B2, B1, RHO, UR0, UI0 = 0, 1, 2, 3, 4, 5, 6, 10, 11, 12

        iota_lane = sb("iota_lane", [P, P])
        iota_slot = sb("iota_slot", [P, SLOTS])
        rev_e = sb("rev_e", [P, NT, E])
        step_t = sb("step_t", [P, E, NT])
        later_t = sb("later_t", [P, E * NT])
        tok1 = sb("tok1", [P, NT])
        spare = sb("spare", [P, 1])

        ld_rows = sem("ld_rows")
        ld_win = sem("ld_win")
        ld_wout = sem("ld_wout")
        ld_misc = sem("ld_misc")
        const_ready = sem("const_ready")
        set_pe = sem("set_pe")
        set_act = sem("set_act")
        set_dve = sem("set_dve")
        set_pool = sem("set_pool")
        NCONST = 9
        NIOTA = 6
        io = Xf[:, 0:1024].bitcast(I32)
        io_lane, io_slot = io[:, 0:P], io[:, 128:128 + SLOTS]
        io_rev = io[:, 256:384].rearrange("p (t e) -> p t e", e=E)
        io_step = io[:, 384:512].rearrange("p (e t) -> p e t", e=E)
        io_tok, io_spare = io[:, 512:528], io[:, 528:529]

        with nc.Block() as block:
            @block.sync
            def _(sp):
                for k, par in enumerate([ln1_w, ln1_b, sc_lin, ln2_w, ln2_b, b2, phz_re, phz_im, lc_re, lc_im]):
                    sp.dma_start(rows[k * NL:(k + 1) * NL, :], par[:, :]).then_inc(ld_rows, 16)
                sp.dma_start(rows[40:56, :], b1.rearrange("l (t p) -> (l t) p", p=P)).then_inc(ld_rows, 16)
                for k, par in enumerate([b_in, lnl_w, lnl_b]):
                    sp.dma_start(rows[56 + k:57 + k, :], par.rearrange("(a d) -> a d", a=1)).then_inc(ld_rows, 16)
                sp.dma_start(nat[:, 0, :], w_in[:, :]).then_inc(ld_win, 16)
                sp.dma_start(nat[:, 1, :].rearrange("p (t d) -> p t d", t=KD),
                             w_out.rearrange("(t p) d -> p t d", p=P)).then_inc(ld_wout, 16)
                sp.dma_start(bout_b, b_out.rearrange("(a d) -> a d", a=1).to_broadcast([P, D])).then_inc(ld_misc, 16)
                sp.dma_start(convw[:, :], conv_w.rearrange("a c j -> a (c j)").to_broadcast([P, 2 * TAPS])).then_inc(ld_misc, 16)
                sp.dma_start(bn_gb[:, 0:1], bn_gamma.rearrange("(a d) -> a d", a=1).to_broadcast([P, 1])).then_inc(ld_misc, 16)
                sp.dma_start(bn_gb[:, 1:2], bn_beta.rearrange("(a d) -> a d", a=1).to_broadcast([P, 1])).then_inc(ld_misc, 16)
                sp.dma_start(gate[:, :, :], gate_w.rearrange("(k p) e -> p k e", p=P)).then_inc(ld_misc, 16)
                sp.wait_ge(ld_misc, 5 * 16)

            @block.gpsimd
            def _(pool):
                g = nc.gpsimd
                g.memset(ident[:, :], 0.0).then_inc(const_ready, 1)
                g.memset(ones[:, :], 1.0).then_inc(const_ready, 1)
                g.memset(ewide[:, :], 0.0).then_inc(const_ready, 1)
                g.memset(inv_col[:, :], 1.0 / P).then_inc(const_ready, 1)
                g.memset(neg_half[:, :], -0.5).then_inc(const_ready, 1)
                g.memset(pos_half[:, :], 0.5).then_inc(const_ready, 1)
                pool.wait_ge(const_ready, 6)
                g.affine_select(out=ident[:, :], in_=ident[:, :], compare_op=ALU.not_equal, fill=1.0, base=0,
                                pattern=[[-1, P]], channel_multiplier=1).then_inc(const_ready, 1)
                g.affine_select(out=utri[:, :], in_=ones[:, :], compare_op=ALU.is_gt, fill=0.0, base=0,
                                pattern=[[1, P]], channel_multiplier=-1).then_inc(const_ready, 1)
                g.affine_select(out=ewide[:, :], in_=ewide[:, :], compare_op=ALU.not_equal, fill=1.0, base=-(P + HALF),
                                pattern=[[1, 3 * P + TAPS - 1]], channel_multiplier=-1).then_inc(const_ready, 1)
                g.iota(io_lane, [[1, P]], base=0, channel_multiplier=0).then_inc(const_ready, 1)
                g.iota(io_slot, [[1, SLOTS]], base=0, channel_multiplier=0).then_inc(const_ready, 1)
                g.iota(io_rev, [[0, NT], [-1, E]], base=E, channel_multiplier=0).then_inc(const_ready, 1)
                g.iota(io_step, [[0, E], [P, NT]], base=0, channel_multiplier=0).then_inc(const_ready, 1)
                g.iota(io_tok, [[P, NT]], base=1, channel_multiplier=1).then_inc(const_ready, 1)
                g.iota(io_spare, [[0, 1]], base=N + 1, channel_multiplier=1).then_inc(const_ready, 1)
                pool.wait_ge(set_dve, 17)
                g.tensor_tensor(tmp[:, 8, :], tmp[:, 6, :], pos_half[:, 0:NL], ALU.pow).then_inc(set_pool, 1)
                g.tensor_tensor(tmp[:, 9, :], tmp[:, 6, :], neg_half[:, 0:NL], ALU.pow).then_inc(set_pool, 1)

            @block.tensor
            def _(pe):
                pe.wait_ge(const_ready, NCONST)
                pe.wait_ge(ld_rows, 14 * 16)
                nc.tensor.transpose(bank[0][:, 0:59], rows[0:59, :], ident[0:59, 0:59]).then_inc(set_pe, 1)
                pe.wait_ge(ld_wout, 16)
                for t in range(KD):
                    mm = nc.tensor.transpose(bank[2 + t // 4][:, (t % 4) * P:(t % 4 + 1) * P],
                                             nat[:, 1, t * P:(t + 1) * P], ident[:, :])
                mm.then_inc(set_pe, 1)
                pe.wait_ge(set_dve, 4)
                nc.tensor.matmul(bank[1][:, 0:NL], center[:, :], layer_par[:, :, B2], start=True, stop=True)
                nc.tensor.matmul(bank[1][:, NL:NL + 1], center[:, :], block_par[:, 0:1],
                                 start=True, stop=True).then_inc(set_pe, 1)
                pe.wait_ge(ld_win, 16)
                for t in range(KD):
                    mm = nc.tensor.matmul(bank[4 + t // 4][:, (t % 4) * P:(t % 4 + 1) * P],
                                          nat[:, 0, t * P:(t + 1) * P], center[:, :], start=True, stop=True)
                mm.then_inc(set_pe, 1)
                pe.wait_ge(set_act, 2)
                for n in range(2):
                    mm = nc.tensor.matmul(bank[6 + n][:, :], block_par[:, 2:3].to_broadcast([P, P]),
                                          nat[:, 2, n * BANK:(n + 1) * BANK], start=True, stop=True)
                mm.then_inc(set_pe, 1)

            @block.scalar
            def _(act):
                act.wait_ge(set_pe, 2)
                for n in range(2):
                    nc.scalar.copy(nat[:, 2, n * BANK:(n + 1) * BANK], bank[2 + n][:, :]).then_inc(set_act, 1)
                act.wait_ge(set_pe, 4)
                for n in range(2):
                    nc.scalar.copy(win_t[:, 4 * n:4 * n + 4, :].rearrange("p k m -> p (k m)"), bank[4 + n][:, :]).then_inc(set_act, 1)
                act.wait_ge(set_dve, 18)
                nc.scalar.activation(layer_par[:, :, RHO], tmp[:, 10, :], ACT.Tanh).then_inc(set_act, 1)

            @block.vector
            def _(dve):
                v = nc.vector
                n_link = [0]

                def link(ins):
                    n_link[0] += 1
                    ins.then_inc(set_dve, 1)
                    dve.wait_ge(set_dve, n_link[0])

                dve.wait_ge(const_ready, NCONST)
                link(v.tensor_scalar(center[:, :], ident[:, :], -1.0 / P, None, ALU.add))
                dve.wait_ge(set_pe, 1)
                link(v.tensor_copy(layer_par[:, :, 0:6], bank[0][:, 0:24].rearrange("p (k l) -> p l k", k=6)))
                link(v.tensor_copy(layer_par[:, :, B1:B1 + FT], bank[0][:, 40:56].rearrange("p (l t) -> p l t", l=NL)))
                link(v.tensor_copy(block_par[:, 0:3], bank[0][:, 56:59]))
                link(v.tensor_copy(ph[:, :, :], bank[0][:, 24:40].rearrange("p (k l) -> p k l", k=4)))
                re, im, lr, li = (ph[:, k, :] for k in range(4))
                t_re, t_im, t_max, t_inv, t_a, t_b, t_q, t_z, t_sq, t_rsq, t_r, c_m, s_m, t_c, t_s = (tmp[:, k, :] for k in range(15))
                link(v.scalar_tensor_tensor(t_re, re, -1.0, re, ALU.mult, ALU.max))
                link(v.scalar_tensor_tensor(t_im, im, -1.0, im, ALU.mult, ALU.max))
                link(v.tensor_tensor(t_max, t_re, t_im, ALU.max))
                link(v.tensor_scalar(t_inv, t_max, 1e-37, None, ALU.max))
                link(v.reciprocal(t_inv, t_inv))
                link(v.tensor_tensor(t_a, re, t_inv, ALU.mult))
                link(v.tensor_tensor(t_b, im, t_inv, ALU.mult))
                link(v.tensor_scalar(t_z, t_max, 0.0, None, ALU.is_equal))
                link(v.tensor_tensor(t_a, t_a, t_z, ALU.add))
                link(v.tensor_tensor(t_c, t_a, t_a, ALU.mult))
                link(v.tensor_tensor(t_s, t_b, t_b, ALU.mult))
                link(v.tensor_tensor(t_q, t_c, t_s, ALU.add))
                dve.wait_ge(set_pool, 2)
                link(v.tensor_tensor(t_r, t_max, t_sq, ALU.mult))
                assert n_link[0] == 18
                link(v.tensor_tensor(c_m, t_a, t_rsq, ALU.mult))
                link(v.tensor_tensor(s_m, t_b, t_rsq, ALU.mult))
                link(v.tensor_tensor(t_re, lr, c_m, ALU.mult))
                link(v.tensor_tensor(t_im, li, s_m, ALU.mult))
                link(v.tensor_tensor(layer_par[:, :, UR0], t_re, t_im, ALU.subtract))
                link(v.tensor_tensor(t_re, lr, s_m, ALU.mult))
                link(v.tensor_tensor(t_im, li, c_m, ALU.mult))
                link(v.tensor_tensor(t_re, t_re, t_im, ALU.add))
                link(v.tensor_scalar(layer_par[:, :, UI0], t_re, -1.0, None, ALU.mult))
                link(v.memset(cos_t[:, :, 0:1], 1.0))
                link(v.memset(sin_t[:, :, 0:1], 0.0))
                m = 1
                while m < S:
                    cb = c_m.unsqueeze(2).to_broadcast([P, NL, m])
                    sb_ = s_m.unsqueeze(2).to_broadcast([P, NL, m])
                    link(v.tensor_tensor(tab[:, 0, :, 0:m], cos_t[:, :, 0:m], cb, ALU.mult))
                    link(v.tensor_tensor(tab[:, 1, :, 0:m], sin_t[:, :, 0:m], sb_, ALU.mult))
                    link(v.tensor_tensor(tab[:, 2, :, 0:m], sin_t[:, :, 0:m], cb, ALU.mult))
                    link(v.tensor_tensor(tab[:, 3, :, 0:m], cos_t[:, :, 0:m], sb_, ALU.mult))
                    link(v.tensor_tensor(cos_t[:, :, m:2 * m], tab[:, 0, :, 0:m], tab[:, 1, :, 0:m], ALU.subtract))
                    link(v.tensor_tensor(sin_t[:, :, m:2 * m], tab[:, 2, :, 0:m], tab[:, 3, :, 0:m], ALU.add))
                    link(v.tensor_tensor(t_c, c_m, c_m, ALU.mult))
                    link(v.tensor_tensor(t_s, s_m, s_m, ALU.mult))
                    link(v.tensor_tensor(t_q, c_m, s_m, ALU.mult))
                    link(v.tensor_tensor(c_m, t_c, t_s, ALU.subtract))
                    link(v.tensor_scalar(s_m, t_q, 2.0, None, ALU.mult))
                    m *= 2
                dve.wait_ge(set_pe, 3)
                link(v.tensor_copy(layer_par[:, :, B2], bank[1][:, 0:NL]))
                link(v.tensor_copy(block_par[:, 0:1], bank[1][:, NL:NL + 1]))
                dve.wait_ge(set_act, 2)
                for n in range(2):
                    link(v.tensor_scalar(wout_t[:, n * BANK:(n + 1) * BANK], bank[2 + n][:, :], block_par[:, 1:2], None, ALU.mult))
                dve.wait_ge(set_pe, 5)
                dve.wait_ge(ld_misc, 5 * 16)
                for n in range(2):
                    link(v.tensor_tensor(bout_b[:, n * BANK:(n + 1) * BANK], bank[6 + n][:, :],
                                         bout_b[:, n * BANK:(n + 1) * BANK], ALU.add))
                for c in range(2):
                    link(v.tensor_scalar(band[:, c, :], ewide[:, 0:3 * P], convw[:, c * TAPS:c * TAPS + 1], None, ALU.mult))
                    for j in range(1, TAPS):
                        w = convw[:, c * TAPS + j:c * TAPS + j + 1]
                        link(v.scalar_tensor_tensor(band[:, c, :], ewide[:, j:j + 3 * P], w, band[:, c, :], ALU.mult, ALU.add))
                dve.wait_ge(const_ready, NCONST + NIOTA)
                link(v.tensor_copy(iota_lane[:, :], io_lane))
                link(v.tensor_copy(iota_slot[:, :], io_slot))
                link(v.tensor_copy(rev_e[:, :, :], io_rev))
                link(v.tensor_copy(step_t[:, :, :], io_step))
                link(v.tensor_copy(tok1[:, :], io_tok))
                link(v.tensor_copy(spare[:, :], io_spare))
                link(v.tensor_scalar(later_t[:, :], step_t[:, :, :].rearrange("p e t -> p (e t)"), 0.0, None, ALU.is_gt))

        held = sem("held")

        def hold(eng, done, n):
            eng.wait_ge(done, n)
            eng.sem_inc(held, 1)

        ln_stat = sem("ln_stat")
        ln_mean = sem("ln_mean")
        ln_var = sem("ln_var")
        ln_rstd = sem("ln_rstd")
        ln_out = sem("ln_out")

        def ln_stats(dve, src, u, n):
            v = nc.vector
            v.bn_stats(st6[:, u, 0:6], src[:, 0:BANK])
            v.bn_stats(st6[:, u, 6:12], src[:, BANK:D]).then_inc(ln_stat, 1)
            hold(dve, ln_stat, n)
            v.bn_aggr(mv[:, u, :], st6[:, u, :]).then_inc(ln_mean, 1)
            dve.wait_ge(ln_mean, n)
            v.tensor_scalar(ve[:, u, 0:1], mv[:, u, 1:2], EPS, None, ALU.add).then_inc(ln_var, 1)

        def ln_pow(pool, u, n):
            pool.wait_ge(ln_var, n)
            nc.gpsimd.tensor_tensor(rs[:, u, 0:1], ve[:, u, 0:1], neg_half[:, 0:1], ALU.pow).then_inc(ln_rstd, 1)

        def ln_apply(dve, dst, src, u, n):
            dve.wait_ge(ln_rstd, n)
            nc.vector.tensor_scalar(dst, src, mv[:, u, 0:1], rs[:, u, 0:1], ALU.subtract, ALU.mult).then_inc(ln_out, 1)

        x_in = [sem(f"x_in{u}") for u in range(TPC)]
        emb_tp = sem("emb_tp")
        emb_tpev = sem("emb_tpev")
        emb_mm = sem("emb_mm")
        emb_ev = sem("emb_ev")
        xn_t = X[:, :, :].rearrange("p t d -> p (t d)").rearrange("p (k n) -> p k n", k=KD)

        with nc.Block() as block:
            @block.sync
            def _(sp):
                with sp.Fori(0, CH) as q:
                    for u in range(TPC):
                        sp.wait_ge(emb_tp, q * 8 + 2 * u + 2)
                        sp.dma_start(nat[:, u, :], x2d[ds(q * CW + u * P, P), :]).then_inc(x_in[u], 16)

            @block.gpsimd
            def _(pool):
                with pool.Fori(0, CH) as q:
                    for u in range(TPC):
                        ln_pow(pool, u, q * TPC + u + 1)

            @block.vector
            def _(dve):
                with dve.Fori(0, CH) as q:
                    for u in range(TPC + 1):
                        if u < TPC:
                            dve.wait_ge(x_in[u], q * 16 + 16)
                            ln_stats(dve, nat[:, u, :], u, q * TPC + u + 1)
                        if u > 0:
                            ln_apply(dve, nat[:, u - 1, :], nat[:, u - 1, :], u - 1, q * TPC + u)

            @block.tensor
            def _(pe):
                pe.sem_inc(emb_tp, 8)
                with pe.Fori(0, CH) as q:
                    for u in range(TPC):
                        pe.wait_ge(ln_out, q * TPC + u + 1)
                        for h in range(2):
                            pe.wait_ge(emb_tpev, q * 8 + 2 * u + h + 1)
                            for j in range(4):
                                k = 4 * h + j
                                mm = nc.tensor.transpose(bank[2 * (u % 2) + h][:, j * P:(j + 1) * P], nat[:, u, k * P:(k + 1) * P], ident[:, :])
                            mm.then_inc(emb_tp, 1)
                    pe.wait_ge(emb_tpev, q * 8 + 12)
                    pe.wait_ge(emb_ev, q + 1)
                    for k in range(KD):
                        mm = nc.tensor.matmul(bank[4][:, :], win_t[:, k, :], xn_t[:, k, ds(q * CW, CW)], start=(k == 0), stop=(k == KD - 1))
                    mm.then_inc(emb_mm, 1)

            @block.scalar
            def _(act):
                act.sem_inc(emb_tpev, 4)
                act.sem_inc(emb_ev, 1)
                with act.Fori(0, CH) as q:
                    for u in range(TPC):
                        for h in range(2):
                            act.wait_ge(emb_tp, q * 8 + 2 * u + h + 9)
                            nc.scalar.copy(xn_t[:, 4 * h:4 * h + 4, ds(q * CW + u * P, P)],
                                           bank[2 * (u % 2) + h][:, :].rearrange("p (k n) -> p k n", k=4)).then_inc(emb_tpev, 1)
                    act.wait_ge(emb_mm, q + 1)
                    nc.scalar.activation(H[:, ds(q * CW, CW)], bank[4][:, :], ACT.Identity, bias=block_par[:, 0:1]).then_inc(emb_ev, 1)

        assert B == 2 * NL
        GT = 2 * KD
        NG = B // 2
        QUICK = 2
        WINDOW = 8 * QUICK
        WK = WINDOW + S
        LOW, HIGH = -0.5, 0.0
        AIM = KS - WINDOW / 2 + 0.5
        AIM_S = 2 * AIM - S
        cT = Xf[:, 8192:16384].rearrange("p (b k s) -> p b k s", b=4, k=KD)
        tabf = tab.rearrange("p k l s -> p (k l s)")
        cin = [[tabf[:, 0:D], tabf[:, D:2 * D]],
               [win_t.rearrange("p k m -> p (k m)"), fin[:, :, :].rearrange("p a n -> p (a n)")]]
        w = Tf[:, 0:GT * WK].rearrange("p (i s) -> p i s", i=GT)
        under = Tf[:, GT * WK:GT * WK + GT * S // 2].bitcast(BF16).rearrange("p (i s) -> p i s", i=GT)
        so = GT * WK + GT * S // 2

        def in_sel(*shape):
            nonlocal so
            n = 1
            for d in shape:
                n *= d
            so += n
            assert so <= 8192
            names = "abc"[:len(shape)]
            return Tf[:, so - n:so].rearrange(f"p ({' '.join(names)}) -> p {' '.join(names)}", **dict(zip(names, shape)))

        st_c, mv_c = in_sel(GT, 6), in_sel(GT, 2)
        dev, t_lo, t_hi, width, t_1, t_2, s_lo, s_hi, s_1, rise, inv, miss, side, step = (in_sel(GT) for _ in range(14))
        c_low, c_width, c_one, c_aim, c_inv = (in_sel(GT) for _ in range(5))
        m_cnt, off = in_sel(GT), in_sel(GT)
        top8 = in_sel(GT, 8)
        pad01 = w[:, :, 0:WINDOW]
        pad_neg = in_sel(GT, WINDOW)
        off_max, off_any, off_one = in_sel(NG), in_sel(1), in_sel(1)
        off_i = sb("off_i", [P, 1], I32)
        ctx_in = [[sem(f"ctx_in{u}{h}") for h in range(CT)] for u in range(2)]
        ctx_tp, ctx_set, c_stat, c_mean, sel_pool = (sem(n) for n in ("ctx_tp", "ctx_set", "c_stat", "c_mean", "sel_pool"))
        t0_set, s0_sum, t1_set, s1_sum, t2_set, counted, sel_small, w_set = (sem(n) for n in (
            "t0_set", "s0_sum", "t1_set", "s1_sum", "t2_set", "counted", "sel_small", "w_set"))
        round_max, round_rep, mask_done, off_set, off_mm = (sem(n) for n in ("round_max", "round_rep", "mask_done", "off_set", "off_mm"))

        CHAIN = 29
        hid = Xf[:, 0:2 * FT * CW].rearrange("p (q t n) -> p q t n", q=2, t=FT)
        a_buf = Xf[:, 4096:6144]
        b_buf = Xf[:, 6144:8192]
        yn, sq = natf[:, 0:N], natf[:, N:2 * N]
        BC, ZO, HD, VAR, SMALL, PREP = (0, 1), (2, 3), (4, 5), (6, 7), 6, 7
        w1_in, w2_in = sem("w1_in"), sem("w2_in")
        cur_set, cs_set = sem("cur_set"), sem("cs_set")
        w1_tp, w1_u, w1_s, w2_tp, w2_set, b1_mm, b1_set = (sem(n) for n in ("w1_tp", "w1_u", "w1_s", "w2_tp", "w2_set", "b1_mm", "b1_set"))
        sq1, var1, ve1, rt1, bc1, yn1 = (sem(n) for n in ("sq1", "var1", "ve1", "rt1", "bc1", "yn1"))
        sq2, var2, ve2, rt2, bc2, yn2 = (sem(n) for n in ("sq2", "var2", "ve2", "rt2", "bc2", "yn2"))
        act1, a_in, b_in, scanned, a_out, b_out, z_mm, h_mid = (sem(n) for n in ("act1", "a_in", "b_in_", "scanned", "a_out", "b_out_", "z_mm", "h_mid"))
        hid_mm, hid_act, o_mm, h_out = (sem(n) for n in ("hid_mm", "hid_act", "o_mm", "h_out"))

        def chunk(buf, q):
            return buf[:, q * CW:(q + 1) * CW]

        def by_seq(buf, q):
            return chunk(buf, q).rearrange("p (b s) -> p b s", b=BPC)

        def variance(q):
            for i in range(TPC):
                mm = nc.tensor.matmul(bank[VAR[q % 2]][:, i:i + 1], chunk(sq, q)[:, i * P:(i + 1) * P], inv_col[:, :], start=True, stop=True)
            return mm

        def spread(q):
            for i in range(TPC):
                mm = nc.tensor.matmul(bank[BC[q % 2]][:, i * P:(i + 1) * P], rs[:, q, i:i + 1].to_broadcast([P, P]), ident[:, :], start=True, stop=True)
            return mm

        with nc.Block() as block:
            @block.sync
            def _(sp):
                sp.sem_inc(w1_tp, 1)
                sp.sem_inc(w2_tp, 1)
                sp.sem_inc(ctx_tp, 8)
                with sp.Fori(0, NL) as l:
                    sp.wait_ge(w1_tp, l + 1)
                    sp.dma_start(w1raw, w1[ds(l, 1), :, :].rearrange("a (t p) d -> p (a t) d", p=P)).then_inc(w1_in, 16)
                    sp.wait_ge(w2_tp, l + 1)
                    sp.dma_start(w2raw, w2[ds(l, 1), :, :].rearrange("a p f -> p (a f)")).then_inc(w2_in, 16)
                    for u in range(2):
                        sp.wait_ge(ctx_tp, l * 8 + 4 * u + 4)
                        for h in range(CT):
                            sp.dma_start(cin[u][h], ctx_map[ds(l * 2 + u, 1), h * P:(h + 1) * P, :].rearrange("a p l -> p (a l)")).then_inc(ctx_in[u][h], 16)

            @block.gpsimd
            def _(pool):
                g = nc.gpsimd

                def power(q, n, ve_done, done):
                    pool.wait_ge(ve_done, n)
                    g.tensor_tensor(rs[:, q, :], ve[:, q, :], neg_half[:, 0:TPC], ALU.pow).then_inc(done, 1)

                def chain(g_, n, *how):
                    pool.wait_ge(sel_pool, g_ * CHAIN + n + 1)
                    g.tensor_tensor(*how).then_inc(sel_pool, 1)

                def chained(g_, n, done):
                    pool.wait_ge(sel_pool, g_ * CHAIN + n + 1)
                    pool.sem_inc(done, 1)

                def first_thresholds(g_):
                    pool.wait_ge(c_mean, g_ * GT + GT)
                    for n, how in enumerate((
                            (dev, mv_c[:, :, 1], pos_half[:, 0:GT], ALU.pow),
                            (t_lo, dev, c_low, ALU.mult),
                            (t_lo, t_lo, mv_c[:, :, 0], ALU.add),
                            (width, dev, c_width, ALU.mult),
                            (t_hi, t_lo, width, ALU.add))):
                        chain(g_, n, *how)
                    chained(g_, 5, t0_set)

                def third_threshold(g_):
                    pool.wait_ge(s0_sum, g_ * (2 * GT) + 2 * GT)
                    for n, how in enumerate((
                            (rise, s_hi, s_lo, ALU.subtract),
                            (inv, rise, rise, ALU.mult),
                            (inv, inv, c_one, ALU.add),
                            (inv, inv, c_inv, ALU.pow),
                            (inv, inv, rise, ALU.mult),
                            (miss, c_aim, s_lo, ALU.subtract),
                            (miss, miss, width, ALU.mult),
                            (miss, miss, inv, ALU.mult),
                            (t_1, t_lo, miss, ALU.add))):
                        chain(g_, 5 + n, *how)
                    chained(g_, 14, t1_set)

                def last_threshold(g_):
                    pool.wait_ge(s1_sum, g_ * GT + GT)
                    hold(pool, sel_pool, g_ * CHAIN + 15)
                    g.tensor_scalar(side, s_1, AIM_S, None, ALU.is_le).then_inc(sel_pool, 1)
                    pool.wait_ge(counted, g_ * GT + 1)
                    for n, how in enumerate((
                            (rise, rise, side, ALU.mult),
                            (rise, rise, s_lo, ALU.add),
                            (rise, rise, s_1, ALU.subtract),
                            (width, width, side, ALU.mult),
                            (width, width, t_lo, ALU.add),
                            (width, width, t_1, ALU.subtract),
                            (inv, rise, rise, ALU.mult),
                            (inv, inv, c_one, ALU.add),
                            (inv, inv, c_inv, ALU.pow),
                            (rise, rise, inv, ALU.mult),
                            (rise, rise, width, ALU.mult),
                            (miss, c_aim, s_1, ALU.subtract),
                            (miss, miss, rise, ALU.mult),
                            (t_2, t_1, miss, ALU.add))):
                        chain(g_, 15 + n, *how)
                    chained(g_, CHAIN, t2_set)

                def layer(l):
                    sin_l = sin_t[:, ds(l, 1), :].to_broadcast([P, BPC, S])
                    for q in range(CH):
                        hold(pool, act1, l * CH + q + 1)
                        g.tensor_tensor(by_seq(b_buf, q), by_seq(yn, q), sin_l, ALU.mult).then_inc(b_in, 1)
                    for q in range(CH):
                        hold(pool, scanned, l * CH + q + 1)
                        g.tensor_tensor(by_seq(b_buf, q), by_seq(b_buf, q), sin_l, ALU.mult).then_inc(b_out, 1)
                    if not isinstance(l, int):
                        last_threshold(l - 1)
                    for q in range(CH):
                        power(q, l * CH + q + 1, ve2, rt2)
                        if q == 1:
                            first_thresholds(l)
                    for q in range(CH):
                        power(q, l * CH + q + CH + 1, ve1, rt1)
                        if q == 0:
                            third_threshold(l)

                for dst, val in ((c_low, LOW), (c_width, HIGH - LOW), (c_one, 1.0), (c_aim, AIM_S), (c_inv, -1.0)):
                    ins = g.memset(dst, val)
                ins.then_inc(sel_pool, 1)
                for q in range(CH):
                    power(q, q + 1, ve1, rt1)
                layer(0)
                with pool.Fori(1, NL) as l:
                    layer(l)
                last_threshold(NG - 1)

            @block.tensor
            def _(pe):
                def var_first(q, n):
                    pe.wait_ge(sq1, n)
                    if q >= 2:
                        pe.wait_ge(ve1, n - 2)
                    variance(q).then_inc(var1, 1)

                def spread_first(q, n):
                    pe.wait_ge(rt1, n)
                    if q >= 2:
                        pe.wait_ge(yn1, n - 2)
                    spread(q).then_inc(bc1, 1)

                for q in range(CH):
                    var_first(q, q + 1)
                for q in range(CH):
                    spread_first(q, q + 1)
                with pe.Fori(0, NL) as l:
                    base = l * CH

                    def z(q):
                        pe.wait_ge(a_out, base + q + 1)
                        pe.wait_ge(b_out, base + q + 1)
                        if q >= 2:
                            pe.wait_ge(h_mid, base + q - 1)
                        nc.tensor.matmul(bank[ZO[q % 2]][:, :], cs, chunk(a_buf, q), start=True, stop=False)
                        nc.tensor.matmul(bank[ZO[q % 2]][:, :], cs, chunk(b_buf, q), start=False, stop=True).then_inc(z_mm, 1)

                    def var_second(q):
                        pe.wait_ge(sq2, base + q + 1)
                        if q >= 2:
                            pe.wait_ge(ve2, base + q - 1)
                        variance(q).then_inc(var2, 1)

                    def spread_second(q):
                        pe.wait_ge(rt2, base + q + 1)
                        if q >= 2:
                            pe.wait_ge(yn2, base + q - 1)
                        spread(q).then_inc(bc2, 1)

                    def feed_forward(q):
                        pe.wait_ge(yn2, base + q + 1)
                        if q == 0:
                            pe.wait_ge(ctx_set, l * 8 + 10)
                        for t in range(FT):
                            pe.wait_ge(hid_act, l * (CH * FT) + q * FT + t + 1)
                            nc.tensor.matmul(bank[HD[t % 2]][:, :], w1s[:, t * P:(t + 1) * P], chunk(yn, q), start=True, stop=True).then_inc(hid_mm, 1)
                        pe.wait_ge(h_mid if q < 2 else h_out, base + (q + 3 if q < 2 else q - 1))
                        for t in range(FT):
                            pe.wait_ge(hid_act, l * (CH * FT) + q * FT + t + 3)
                            mm = nc.tensor.matmul(bank[ZO[q % 2]][:, :], w2c[:, t, :], hid[:, q % 2, t, :], start=(t == 0), stop=(t == FT - 1))
                        mm.then_inc(o_mm, 1)

                    def fill(n):
                        u, j = divmod(n, 4)
                        if j == 0:
                            for h in range(CT):
                                pe.wait_ge(ctx_in[u][h], l * 16 + 16)
                        pe.wait_ge(ctx_set, l * 8 + n + 1)
                        for k in (2 * j, 2 * j + 1):
                            for h in range(CT):
                                mm = nc.tensor.transpose(bank[HD[j % 2]][:, (k % 2) * S + h * P:(k % 2) * S + (h + 1) * P],
                                                         cin[u][h][:, k * P:(k + 1) * P], ident[:, :])
                        mm.then_inc(ctx_tp, 1)

                    pe.wait_ge(w1_in, l * 16 + 16)
                    pe.wait_ge(ve1, base + CH)
                    for t in range(FT):
                        mm = nc.tensor.transpose(bank[PREP][:, t * P:(t + 1) * P], w1raw[:, t, :], ident[:, :])
                    mm.then_inc(w1_tp, 1)
                    fill(0)
                    fill(1)
                    pe.wait_ge(w1_u, l + 1)
                    pe.wait_ge(w1_s, l + 1)
                    pe.wait_ge(w2_in, l * 16 + 16)
                    for t in range(FT):
                        mm = nc.tensor.matmul(bank[PREP][:, t * P:(t + 1) * P], w2raw[:, t * P:(t + 1) * P], center[:, :], start=True, stop=True)
                    mm.then_inc(w2_tp, 1)
                    pe.wait_ge(cur_set, l + 1)
                    for t in range(FT):
                        mm = nc.tensor.matmul(bank[SMALL][:, 32 + t:33 + t], w1u[:, t * P:(t + 1) * P], cur[:, LN2B:LN2B + 1], start=True, stop=True)
                    mm.then_inc(b1_mm, 1)
                    pe.wait_ge(cs_set, l + 1)
                    for n in range(2, 6):
                        fill(n)
                    z(0)
                    fill(6)
                    fill(7)
                    z(1)
                    z(2)
                    pe.wait_ge(b1_set, l + 1)
                    pe.wait_ge(w2_set, l + 1)
                    var_second(0)
                    z(3)
                    var_second(1)
                    spread_second(0)
                    var_second(2)
                    spread_second(1)
                    feed_forward(0)
                    var_second(3)
                    spread_second(2)
                    feed_forward(1)
                    spread_second(3)
                    var_first(0, base + CH + 1)
                    feed_forward(2)
                    var_first(1, base + CH + 2)
                    spread_first(0, base + CH + 1)
                    feed_forward(3)
                    var_first(2, base + CH + 3)
                    spread_first(1, base + CH + 2)
                    var_first(3, base + CH + 4)
                    spread_first(2, base + CH + 3)
                    spread_first(3, base + CH + 4)
                pe.wait_ge(off_set, 1)
                nc.tensor.matmul(bank[0][:, 0:1], ones[:, :], off_any[:, 0:1], start=True, stop=True).then_inc(off_mm, 1)

            @block.scalar
            def _(act):
                a = nc.scalar

                def square(q, done):
                    a.activation(chunk(sq, q), chunk(H, q), ACT.Square).then_inc(done, 1)

                act.sem_inc(hid_act, 2)
                act.sem_inc(ctx_set, 2)
                for q in range(CH):
                    square(q, sq1)
                def masks(g):
                    hold(act, round_rep, (g + 1) * (QUICK * GT) + GT)
                    for u in range(2):
                        a.activation(M[:, :, ds((g * 2 + u) * S, S)], w[:, u * KD:(u + 1) * KD, WINDOW:WK][:, :, ::-1], ACT.Relu,
                                     scale=1e-30, bias=ones[:, 0:1]).then_inc(mask_done, 1)

                def layer(l):
                    act.wait_ge(cur_set, l + 1)
                    for q in range(CH):
                        if q == 2:
                            act.wait_ge(w1_tp, l + 2)
                            a.copy(w1u, bank[PREP][:, :]).then_inc(w1_u, 1)
                        act.wait_ge(yn1, l * CH + q + 1)
                        a.activation(chunk(yn, q), chunk(yn, q), ACT.Silu, scale=cur[:, LN1W:LN1W + 1], bias=cur[:, LN1B:LN1B + 1]).then_inc(act1, 1)
                    act.wait_ge(w2_tp, l + 2)
                    a.copy(w2c.rearrange("p t m -> p (t m)"), bank[PREP][:, :]).then_inc(w2_set, 1)
                    for n in range(8):
                        act.wait_ge(ctx_tp, l * 8 + n + 9)
                        hold(act, w_set, l * 2 + 2)
                        a.copy(cT[:, ds((l % 2) * 2 + n // 4, 1), 2 * (n % 4):2 * (n % 4) + 2, :].rearrange("p a k s -> p (a k) s"),
                               bank[HD[n % 2]][:, :].rearrange("p (k s) -> p k s", k=2)[:, :, ::-1]).then_inc(ctx_set, 1)
                    for q in range(CH):
                        act.wait_ge(h_mid, l * CH + q + 1)
                        square(q, sq2)
                    act.wait_ge(b1_set, l + 1)
                    def count_signs(thr, sums, done, i):
                        u, k = divmod(i, KD)
                        a.activation(M[:, k, ds((l * 2 + u) * S, S)], cT[:, ds((l % 2) * 2 + u, 1), k, :].rearrange("p a s -> p (a s)"), ACT.Sign,
                                     scale=-1.0, bias=thr[:, i:i + 1], accum_out=sums[:, i:i + 1]).then_inc(done, 1)

                    def search(q):
                        if q == 0 and not isinstance(l, int):
                            masks(l - 2)
                        if q == 0:
                            hold(act, t0_set, l + 2)
                        for n in range(*((0, 10), (10, 21), (21, 32), (0, 0))[q]):
                            if n == GT:
                                hold(act, s0_sum, l * (2 * GT) + GT)
                            count_signs(*((t_lo, s_lo) if n < GT else (t_hi, s_hi)), s0_sum, n % GT)
                        if q == 3:
                            hold(act, t1_set, l + 1)
                            for i in range(GT):
                                count_signs(t_1, s_1, s1_sum, i)

                    for q in range(CH):
                        for t in range(FT):
                            if q >= 2:
                                act.wait_ge(o_mm, l * CH + q - 1)
                            act.wait_ge(hid_mm, l * (CH * FT) + q * FT + t + 1)
                            a.activation(hid[:, q % 2, t, :], bank[HD[t % 2]][:, :], ACT.Silu, bias=b1f[:, t:t + 1]).then_inc(hid_act, 1)
                        if q > 0:
                            act.wait_ge(h_out, l * CH + q)
                            square(q - 1, sq1)
                        if q < CH - 1:
                            search(q)
                    act.wait_ge(h_out, l * CH + CH)
                    square(CH - 1, sq1)
                    search(CH - 1)

                layer(0)
                layer(1)
                with act.Fori(2, NL) as l:
                    layer(l)
                for g in range(NG - 2, NG):
                    masks(g)

            @block.vector
            def _(dve):
                v = nc.vector

                def tile(g, i):
                    return cT[:, ds((g % 2) * 2 + i // KD, 1), i % KD, :].rearrange("p a s -> p (a s)")

                def stats(g, first):
                    for i in range(first, first + 4):
                        if i % 2 == 0:
                            hold(dve, ctx_set, g * 8 + i // 2 + 3)
                        v.bn_stats(st_c[:, i, :], tile(g, i)).then_inc(c_stat, 1)

                def means(g):
                    hold(dve, t0_set, g + 1)
                    for i in range(GT):
                        hold(dve, c_stat, g * GT + i + 1)
                        v.bn_aggr(mv_c[:, i, :], st_c[:, i, :]).then_inc(c_mean, 1)

                def counts(g, u):
                    if u == 0:
                        hold(dve, t2_set, g + 1)
                        hold(dve, w_set, g * 2 + 4)
                    for i in range(u * KD, (u + 1) * KD):
                        v.tensor_scalar(under[:, i, :], tile(g, i), t_2[:, i:i + 1], 0.0, ALU.is_lt, ALU.add,
                                        accum_out=m_cnt[:, i:i + 1]).then_inc(counted, 1)

                def without_under(g):
                    hold(dve, mask_done, g * 2 + 2)
                    for u in range(2):
                        hold(dve, counted, g * GT + (u + 1) * KD + 1)
                        v.scalar_tensor_tensor(w[:, u * KD:(u + 1) * KD, WINDOW:WK], under[:, u * KD:(u + 1) * KD, :], -FLT_MAX,
                                               cT[:, ds((g % 2) * 2 + u, 1), :, :].rearrange("p a k s -> p (a k) s"), ALU.mult, ALU.subtract).then_inc(w_set, 1)

                def fill_pads(g):
                    fill = m_cnt[:, :].unsqueeze(2).to_broadcast([P, GT, WINDOW])
                    v.scalar_tensor_tensor(pad01, iota_lane[:, 0:WINDOW].unsqueeze(1).to_broadcast([P, GT, WINDOW]), float(KS - WINDOW), fill,
                                           ALU.add, ALU.is_lt).then_inc(sel_small, 1)
                    v.tensor_scalar(off[:, :], m_cnt[:, :], -float(KS - WINDOW // 2), None, ALU.add).then_inc(sel_small, 1)
                    hold(dve, sel_small, g * 6 + 1)
                    v.tensor_scalar(pad_neg, pad01, -1.0, FLT_MAX, ALU.add, ALU.mult).then_inc(sel_small, 1)
                    hold(dve, sel_small, g * 6 + 2)
                    v.tensor_tensor(off[:, :], off[:, :], off[:, :], ALU.mult).then_inc(sel_small, 1)
                    hold(dve, sel_small, g * 6 + 3)
                    v.scalar_tensor_tensor(pad01, pad01, FLT_MAX, pad_neg, ALU.mult, ALU.add).then_inc(sel_small, 1)
                    hold(dve, sel_small, g * 6 + 4)
                    v.tensor_reduce(off_max[:, ds(g, 1)], off[:, :], AX.X, ALU.max).then_inc(sel_small, 1)
                    hold(dve, sel_small, g * 6 + 5)
                    hold(dve, w_set, g * 2 + 6)

                def take(n_before, pads, part, tiles=range(GT)):
                    for i in tiles:
                        if i % 4 == 0:
                            hold(dve, (round_rep, round_max)[part], n_before + i + 4)
                        if part == 0:
                            v.max(top8[:, i, :], w[:, i, pads:]).then_inc(round_max, 1)
                        else:
                            v.match_replace(w[:, i, pads:], top8[:, i, :], w[:, i, pads:], -FLT_MAX).then_inc(round_rep, 1)

                def plus_eps(q, n, var_done, done):
                    dve.wait_ge(var_done, n)
                    v.tensor_scalar(ve[:, q, :], bank[VAR[q % 2]][:, 0:TPC], EPS, None, ALU.add).then_inc(done, 1)

                def scale(q, n, bc_done, done):
                    dve.wait_ge(bc_done, n)
                    v.tensor_tensor(chunk(yn, q), chunk(H, q), bank[BC[q % 2]][:, :], ALU.mult).then_inc(done, 1)

                dve.sem_inc(counted, 1)
                dve.sem_inc(mask_done, 2)
                dve.sem_inc(round_rep, GT)
                dve.sem_inc(w_set, 4)
                dve.sem_inc(t0_set, 1)
                for q in range(CH):
                    plus_eps(q, q + 1, var1, ve1)
                for q in range(CH):
                    scale(q, q + 1, bc1, yn1)
                def layer(l):
                    back = not isinstance(l, int) or l > 0
                    rounds = not isinstance(l, int)
                    base = l * CH
                    cos_l = cos_t[:, ds(l, 1), :].to_broadcast([P, BPC, S])
                    hold(dve, yn1, base + CH)
                    v.tensor_copy(cur[:, :], layer_par[:, ds(l, 1), :].rearrange("p a k -> p (a k)")).then_inc(cur_set, 1)
                    dve.wait_ge(cur_set, l + 1)
                    v.tensor_scalar(cs, center[:, :], cur[:, SCL:SCL + 1], None, ALU.mult).then_inc(cs_set, 1)
                    if rounds:
                        take(((l - 2) * QUICK + 1) * GT, 0, 0, range(8, 16))
                    rho = cur[:, RHO:RHO + 1].to_broadcast([P, S])

                    def turn_in(q):
                        hold(dve, act1, base + q + 1)
                        v.tensor_tensor(by_seq(a_buf, q), by_seq(yn, q), cos_l, ALU.mult).then_inc(a_in, 1)

                    def scan(q):
                        dve.wait_ge(a_in, base + q + 1)
                        dve.wait_ge(b_in, base + q + 1)
                        for b in range(BPC):
                            for buf, first in ((a_buf, UR0), (b_buf, UI0)):
                                part = buf[:, q * CW + b * S:q * CW + (b + 1) * S]
                                sc = v.tensor_tensor_scan(part, rho, part, cur[:, first:first + 1], ALU.mult, ALU.add)
                        sc.then_inc(scanned, 1)

                    def turn_out(q):
                        hold(dve, scanned, base + q + 1)
                        v.tensor_tensor(by_seq(a_buf, q), by_seq(a_buf, q), cos_l, ALU.mult).then_inc(a_out, 1)

                    def middle(q):
                        dve.wait_ge(z_mm, base + q + 1)
                        v.tensor_tensor(chunk(H, q), chunk(H, q), bank[ZO[q % 2]][:, :], ALU.add).then_inc(h_mid, 1)

                    def last(q):
                        dve.wait_ge(o_mm, base + q + 1)
                        v.scalar_tensor_tensor(chunk(H, q), bank[ZO[q % 2]][:, :], cur[:, B2:B2 + 1], chunk(H, q), ALU.add, ALU.add).then_inc(h_out, 1)

                    turn_in(0)
                    turn_in(1)
                    scan(0)
                    dve.wait_ge(w1_u, l + 1)
                    v.tensor_scalar(w1s, bank[PREP][:, :], cur[:, LN2W:LN2W + 1], None, ALU.mult).then_inc(w1_s, 1)
                    turn_in(2)
                    turn_out(0)
                    scan(1)
                    turn_in(3)
                    turn_out(1)
                    scan(2)
                    dve.wait_ge(b1_mm, l + 1)
                    v.tensor_tensor(b1f, bank[SMALL][:, 32:32 + FT], cur[:, B1:B1 + FT], ALU.add).then_inc(b1_set, 1)
                    scan(3)
                    turn_out(2)
                    turn_out(3)
                    middle(0)
                    stats(l, 0)
                    middle(1)
                    stats(l, 4)
                    middle(2)
                    stats(l, 8)
                    plus_eps(0, base + 1, var2, ve2)
                    middle(3)
                    stats(l, 12)
                    plus_eps(1, base + 2, var2, ve2)
                    means(l)
                    scale(0, base + 1, bc2, yn2)
                    plus_eps(2, base + 3, var2, ve2)
                    if rounds:
                        take(((l - 2) * QUICK + 1) * GT, 0, 1, range(0, 8))
                    scale(1, base + 2, bc2, yn2)
                    if rounds:
                        take(((l - 2) * QUICK + 1) * GT, 0, 1, range(8, 16))
                    if back:
                        counts(l - 1, 0)
                    last(0)
                    plus_eps(3, base + 4, var2, ve2)
                    scale(2, base + 3, bc2, yn2)
                    if back:
                        counts(l - 1, 1)
                        without_under(l - 1)
                    last(1)
                    scale(3, base + 4, bc2, yn2)
                    plus_eps(0, base + CH + 1, var1, ve1)
                    if back:
                        fill_pads(l - 1)
                        take((l - 1) * QUICK * GT, 0, 0, range(0, 12))
                    last(2)
                    plus_eps(1, base + CH + 2, var1, ve1)
                    scale(0, base + CH + 1, bc1, yn1)
                    if back:
                        take((l - 1) * QUICK * GT, 0, 0, range(12, 16))
                        take((l - 1) * QUICK * GT, 0, 1)
                    last(3)
                    plus_eps(2, base + CH + 3, var1, ve1)
                    scale(1, base + CH + 2, bc1, yn1)
                    if back:
                        take(((l - 1) * QUICK + 1) * GT, 0, 0, range(0, 4))
                    plus_eps(3, base + CH + 4, var1, ve1)
                    scale(2, base + CH + 3, bc1, yn1)
                    if back:
                        take(((l - 1) * QUICK + 1) * GT, 0, 0, range(4, 8))
                    scale(3, base + CH + 4, bc1, yn1)

                layer(0)
                layer(1)
                with dve.Fori(2, NL) as l:
                    layer(l)
                g = NG - 1
                take(((g - 1) * QUICK + 1) * GT, 0, 0, range(8, 16))
                take(((g - 1) * QUICK + 1) * GT, 0, 1)
                for u in range(2):
                    counts(g, u)
                without_under(g)
                fill_pads(g)
                for r in range(QUICK):
                    for part in range(2):
                        take((g * QUICK + r) * GT, 0, part)
                hold(dve, sel_small, NG * 6)
                v.tensor_reduce(off_one, off_max, AX.X, ALU.max).then_inc(sel_small, 1)
                hold(dve, sel_small, NG * 6 + 1)
                v.tensor_scalar(off_any, off_one, float((WINDOW // 2) ** 2), None, ALU.is_gt).then_inc(off_set, 1)
                hold(dve, off_mm, 1)
                v.tensor_copy(off_i[:, :], bank[0][:, 0:1]).then_inc(sel_small, 1)


        cin_all = Xf[:, 0:CT * D].rearrange("p (h l) -> p h l", h=CT)
        WA = S + PADS
        w_all = Xf[:, CT * D:CT * D + KD * WA].rearrange("p (i s) -> p i s", i=KD)
        top_all = Xf[:, 8192:8192 + KD * 8].rearrange("p (i s) -> p i s", i=KD)
        all_in, all_tp, all_w, all_max, all_rep, all_mask = (sem(n) for n in ("all_in", "all_tp", "all_w", "all_max", "all_rep", "all_mask"))

        with nc.Block() as block:
            @block.sync
            def _(sp):
                missed = sp.value_load(off_i[0:1, 0:1], min_val=0, max_val=P)
                with sp.If(missed > 0):
                    sp.sem_inc(all_tp, 1)
                    with sp.Fori(0, B) as b:
                        sp.wait_ge(all_tp, b + 1)
                        sp.dma_start(cin_all, ctx_map[ds(b, 1), :, :].rearrange("a (h p) l -> p (a h) l", p=P)).then_inc(all_in, 16)

            @block.tensor
            def _(pe):
                missed = pe.value_load(off_i[0:1, 0:1], min_val=0, max_val=P)
                with pe.If(missed > 0):
                    with pe.Fori(0, B) as b:
                        pe.wait_ge(all_in, b * 16 + 16)
                        pe.wait_ge(all_w, b * 5 + 1)
                        for k in range(KD):
                            for h in range(CT):
                                mm = nc.tensor.transpose(bank[k // 2][:, (k % 2) * S + h * P:(k % 2) * S + (h + 1) * P],
                                                         cin_all[:, h, k * P:(k + 1) * P], ident[:, :])
                        mm.then_inc(all_tp, 1)

            @block.vector
            def _(dve):
                v = nc.vector
                missed = dve.value_load(off_i[0:1, 0:1], min_val=0, max_val=P)
                with dve.If(missed > 0):
                    dve.sem_inc(all_w, 1)
                    dve.sem_inc(all_mask, 1)
                    dve.sem_inc(all_rep, KD)
                    with dve.Fori(0, B) as b:
                        hold(dve, all_mask, b + 1)
                        v.memset(w_all[:, :, 0:PADS], FLT_MAX).then_inc(all_w, 1)
                        hold(dve, all_tp, b + 2)
                        for j in range(4):
                            v.tensor_scalar(w_all[:, 2 * j:2 * j + 2, PADS:WA], bank[j][:, :].rearrange("p (k s) -> p k s", k=2)[:, :, ::-1],
                                            -1.0, None, ALU.mult).then_inc(all_w, 1)
                        hold(dve, all_w, b * 5 + 6)
                        with dve.Fori(0, ROUNDS) as r:
                            n = (b * ROUNDS + r) * KD
                            for i in range(KD):
                                hold(dve, all_rep, n + i + 1)
                                v.max(top_all[:, i, :], w_all[:, i, :]).then_inc(all_max, 1)
                            for i in range(KD):
                                hold(dve, all_max, n + i + 1)
                                v.match_replace(w_all[:, i, :], top_all[:, i, :], w_all[:, i, :], -FLT_MAX).then_inc(all_rep, 1)
                        hold(dve, all_rep, b * (ROUNDS * KD) + (ROUNDS + 1) * KD)
                        v.tensor_scalar(M[:, :, ds(b * S, S)], w_all[:, :, PADS:WA][:, :, ::-1], -FLT_MAX, None, ALU.is_gt).then_inc(all_mask, 1)

        UN = 4
        UNITS = ((), (0,), (1,), (2, 3))
        KU = KD // 2
        ring = [nat[:, 2 + u, :] for u in range(2)]
        crux = [H[:, u * KU * S:(u + 1) * KU * S].rearrange("p (k s) -> p k s", k=KU) for u in range(2)]
        rest = fin[:, :, :].rearrange("p a n -> p (a n)").rearrange("p (k s) -> p k s", k=KU)
        pooled = ewide[:, 0:4 * KD * B].rearrange("p (m i k b) -> p m i k b", m=2, i=2, k=KD)
        spill = sb("spill", [P, KU // 2, S], BF16)
        junk = [bank[1][:, k * S:(k + 1) * S] for k in range(KU // 2)] + [spill[:, k, :] for k in range(KU // 2)]
        r_in = [sem(f"r_in{u}") for u in range(TPC)]
        r_bias, o2_mm, x1_done, x1_tp, x1_tpev, tot_mm = (sem(n) for n in ("r_bias", "o2_mm", "x1_done", "x1_tp", "x1_tpev", "tot_mm"))
        cr_mul, cr_max, cr_sum, re_sub, re_max, av_set = (sem(n) for n in ("cr_mul", "cr_max", "cr_sum", "re_sub", "re_max", "av_set"))

        def row_of(q, u):
            return X[:, ds(q * TPC + u, 1), :].rearrange("p a d -> p (a d)")

        def unit(buf, q, j):
            return buf[:, (j % 2) * KU:(j % 2 + 1) * KU, ds(q * CW + (j // 2) * S, S)]

        def pool_at(m, i, q, j):
            return pooled[:, m, i, (j % 2) * KU:(j % 2 + 1) * KU, ds(q * BPC + j // 2, 1)].rearrange("p k b -> p (k b)")

        with nc.Block() as block:
            @block.sync
            def _(sp):
                sp.sem_inc(x1_done, 8)
                with sp.Fori(0, CH) as q:
                    for u in range(TPC):
                        sp.wait_ge(x1_done, q * 8 + 2 * u + 2)
                        sp.dma_start(row_of(q, u), x2d[ds(q * CW + u * P, P), :]).then_inc(r_in[u], 16)

            @block.gpsimd
            def _(pool):
                def others(q, j):
                    pool.wait_ge(cr_mul, q * UN + j + 1)
                    hold(pool, re_max, q * UN + j + 1)
                    nc.gpsimd.tensor_tensor(rest, unit(T, q, j), crux[j % 2], ALU.subtract).then_inc(re_sub, 1)

                def bias(q, u):
                    hold(pool, r_in[u], q * 16 + 16)
                    nc.gpsimd.tensor_tensor(row_of(q, u), row_of(q, u), bout_b, ALU.add).then_inc(r_bias, 1)

                def tiles(q):
                    for u in range(TPC):
                        if not isinstance(q, int) or q > 0:
                            for j in UNITS[u]:
                                others(q - 1, j)
                        ln_pow(pool, u, q * TPC + u + NT + 1)
                        if not isinstance(q, int) or q < CH - 1 or u < 2:
                            bias(q + (u + 2) // TPC, (u + 2) % TPC)

                bias(0, 0)
                bias(0, 1)
                tiles(0)
                with pool.Fori(1, CH - 1) as q:
                    tiles(q)
                tiles(CH - 1)
                for j in range(UN):
                    others(CH - 1, j)

            @block.scalar
            def _(act):
                a = nc.scalar

                def sums(q, j):
                    hold(act, cr_mul, q * UN + j + 1)
                    hold(act, cr_sum, q * UN + j + 2)
                    for k in range(KU):
                        ins = a.activation(junk[k], crux[j % 2][:, k, :], ACT.Copy,
                                           accum_out=pooled[:, 1, 0, (j % 2) * KU + k, ds(q * BPC + j // 2, 1)])
                    ins.then_inc(cr_sum, 1)

                def tiles(q, pools):
                    for u in range(TPC):
                        for h in range(2):
                            act.wait_ge(x1_tp, q * 8 + 2 * u + h + 1)
                            a.copy(T[:, 4 * h:4 * h + 4, ds(q * CW + u * P, P)],
                                   bank[6 + h][:, :].rearrange("p (k n) -> p k n", k=4)).then_inc(x1_tpev, 1)
                        if pools:
                            for j in UNITS[u]:
                                sums(q - 1, j)

                act.sem_inc(x1_tpev, 2)
                act.sem_inc(cr_sum, 2)
                tiles(0, False)
                with act.Fori(1, CH) as q:
                    tiles(q, True)
                for j in range(UN):
                    sums(CH - 1, j)

            @block.tensor
            def _(pe):
                def products(q, u):
                    for n in range(2):
                        pe.wait_ge(x1_done, q * 8 + 2 * u + n + 5)
                        nc.tensor.matmul(bank[2 + 2 * (u % 2) + n][:, :], yn[:, q * CW + u * P:q * CW + (u + 1) * P],
                                         wout_t[:, n * BANK:(n + 1) * BANK], start=True, stop=True).then_inc(o2_mm, 1)

                def turned(q, u):
                    pe.wait_ge(ln_out, q * TPC + u + NT + 1)
                    for h in range(2):
                        pe.wait_ge(x1_tpev, q * 8 + 2 * u + h + 1)
                        for j in range(4):
                            k = 4 * h + j
                            mm = nc.tensor.transpose(bank[6 + h][:, j * P:(j + 1) * P], ring[u % 2][:, k * P:(k + 1) * P], ident[:, :])
                        mm.then_inc(x1_tp, 1)
                    for k in range(KD):
                        at = (q * TPC + u) * KD + k
                        mm = nc.tensor.matmul(bank[0][:, at:at + 1], ring[u % 2][:, k * P:(k + 1) * P], ones[:, 0:1], start=True, stop=True)
                    mm.then_inc(tot_mm, 1)

                for t in range(NT + 2):
                    if t < NT:
                        products(*divmod(t, TPC))
                    if t >= 2:
                        turned(*divmod(t - 2, TPC))

            @block.vector
            def _(dve):
                v = nc.vector

                def largest(src, i, q, j, done):
                    v.tensor_reduce(pool_at(0, i, q, j), src, AX.X, ALU.max).then_inc(done, 1)

                def crucial(q, j):
                    hold(dve, x1_tpev, q * 8 + 10)
                    hold(dve, cr_sum, q * UN + j + 1)
                    v.tensor_tensor(crux[j % 2], unit(T, q, j), unit(M, q, j), ALU.mult).then_inc(cr_mul, 1)

                def maxima(q, j):
                    dve.wait_ge(cr_mul, q * UN + j + 1)
                    largest(crux[j % 2], 0, q, j, cr_max)
                    dve.wait_ge(re_sub, q * UN + j + 1)
                    largest(rest, 1, q, j, re_max)

                def normed(q, u):
                    hold(dve, tot_mm, q * TPC + u + 1)
                    ln_apply(dve, ring[u % 2], row_of(q, u), u, q * TPC + u + NT + 1)

                def tiles(q, pools):
                    for u in range(TPC):
                        if u > 0 or pools:
                            normed(q - (u == 0), (u - 1) % TPC)
                        row = row_of(q, u)
                        dve.wait_ge(r_bias, q * TPC + u + 1)
                        for n in range(2):
                            hold(dve, o2_mm, q * 8 + 2 * u + n + 1)
                            v.tensor_tensor(row[:, n * BANK:(n + 1) * BANK], bank[2 + 2 * (u % 2) + n][:, :],
                                            row[:, n * BANK:(n + 1) * BANK], ALU.add).then_inc(x1_done, 1)
                        units = UNITS[u] if pools else ()
                        for j in units[:1]:
                            crucial(q - 1, j)
                        hold(dve, x1_done, q * 8 + 2 * u + 10)
                        ln_stats(dve, row, u, q * TPC + u + NT + 1)
                        for j in units:
                            if j != units[0]:
                                crucial(q - 1, j)
                            maxima(q - 1, j)

                dve.sem_inc(tot_mm, 2)
                dve.sem_inc(re_max, 1)
                tiles(0, False)
                with dve.Fori(1, CH) as q:
                    tiles(q, True)
                normed(CH - 1, TPC - 1)
                for j in range(UN):
                    crucial(CH - 1, j)
                    maxima(CH - 1, j)
                avg = [pooled[:, 1, i, :, :] for i in range(2)]
                dve.wait_ge(tot_mm, NT + 2)
                dve.wait_ge(cr_sum, NT + 2)
                v.tensor_reduce(avg[1].rearrange("p k b -> p b k"), bank[0][:, 0:NT * KD].rearrange("p (b h k) -> p b k h", h=CT, k=KD),
                                AX.X, ALU.add).then_inc(av_set, 1)
                dve.wait_ge(av_set, 1)
                v.tensor_tensor(avg[1], avg[1], avg[0], ALU.subtract).then_inc(av_set, 1)
                dve.wait_ge(av_set, 2)
                for i, n in enumerate((KC, KS)):
                    v.tensor_scalar(avg[i], avg[i], 1.0 / n, None, ALU.mult).then_inc(av_set, 1)

        lo = 0

        def in_late(*shape):
            nonlocal lo
            n = 1
            for s in shape:
                n *= s
            lo += n
            flat = late[:, lo - n:lo]
            names = "abcd"[:len(shape)]
            return flat.rearrange(f"p ({' '.join(names)}) -> p {' '.join(names)}", **dict(zip(names, shape)))

        z = in_late(2, KD * B)
        zz = in_late(2, KD * B)
        gsum = in_late(2)
        gmean = in_late(2)
        gvar = in_late(2)
        grs = in_late(2)
        g_dve, g_pe, g_pool, g_act = (sem(n) for n in ("g_dve", "g_pe", "g_pool", "g_act"))
        CNT = D * B

        with nc.Block() as block:
            @block.tensor
            def _(pe):
                pin = pooled[:, :, :, :, :].rearrange("p m i k b -> p m i (k b)")
                zb = bank[0][:, 0:2 * KD * B].rearrange("p (i n) -> p i n", i=2)
                edge = B
                for c in range(2):
                    nc.tensor.matmul(zb[:, :, :], band[:, c, P:2 * P], pin[:, c, :, :], start=(c == 0), stop=False, skip_group_check=True)
                for c in range(2):
                    for i in range(2):
                        nc.tensor.matmul(zb[:, i, edge:], band[:, c, 2 * P:3 * P], pin[:, c, i, 0:KD * B - edge], start=False, stop=False, skip_group_check=True)
                        mm = nc.tensor.matmul(zb[:, i, 0:KD * B - edge], band[:, c, 0:P], pin[:, c, i, edge:], start=False, stop=(c == 1 and i == 1),
                                              skip_group_check=True)
                mm.then_inc(g_pe, 1)
                pe.wait_ge(g_dve, 2)
                nc.tensor.matmul(bank[1][:, 0:2], ones[:, :], gsum[:, :], start=True, stop=True).then_inc(g_pe, 1)
                pe.wait_ge(g_dve, 6)
                nc.tensor.matmul(bank[2][:, 0:2], ones[:, :], gsum[:, :], start=True, stop=True).then_inc(g_pe, 1)

            @block.gpsimd
            def _(pool):
                pool.wait_ge(g_dve, 7)
                nc.gpsimd.tensor_tensor(grs[:, :], gvar[:, :], neg_half[:, 0:2], ALU.pow).then_inc(g_pool, 1)

            @block.scalar
            def _(act):
                act.wait_ge(g_dve, 10)
                nc.scalar.activation(z[:, :, :], z[:, :, :], ACT.Sigmoid).then_inc(g_act, 1)

            @block.vector
            def _(dve):
                v = nc.vector
                n_link = [0]

                def link(ins):
                    n_link[0] += 1
                    ins.then_inc(g_dve, 1)
                    dve.wait_ge(g_dve, n_link[0])

                dve.wait_ge(g_pe, 1)
                link(v.tensor_copy(z[:, :, :], bank[0][:, 0:2 * KD * B].rearrange("p (i n) -> p i n", i=2)))
                link(v.tensor_reduce(gsum[:, :], z[:, :, :], AX.X, ALU.add))
                dve.wait_ge(g_pe, 2)
                link(v.tensor_scalar(gmean[:, :], bank[1][:, 0:2], 1.0 / CNT, None, ALU.mult))
                link(v.tensor_tensor(z[:, :, :], z[:, :, :], gmean[:, :].unsqueeze(2).to_broadcast([P, 2, KD * B]), ALU.subtract))
                link(v.tensor_tensor(zz[:, :, :], z[:, :, :], z[:, :, :], ALU.mult))
                link(v.tensor_reduce(gsum[:, :], zz[:, :, :], AX.X, ALU.add))
                dve.wait_ge(g_pe, 3)
                link(v.tensor_scalar(gvar[:, :], bank[2][:, 0:2], 1.0 / CNT, EPS, ALU.mult, ALU.add))
                dve.wait_ge(g_pool, 1)
                link(v.tensor_tensor(z[:, :, :], z[:, :, :], grs[:, :].unsqueeze(2).to_broadcast([P, 2, KD * B]), ALU.mult))
                link(v.tensor_scalar(z[:, :, :], z[:, :, :], bn_gb[:, 0:1], bn_gb[:, 1:2], ALU.mult, ALU.add))
                link(v.tensor_scalar(z[:, :, :], z[:, :, :], 0.0, None, ALU.max))
                dve.wait_ge(g_act, 1)
                link(v.tensor_tensor(z[:, 0, :], z[:, 0, :], z[:, 1, :], ALU.subtract))

        logits = sb("logits", [P, NT, E])
        gsel = [natf[:, u * N:(u + 1) * N].rearrange("p (k s) -> p k s", k=KD) for u in range(2)]
        nring = [H[:, u * D:(u + 1) * D] for u in range(2)]
        xt = [fin[:, :, :].rearrange("p a n -> p (a n)").rearrange("p (k n) -> p k n", k=KD),
              late[:, D:2 * D].rearrange("p (k n) -> p k n", k=KD)]
        assert lo <= D
        wslot = Tf.rearrange("p (w k n) -> p w k n", w=2, k=KD)
        out_init = sem("out_init")
        w_in_sem = [sem(f"w_in{w}") for w in range(2)]
        nrm_st = [sem(f"nrm_st{u}") for u in range(2)]
        gmul, gm_done, back_mm, x2_done = (sem(n) for n in ("gmul", "gm_done", "back_mm", "x2_done"))
        l_tp, l_tpev, l_mm, l_ev = (sem(n) for n in ("l_tp", "l_tpev", "l_mm", "l_ev"))

        def expert_src(e):
            return expert_w[e, :, :].rearrange("(k p) n -> p k n", p=P)

        def peeled(body):
            def run(eng):
                for b in range(2):
                    body(b, b)
                with eng.Fori(1, B // 2 - 1) as i:
                    for s_ in range(2):
                        body(i * 2 + s_, s_)
                for b in range(B - 2, B):
                    body(b, b % 2)
            return run

        with nc.Block() as block:
            @block.sync
            def _(sp):
                with sp.Fori(0, B) as b:
                    for h in range(CT):
                        t = b * CT + h
                        sp.wait_ge(x2_done, t * 2 + 6)
                        sp.dma_start(out[ds(t * P, P), :], X[:, ds(t, 1), :].rearrange("p a d -> p (a d)")).then_inc(out_init, 16)
                        sp.wait_ge(ln_out, t + 2 * NT + 1)
                        sp.dma_start(x_nrm[ds(t * P, P), :], nring[h]).then_inc(nrm_st[h], 16)
                sp.dma_start(out[N:N + P, :], X[:, 0, :]).then_inc(out_init, 16)
                sp.wait_ge(gm_done, B)
                for w in range(2):
                    sp.dma_start(wslot[:, w, :, :], expert_src(w)).then_inc(w_in_sem[w], 16)

            @block.gpsimd
            def _(pool):
                with pool.Fori(0, CH) as q:
                    for u in range(TPC):
                        ln_pow(pool, u, q * TPC + u + 2 * NT + 1)

            @block.scalar
            def _(act):
                a = nc.scalar

                def gates_of(b, par):
                    hold(act, back_mm, b * 2 + 2)
                    for k in range(KD):
                        ins = a.activation(gsel[par][:, k, :], M[:, k, ds(b * S, S)], ACT.Identity,
                                           scale=z[:, 0, ds(k * B + b, 1)], bias=z[:, 1, ds(k * B + b, 1)])
                    ins.then_inc(gmul, 1)

                def copies(b, h):
                    t = b * CT + h
                    act.wait_ge(l_mm, t + 1)
                    for n in range(2):
                        act.wait_ge(l_tp, t * 2 + n + 5)
                        a.copy(xt[h][:, 4 * n:4 * n + 4, :], bank[4 + n][:, :].rearrange("p (k n) -> p k n", k=4)).then_inc(l_tpev, 1)

                def step(b, par):
                    if not isinstance(b, int) or b > 0:
                        copies(b - 1, 0)
                    if not isinstance(b, int) or b < B - 2:
                        gates_of(b + 2, par)
                    if not isinstance(b, int) or b > 0:
                        copies(b - 1, 1)

                act.sem_inc(back_mm, 4)
                act.sem_inc(l_tpev, 2)
                gates_of(0, 0)
                gates_of(1, 1)
                peeled(step)(act)
                for h in range(CT):
                    copies(B - 1, h)

            @block.tensor
            def _(pe):
                def back(b, par):
                    pe.wait_ge(gm_done, b + 1)
                    for h in range(CT):
                        pe.wait_ge(x2_done, (b * CT + h) * 2 + 2)
                        for k in range(KD):
                            mm = nc.tensor.transpose(bank[2 * h + k // 4][:, (k % 4) * P:(k % 4 + 1) * P], gsel[par][:, k, h * P:(h + 1) * P], ident[:, :])
                        mm.then_inc(back_mm, 1)

                def forth(b, h):
                    t = b * CT + h
                    pe.wait_ge(ln_out, t + 2 * NT + 1)
                    for n in range(2):
                        pe.wait_ge(l_tpev, t * 2 + n + 1)
                        for j in range(4):
                            k = 4 * n + j
                            mm = nc.tensor.transpose(bank[4 + n][:, j * P:(j + 1) * P], nring[h][:, k * P:(k + 1) * P], ident[:, :])
                        mm.then_inc(l_tp, 1)

                def gate_logits(b, h):
                    t = b * CT + h
                    pe.wait_ge(l_tpev, t * 2 + 4)
                    for k in range(KD):
                        mm = nc.tensor.matmul(bank[6][:, ds(t * E, E)], xt[h][:, k, :], gate[:, k, :], start=(k == 0), stop=(k == KD - 1))
                    mm.then_inc(l_mm, 1)

                def step(b, par):
                    back(b, par)
                    if not isinstance(b, int) or b > 0:
                        forth(b - 1, 0)
                        if not isinstance(b, int) or b > 1:
                            gate_logits(b - 2, 1)
                        forth(b - 1, 1)
                        gate_logits(b - 1, 0)

                pe.sem_inc(l_mm, 2)
                peeled(step)(pe)
                forth(B - 1, 0)
                gate_logits(B - 2, 1)
                forth(B - 1, 1)
                for h in range(CT):
                    gate_logits(B - 1, h)

            @block.vector
            def _(dve):
                v = nc.vector

                def row_at(t):
                    return X[:, ds(t, 1), :].rearrange("p a d -> p (a d)")

                def gated(b, par):
                    hold(dve, gmul, b + 1)
                    v.tensor_tensor(gsel[par], gsel[par], T[:, :, ds(b * S, S)], ALU.mult).then_inc(gm_done, 1)

                def residual(b, par, h):
                    t = b * CT + h
                    hold(dve, back_mm, t + 5)
                    for n in range(2):
                        part = row_at(t)[:, n * BANK:(n + 1) * BANK]
                        v.tensor_tensor(part, part, bank[2 * h + n][:, :], ALU.add).then_inc(x2_done, 1)
                    hold(dve, x2_done, t * 2 + 6)
                    ln_stats(dve, row_at(t), 2 * par + h, t + 2 * NT + 1)

                def normed(b, par, h):
                    t = b * CT + h
                    dve.wait_ge(nrm_st[h], b * 16 + 16)
                    hold(dve, l_tp, t * 2 + 2)
                    ln_apply(dve, nring[h], row_at(t), 2 * par + h, t + 2 * NT + 1)

                def step(b, par):
                    residual(b, par, 0)
                    if not isinstance(b, int) or b > 0:
                        normed(b - 1, 1 - par, 1)
                    if not isinstance(b, int) or b < B - 1:
                        gated(b + 1, 1 - par)
                    residual(b, par, 1)
                    normed(b, par, 0)

                for u in range(2):
                    dve.sem_inc(nrm_st[u], 16)
                dve.sem_inc(l_tp, 4)
                dve.sem_inc(x2_done, 4)
                gated(0, 0)
                peeled(step)(dve)
                normed(B - 1, 1, 1)
                dve.wait_ge(l_mm, NT + 2)
                v.tensor_copy(logits[:, :, :].rearrange("p t e -> p (t e)"), bank[6][:, 0:NT * E]).then_inc(l_ev, 1)

        Mf = M[:, :, :].rearrange("p k n -> p (k n)").bitcast(F32)
        xo = 0

        def small(*shape, dt=F32):
            nonlocal xo
            n = 1
            for s in shape:
                n *= s
            xo += n
            assert xo <= KD * N // 2
            flat = Mf[:, xo - n:xo]
            names = "abc"[:len(shape)]
            return (flat if dt == F32 else flat.bitcast(dt)).rearrange(f"p ({' '.join(names)}) -> p {' '.join(names)}", **dict(zip(names, shape)))

        best = small(2, NT)
        hot = small(2, NT, E)
        eq = small(NT, E)
        first = small(NT)
        masked = small(NT, E)
        either = small(NT, E)
        e2 = small(NT)
        prob = small(2, NT)
        tot = small(E, NT)
        upto = small(E, NT)
        full = small(E, NT)
        need = small(E)
        end = small(E)
        begin = small(E)
        place = small(NT, E)
        pos = small(2, NT)
        pos_i = small(2, NT, dt=I32)
        lane_i = small(2, NT, dt=I32)
        lane = small(2, NT)
        slot = small(2, NT)
        past = small(E, SLOTS)
        who = small(SLOTS)
        who_i = small(SLOTS, dt=I32)
        odd_i = small(SLOTS, dt=I32)
        ready_i = small(SLOTS, dt=I32)
        end_i = small(E, dt=I32)
        hot_lane = small(2, P)
        hot_slot = small(2, 2, SLOTS)
        zero_l = small(P)
        tokp1 = small(SLOTS)
        pair_p = small(SLOTS)
        unused = small(SLOTS)
        tok_f = small(SLOTS)
        src_i = small(SLOTS, dt=U32)
        dst_i = small(SLOTS, dt=U32)
        r_dve, r_act, r_pe, hot_set, hot_mm = (sem(n) for n in ("r_dve", "r_act", "r_pe", "hot_set", "hot_mm"))

        with nc.Block() as block:
            @block.scalar
            def _(act):
                act.wait_ge(r_dve, 13)
                nc.scalar.activation(e2[:, :], e2[:, :], ACT.Exp).then_inc(r_act, 1)

            @block.tensor
            def _(pe):
                pe.wait_ge(r_dve, 12)
                nc.tensor.matmul(bank[0][:, 0:NT * E], utri[:, :], either[:, :, :].rearrange("p t e -> p (t e)"), start=True, stop=True)
                nc.tensor.matmul(bank[1][:, 0:NT * E], ones[:, :], either[:, :, :].rearrange("p t e -> p (t e)"), start=True, stop=True).then_inc(r_pe, 1)
                pe.wait_ge(r_dve, 17)
                nc.tensor.matmul(bank[2][:, 0:2 * SLOTS], zero_l[:, :], band[:, 0, 0:2 * SLOTS], start=True, stop=False, skip_group_check=True)
                with pe.Fori(0, NT) as t:
                    for k in range(2):
                        pe.wait_ge(hot_set, t * 2 + k + 1)
                        nc.tensor.matmul(bank[2][:, 0:2 * SLOTS], hot_lane[:, k, :], hot_slot[:, k, :, :].rearrange("p a s -> p (a s)"),
                                         start=False, stop=False, skip_group_check=True).then_inc(hot_mm, 1)
                nc.tensor.matmul(bank[2][:, 0:2 * SLOTS], zero_l[:, :], band[:, 0, 0:2 * SLOTS], start=False, stop=True, skip_group_check=True).then_inc(r_pe, 1)

            @block.vector
            def _(dve):
                v = nc.vector
                n_link = [0]

                def link(ins):
                    n_link[0] += 1
                    ins.then_inc(r_dve, 1)
                    dve.wait_ge(r_dve, n_link[0])

                def over_e(ap):
                    return ap.unsqueeze(2).to_broadcast([P, NT, E])

                link(v.tensor_reduce(best[:, 0, :], logits[:, :, :], AX.X, ALU.max))
                link(v.tensor_tensor(eq[:, :, :], logits[:, :, :], over_e(best[:, 0, :]), ALU.is_equal))
                link(v.tensor_tensor(eq[:, :, :], eq[:, :, :], rev_e[:, :, :], ALU.mult))
                link(v.tensor_reduce(first[:, :], eq[:, :, :], AX.X, ALU.max))
                link(v.tensor_tensor(hot[:, 0, :, :], eq[:, :, :], over_e(first[:, :]), ALU.is_equal))
                link(v.scalar_tensor_tensor(masked[:, :, :], hot[:, 0, :, :], -FLT_MAX, logits[:, :, :], ALU.mult, ALU.add))
                link(v.tensor_reduce(best[:, 1, :], masked[:, :, :], AX.X, ALU.max))
                link(v.tensor_tensor(eq[:, :, :], masked[:, :, :], over_e(best[:, 1, :]), ALU.is_equal))
                link(v.tensor_tensor(eq[:, :, :], eq[:, :, :], rev_e[:, :, :], ALU.mult))
                link(v.tensor_reduce(first[:, :], eq[:, :, :], AX.X, ALU.max))
                link(v.tensor_tensor(hot[:, 1, :, :], eq[:, :, :], over_e(first[:, :]), ALU.is_equal))
                link(v.tensor_tensor(either[:, :, :], hot[:, 0, :, :], hot[:, 1, :, :], ALU.add))
                assert n_link[0] == 12
                link(v.tensor_tensor(e2[:, :], best[:, 1, :], best[:, 0, :], ALU.subtract))
                dve.wait_ge(r_act, 1)
                link(v.tensor_scalar(prob[:, 0, :], e2[:, :], 1.0, None, ALU.add))
                link(v.reciprocal(prob[:, 0, :], prob[:, 0, :]))
                link(v.tensor_tensor(prob[:, 1, :], e2[:, :], prob[:, 0, :], ALU.mult))
                link(v.memset(zero_l[:, :], 0.0))
                assert n_link[0] == 17
                dve.wait_ge(r_pe, 1)
                link(v.tensor_copy(tot[:, :, :], bank[1][:, 0:NT * E].rearrange("p (t e) -> p e t", e=E)))
                link(v.tensor_tensor_scan(upto[:, :, :].rearrange("p e t -> p (e t)"), later_t[:, :], tot[:, :, :].rearrange("p e t -> p (e t)"),
                                          0.0, ALU.mult, ALU.add))
                link(v.tensor_tensor(full[:, :, :], step_t[:, :, :], upto[:, :, NT - 1:NT].to_broadcast([P, E, NT]), ALU.is_lt))
                link(v.tensor_reduce(need[:, :], full[:, :, :], AX.X, ALU.add))
                link(v.tensor_tensor_scan(end[:, :], ones[:, 0:E], need[:, :], 0.0, ALU.mult, ALU.add))
                link(v.tensor_tensor(begin[:, :], end[:, :], need[:, :], ALU.subtract))
                link(v.tensor_tensor(upto[:, :, :], upto[:, :, :], tot[:, :, :], ALU.subtract))
                link(v.scalar_tensor_tensor(upto[:, :, :], begin[:, :].unsqueeze(2).to_broadcast([P, E, NT]), float(P), upto[:, :, :], ALU.mult, ALU.add))
                link(v.tensor_tensor(place[:, :, :], bank[0][:, 0:NT * E].rearrange("p (t e) -> p t e", e=E),
                                     upto[:, :, :].rearrange("p e t -> p t e"), ALU.add))
                for k in range(2):
                    link(v.tensor_tensor(eq[:, :, :], hot[:, k, :, :], place[:, :, :], ALU.mult))
                    link(v.tensor_reduce(pos[:, k, :], eq[:, :, :], AX.X, ALU.add))
                link(v.tensor_copy(pos_i[:, :, :], pos[:, :, :]))
                link(v.tensor_scalar(lane_i[:, :, :], pos_i[:, :, :], P - 1, None, ALU.bitwise_and))
                link(v.tensor_copy(lane[:, :, :], lane_i[:, :, :]))
                link(v.tensor_scalar(pos_i[:, :, :], pos_i[:, :, :], 7, None, ALU.logical_shift_right))
                link(v.tensor_copy(slot[:, :, :], pos_i[:, :, :]))
                link(v.tensor_tensor(past[:, :, :], iota_slot[:, :].unsqueeze(1).to_broadcast([P, E, SLOTS]),
                                     end[:, :].unsqueeze(2).to_broadcast([P, E, SLOTS]), ALU.is_ge))
                link(v.tensor_reduce(who[:, :], past[:, :, :].rearrange("p e s -> p s e"), AX.X, ALU.add))
                link(v.tensor_scalar(who[:, :], who[:, :], float(E - 1), None, ALU.min))
                link(v.tensor_copy(who_i[:, :], who[:, :]))
                link(v.tensor_scalar(odd_i[:, :], who_i[:, :], 1, None, ALU.bitwise_and))
                link(v.tensor_scalar(ready_i[:, :], who[:, :], 1.0, None, ALU.add))
                link(v.tensor_scalar(end_i[:, :], end[:, :], 1.0, None, ALU.add))
                dve.sem_inc(hot_mm, 2)
                with dve.Fori(0, NT) as t:
                    for k in range(2):
                        dve.wait_ge(hot_mm, t * 2 + k + 1)
                        v.tensor_scalar(hot_lane[:, k, :], iota_lane[:, :], lane[:, k, ds(t, 1)], None, ALU.is_equal)
                        v.tensor_scalar(hot_slot[:, k, 0, :], iota_slot[:, :], slot[:, k, ds(t, 1)], tok1[:, ds(t, 1)], ALU.is_equal, ALU.mult)
                        v.tensor_scalar(hot_slot[:, k, 1, :], iota_slot[:, :], slot[:, k, ds(t, 1)], prob[:, k, ds(t, 1)],
                                        ALU.is_equal, ALU.mult).then_inc(hot_set, 1)
                dve.wait_ge(r_pe, 2)
                link(v.tensor_copy(tokp1[:, :], bank[2][:, 0:SLOTS]))
                link(v.tensor_copy(pair_p[:, :], bank[2][:, SLOTS:2 * SLOTS]))
                link(v.tensor_scalar(unused[:, :], tokp1[:, :], 0.0, spare[:, 0:1], ALU.is_equal, ALU.mult))
                link(v.tensor_scalar(tok_f[:, :], tokp1[:, :], -1.0, 0.0, ALU.add, ALU.max))
                link(v.tensor_copy(src_i[:, :], tok_f[:, :]))
                link(v.tensor_tensor(tok_f[:, :], tokp1[:, :], unused[:, :], ALU.add))
                link(v.tensor_scalar(dst_i[:, :], tok_f[:, :], -1.0, None, ALU.add))

        xg = [Xf[:, u * D:(u + 1) * D] for u in range(UNR)]
        xgt = [Xf[:, (3 + u) * D:(4 + u) * D].rearrange("p (k n) -> p k n", k=KD) for u in range(UNR)]
        yv = [Xf[:, (6 + u) * D:(7 + u) * D] for u in range(UNR)]
        col_s = [sb(f"col_s{u}", [P, 1], U32) for u in range(UNR)]
        col_d = [sb(f"col_d{u}", [P, 1], U32) for u in range(UNR)]
        col_p = [sb(f"col_p{u}", [P, 1]) for u in range(UNR)]
        xg_in = [sem(f"xg_in{u}") for u in range(UNR)]
        src_set, cols_set, xg_tp, xg_tpev, y_mm, y_act, y_dve, y_out, w_ready, tile_mm = (sem(n) for n in (
            "src_set", "cols_set", "xg_tp", "xg_tpev", "y_mm", "y_act", "y_dve", "y_out", "w_ready", "tile_mm"))

        with nc.Block() as block:
            @block.sync
            def _(sp):
                for w in range(2):
                    sp.wait_ge(w_in_sem[w], 16)
                    sp.sem_inc(w_ready, 1)
                with sp.Fori(0, E // 2 - 1) as i:
                    for w in range(2):
                        used = sp.value_load(end_i[0:1, ds(i * 2 + w, 1)], min_val=1, max_val=SLOTS + 1)
                        sp.wait_ge(tile_mm, used)
                        sp.dma_start(wslot[:, w, :, :], expert_w[ds(i * 2 + w + 2, 1), :, :].rearrange("a (k p) n -> p (a k) n", p=P)).then_inc(w_in_sem[w], 16)
                    for w in range(2):
                        sp.wait_ge(w_in_sem[w], i * 16 + 32)
                        sp.sem_inc(w_ready, 1)

            @block.gpsimd
            def _(pool):
                g = nc.gpsimd

                def gather(j, u):
                    pool.wait_ge(src_set, j + 1)
                    hold(pool, xg_tp, j * 2 + 2)
                    g.indirect_dma_start(out=xg[u], out_offset=None, in_=x_nrm[:, :],
                                         in_offset=bass.IndirectOffsetOnAxis(ap=col_s[u][:, 0:1], axis=0)).then_inc(xg_in[u], 16)

                def scatter(j, u, first=False):
                    pool.wait_ge(y_act, j + UNR + 1)
                    pool.wait_ge(y_dve, j + UNR + 1)
                    if not first:
                        pool.wait_ge(y_out, j * 16)
                    pool.sem_inc(held, 1)
                    g.indirect_dma_start(out=out[:, :], out_offset=bass.IndirectOffsetOnAxis(ap=col_d[u][:, 0:1], axis=0),
                                         in_=yv[u], in_offset=None, compute_op=ALU.add).then_inc(y_out, 16)

                for u in range(2):
                    pool.wait_ge(nrm_st[u], B * 16 + 16)
                pool.wait_ge(out_init, NT * 16 + 16)
                for u in range(UNR):
                    gather(u, u)
                for u in range(UNR):
                    gather(UNR + u, u)
                    scatter(u, u, first=u == 0)
                with pool.Fori(2, SLOTS // UNR) as i:
                    for u in range(UNR):
                        gather(i * UNR + u, u)
                        scatter(i * UNR + u - UNR, u)
                for u in range(UNR):
                    scatter(SLOTS - UNR + u, u)
                pool.wait_ge(y_out, SLOTS * 16)

            @block.tensor
            def _(pe):
                def turned(i, u):
                    j = i * UNR + u
                    pe.wait_ge(xg_in[u], i * 16 + 16)
                    for h in range(2):
                        pe.wait_ge(xg_tpev, j * 2 + h + 1)
                        for c in range(4):
                            k = 4 * h + c
                            mm = nc.tensor.transpose(bank[6 + h][:, c * P:(c + 1) * P], xg[u][:, k * P:(k + 1) * P], ident[:, :])
                        mm.then_inc(xg_tp, 1)

                def products(i, u):
                    j = i * UNR + u
                    ready = pe.value_load(ready_i[0:1, ds(j, 1)], min_val=1, max_val=E)
                    odd = pe.value_load(odd_i[0:1, ds(j, 1)], min_val=0, max_val=1)
                    pe.wait_ge(w_ready, ready)
                    pe.wait_ge(xg_tpev, j * 2 + 4)
                    pe.wait_ge(y_act, j + 1)
                    pe.wait_ge(y_dve, j + 1)
                    for n in range(2):
                        for k in range(KD):
                            mm = nc.tensor.matmul(bank[2 * u + n][:, :], xgt[u][:, k, :],
                                                  Tf[:, ds(odd * (KD * D) + (k * D + n * BANK), BANK)], start=(k == 0), stop=(k == KD - 1))
                        mm.then_inc(y_mm if n == 0 else tile_mm, 1)

                pe.sem_inc(xg_tp, 6)
                pe.sem_inc(tile_mm, 1)
                turned(0, 0)
                with pe.Fori(0, SLOTS // UNR - 1) as i:
                    for u in range(UNR):
                        turned(i + (u + 1) // UNR, (u + 1) % UNR)
                        products(i, u)
                for u in range(UNR):
                    if u + 1 < UNR:
                        turned(SLOTS // UNR - 1, u + 1)
                    products(SLOTS // UNR - 1, u)

            @block.scalar
            def _(act):
                def copies(j, u):
                    for h in range(2):
                        act.wait_ge(xg_tp, j * 2 + h + 7)
                        nc.scalar.copy(xgt[u][:, 4 * h:4 * h + 4, :].rearrange("p k n -> p (k n)"), bank[6 + h][:, :]).then_inc(xg_tpev, 1)

                def first_half(j, u):
                    act.wait_ge(y_mm, j + 1)
                    act.wait_ge(cols_set, j + 1)
                    nc.scalar.activation(yv[u][:, 0:BANK], bank[2 * u][:, :], ACT.Copy, scale=col_p[u][:, 0:1]).then_inc(y_act, 1)

                act.sem_inc(xg_tpev, 2)
                act.sem_inc(y_act, UNR)
                copies(0, 0)
                with act.Fori(0, SLOTS // UNR - 1) as i:
                    for u in range(UNR):
                        copies(i * UNR + u + 1, (u + 1) % UNR)
                        first_half(i * UNR + u, u)
                for u in range(UNR):
                    j = SLOTS - UNR + u
                    if u + 1 < UNR:
                        copies(j + 1, u + 1)
                    first_half(j, u)

            @block.vector
            def _(dve):
                v = nc.vector

                def sources(j, u):
                    v.tensor_copy(col_s[u][:, :], src_i[:, ds(j, 1)]).then_inc(src_set, 1)

                def columns(j, u):
                    v.tensor_copy(col_d[u][:, :], dst_i[:, ds(j, 1)])
                    v.tensor_copy(col_p[u][:, :], pair_p[:, ds(j, 1)]).then_inc(cols_set, 1)

                def second_half(j, u):
                    dve.wait_ge(cols_set, j + 1)
                    dve.wait_ge(tile_mm, j + 2)
                    v.tensor_scalar(yv[u][:, BANK:D], bank[2 * u + 1][:, :], col_p[u][:, 0:1], None, ALU.mult).then_inc(y_dve, 1)

                dve.sem_inc(y_dve, UNR)
                for u in range(UNR):
                    sources(u, u)
                    columns(u, u)
                with dve.Fori(0, SLOTS // UNR - 1) as i:
                    for u in range(UNR):
                        j = i * UNR + u
                        dve.wait_ge(xg_tp, j * 2 + 8)
                        sources(j + UNR, u)
                        second_half(j, u)
                        dve.wait_ge(y_out, j * 16 + 16)
                        columns(j + UNR, u)
                for u in range(UNR):
                    second_half(SLOTS - UNR + u, u)


_INS = ['x', 'ctx_4096', 'L0_attn_Win', 'L0_attn_bin', 'L0_attn_ln1_w', 'L0_attn_ln1_b', 'L0_attn_phz_re', 'L0_attn_phz_im',
        'L0_attn_lc_re', 'L0_attn_lc_im', 'L0_attn_sc_lin', 'L0_attn_ln2_w', 'L0_attn_ln2_b', 'L0_attn_W1', 'L0_attn_b1',
        'L0_attn_W2', 'L0_attn_b2', 'L0_attn_lnl_w', 'L0_attn_lnl_b', 'L0_attn_Wout', 'L0_attn_bout', 'L0_xattn_conv_w',
        'L0_xattn_bn_gamma', 'L0_xattn_bn_beta', 'L0_ffn_gate_w', 'L0_ffn_expert_w']


def kernel(**inputs):
    import numpy as _np
    import concourse.bacc as _bacc
    from concourse import mybir as _mybir
    from concourse.bass_utils import run_bass_kernel_spmd as _run

    nc = _bacc.Bacc("TRN2", target_bir_lowering=False, num_devices=1)
    arrays, args = {}, []
    for name in _INS:
        a = _np.ascontiguousarray(inputs[name])
        arrays[f"in_{name}_dram"] = a
        args.append(nc.dram_tensor(f"in_{name}_dram", a.shape, _mybir.dt.from_np(a.dtype), kind="ExternalInput").ap())
    b, s, d = inputs["x"].shape
    res = nc.dram_tensor("out_0_dram", (b * s + 128, d), _mybir.dt.float32, kind="ExternalOutput").ap()
    decoder_kernel(nc, *args, res)
    r = _run(nc, [arrays], core_ids=[0])
    return r.results[0]["out_0_dram"][:b * s].reshape(b, s, d)
```

```python
from contextlib import ExitStack

import concourse.bass as bass
from concourse import mybir

F32 = mybir.dt.float32
I32 = mybir.dt.int32
U32 = mybir.dt.uint32
BF16 = mybir.dt.bfloat16

ALU = mybir.AluOpType
ACT = mybir.ActivationFunctionType
AX = mybir.AxisListType
ds = bass.ds

P = 128
BANK = 512
EPS = 1e-5
FLT_MAX = 3.4028234663852886e38
LAMBDA = 0.6


def crucial_count(c):
    f = int(LAMBDA * c // 1)
    return f + f % 2


def decoder_kernel(nc, x, ctx_map, w_in, b_in, ln1_w, ln1_b, phz_re, phz_im, lc_re, lc_im, sc_lin, ln2_w, ln2_b,
                   w1, b1, w2, b2, lnl_w, lnl_b, w_out, b_out, conv_w, bn_gamma, bn_beta, gate_w, expert_w, out):
    B, S, D = x.shape
    DM = w_in.shape[0]
    NL = ln1_w.shape[0]
    FF = w1.shape[1]
    E = gate_w.shape[1]
    N = B * S
    NT = N // P
    KD = D // P
    FT = FF // P
    CW = BANK
    CH = N // CW
    TPC = CW // P
    BPC = CW // S
    CT = S // P
    KC = crucial_count(S)
    KS = S - KC
    ROUNDS = -(-KS // 8)
    PADS = ROUNDS * 8 - KS
    SLOTS = 2 * N // P + E - 1
    IN_FLIGHT = 3
    TAPS = conv_w.shape[2]
    HALF = TAPS // 2
    assert DM == P and SLOTS % IN_FLIGHT == 0 and D == 2 * BANK

    x2d = x.rearrange("b s d -> (b s) d")
    x_nrm = nc.dram_tensor("x_nrm", [N, D], F32, kind="Internal").ap()

    ctx = ExitStack()
    with ctx:
        def sb(name, shape, dt=F32):
            return ctx.enter_context(nc.sbuf_tensor(name, shape, dt))

        def sem(name):
            return ctx.enter_context(nc.semaphore(name))

        X = sb("X", [P, NT, D])
        Xf = X[:, :, :].rearrange("p t d -> p (t d)")
        T = sb("T", [P, KD, N])
        Tf = T[:, :, :].rearrange("p k n -> p (k n)")
        M = sb("M", [P, KD, N], mybir.dt.bfloat16)
        H = sb("H", [P, N])
        nat = sb("nat", [P, TPC, D])
        natf = nat[:, :, :].rearrange("p u d -> p (u d)")
        fin = sb("fin", [P, 2, CW])
        bank = [ctx.enter_context(nc.psum_tensor(f"bank{i}", [P, BANK], F32)) for i in range(8)]

        ident = sb("ident", [P, P])
        ones = sb("ones", [P, P])
        utri = sb("utri", [P, P])
        center = sb("center", [P, P])
        inv_col = sb("inv_col", [P, 1])
        neg_half = sb("neg_half", [P, NT])
        pos_half = sb("pos_half", [P, NT])
        late = sb("late", [P, 2 * D])
        wout_t, bout_b = late[:, 0:D], late[:, D:2 * D]
        gate = sb("gate", [P, KD, E])
        convw = sb("convw", [P, 2 * TAPS])
        bn_gb = sb("bn_gb", [P, 2])
        ewide = sb("ewide", [P, 3 * P + TAPS - 1])
        band = sb("band", [P, 2, 3 * P])
        layer_par = sb("layer_par", [P, NL, 13])
        block_par = sb("block_par", [P, 4])
        cur = sb("cur", [P, 13])
        st6 = sb("st6", [P, TPC, 12])
        mv = sb("mv", [P, TPC, 2])
        ve = sb("ve", [P, TPC, 4])
        rs = sb("rs", [P, TPC, 4])

        o = 8192

        def in_t(n):
            nonlocal o
            o += n
            return Tf[:, o - n:o]

        cos_t = in_t(NL * S).rearrange("p (l s) -> p l s", l=NL)
        sin_t = in_t(NL * S).rearrange("p (l s) -> p l s", l=NL)
        win_t = in_t(D).rearrange("p (k m) -> p k m", k=KD)
        w1raw = in_t(FF).rearrange("p (t m) -> p t m", t=FT)
        w2raw = in_t(FF)
        w1u = in_t(FF)
        w1s = in_t(FF)
        w2c = in_t(FF).rearrange("p (t m) -> p t m", t=FT)
        cs = in_t(P)
        b1f = in_t(FT)
        rows = in_t(P)
        ph = in_t(4 * NL).rearrange("p (k l) -> p k l", k=4)
        tmp = in_t(16 * NL).rearrange("p (k l) -> p k l", k=16)
        tab = in_t(4 * NL * S // 2).rearrange("p (k l s) -> p k l s", k=4, l=NL)
        assert o <= KD * N

        LN1W, LN1B, SCL, LN2W, LN2B, B2, B1, RHO, UR0, UI0 = 0, 1, 2, 3, 4, 5, 6, 10, 11, 12

        iota_lane = sb("iota_lane", [P, P])
        iota_slot = sb("iota_slot", [P, SLOTS])
        rev_e = sb("rev_e", [P, NT, E])
        step_t = sb("step_t", [P, E, NT])
        later_t = sb("later_t", [P, E * NT])
        tok1 = sb("tok1", [P, NT])
        spare = sb("spare", [P, 1])

        ld_rows = sem("ld_rows")
        ld_win = sem("ld_win")
        ld_wout = sem("ld_wout")
        ld_misc = sem("ld_misc")
        const_ready = sem("const_ready")
        set_pe = sem("set_pe")
        set_act = sem("set_act")
        set_dve = sem("set_dve")
        set_pool = sem("set_pool")
        NCONST = 9
        io = Tf[:, 0:1024].bitcast(I32)
        io_lane, io_slot = io[:, 0:P], io[:, 128:128 + SLOTS]
        io_rev = io[:, 256:384].rearrange("p (t e) -> p t e", e=E)
        io_step = io[:, 384:512].rearrange("p (e t) -> p e t", e=E)
        io_tok, io_spare = io[:, 512:528], io[:, 528:529]

        with nc.Block() as block:
            @block.sync
            def _(sp):
                for k, par in enumerate([ln1_w, ln1_b, sc_lin, ln2_w, ln2_b, b2, phz_re, phz_im, lc_re, lc_im]):
                    sp.dma_start(rows[k * NL:(k + 1) * NL, :], par[:, :]).then_inc(ld_rows, 16)
                sp.dma_start(rows[40:56, :], b1.rearrange("l (t p) -> (l t) p", p=P)).then_inc(ld_rows, 16)
                for k, par in enumerate([b_in, lnl_w, lnl_b]):
                    sp.dma_start(rows[56 + k:57 + k, :], par.rearrange("(a d) -> a d", a=1)).then_inc(ld_rows, 16)
                sp.dma_start(nat[:, 0, :], w_in[:, :]).then_inc(ld_win, 16)
                sp.dma_start(nat[:, 1, :].rearrange("p (t d) -> p t d", t=KD),
                             w_out.rearrange("(t p) d -> p t d", p=P)).then_inc(ld_wout, 16)
                sp.dma_start(bout_b, b_out.rearrange("(a d) -> a d", a=1).to_broadcast([P, D])).then_inc(ld_misc, 16)
                sp.dma_start(convw[:, :], conv_w.rearrange("a c j -> a (c j)").to_broadcast([P, 2 * TAPS])).then_inc(ld_misc, 16)
                sp.dma_start(bn_gb[:, 0:1], bn_gamma.rearrange("(a d) -> a d", a=1).to_broadcast([P, 1])).then_inc(ld_misc, 16)
                sp.dma_start(bn_gb[:, 1:2], bn_beta.rearrange("(a d) -> a d", a=1).to_broadcast([P, 1])).then_inc(ld_misc, 16)
                sp.dma_start(gate[:, :, :], gate_w.rearrange("(k p) e -> p k e", p=P)).then_inc(ld_misc, 16)
                sp.wait_ge(ld_misc, 5 * 16)

            @block.gpsimd
            def _(pool):
                g = nc.gpsimd
                g.memset(ident[:, :], 0.0).then_inc(const_ready, 1)
                g.memset(ones[:, :], 1.0).then_inc(const_ready, 1)
                g.memset(ewide[:, :], 0.0).then_inc(const_ready, 1)
                g.memset(inv_col[:, :], 1.0 / P).then_inc(const_ready, 1)
                g.memset(neg_half[:, :], -0.5).then_inc(const_ready, 1)
                g.memset(pos_half[:, :], 0.5).then_inc(const_ready, 1)
                pool.wait_ge(const_ready, 6)
                g.affine_select(out=ident[:, :], in_=ident[:, :], compare_op=ALU.not_equal, fill=1.0, base=0,
                                pattern=[[-1, P]], channel_multiplier=1).then_inc(const_ready, 1)
                g.affine_select(out=utri[:, :], in_=ones[:, :], compare_op=ALU.is_gt, fill=0.0, base=0,
                                pattern=[[1, P]], channel_multiplier=-1).then_inc(const_ready, 1)
                g.affine_select(out=ewide[:, :], in_=ewide[:, :], compare_op=ALU.not_equal, fill=1.0, base=-(P + HALF),
                                pattern=[[1, 3 * P + TAPS - 1]], channel_multiplier=-1).then_inc(const_ready, 1)
                g.iota(io_lane, [[1, P]], base=0, channel_multiplier=0).then_inc(const_ready, 1)
                g.iota(io_slot, [[1, SLOTS]], base=0, channel_multiplier=0).then_inc(const_ready, 1)
                g.iota(io_rev, [[0, NT], [-1, E]], base=E, channel_multiplier=0).then_inc(const_ready, 1)
                g.iota(io_step, [[0, E], [P, NT]], base=0, channel_multiplier=0).then_inc(const_ready, 1)
                g.iota(io_tok, [[P, NT]], base=1, channel_multiplier=1).then_inc(const_ready, 1)
                g.iota(io_spare, [[0, 1]], base=N + 1, channel_multiplier=1).then_inc(const_ready, 1)
                pool.wait_ge(set_dve, 17)
                g.tensor_tensor(tmp[:, 8, :], tmp[:, 6, :], pos_half[:, 0:NL], ALU.pow).then_inc(set_pool, 1)
                g.tensor_tensor(tmp[:, 9, :], tmp[:, 6, :], neg_half[:, 0:NL], ALU.pow).then_inc(set_pool, 1)

            @block.tensor
            def _(pe):
                pe.wait_ge(const_ready, NCONST)
                pe.wait_ge(ld_rows, 14 * 16)
                nc.tensor.transpose(bank[0][:, 0:59], rows[0:59, :], ident[0:59, 0:59]).then_inc(set_pe, 1)
                pe.wait_ge(ld_wout, 16)
                for t in range(KD):
                    mm = nc.tensor.transpose(bank[2 + t // 4][:, (t % 4) * P:(t % 4 + 1) * P],
                                             nat[:, 1, t * P:(t + 1) * P], ident[:, :])
                mm.then_inc(set_pe, 1)
                pe.wait_ge(set_dve, 4)
                nc.tensor.matmul(bank[1][:, 0:NL], center[:, :], layer_par[:, :, B2], start=True, stop=True)
                nc.tensor.matmul(bank[1][:, NL:NL + 1], center[:, :], block_par[:, 0:1],
                                 start=True, stop=True).then_inc(set_pe, 1)
                pe.wait_ge(ld_win, 16)
                for t in range(KD):
                    mm = nc.tensor.matmul(bank[4 + t // 4][:, (t % 4) * P:(t % 4 + 1) * P],
                                          nat[:, 0, t * P:(t + 1) * P], center[:, :], start=True, stop=True)
                mm.then_inc(set_pe, 1)
                pe.wait_ge(set_act, 2)
                for n in range(2):
                    mm = nc.tensor.matmul(bank[6 + n][:, :], block_par[:, 2:3].to_broadcast([P, P]),
                                          nat[:, 2, n * BANK:(n + 1) * BANK], start=True, stop=True)
                mm.then_inc(set_pe, 1)

            @block.scalar
            def _(act):
                act.wait_ge(set_pe, 2)
                for n in range(2):
                    nc.scalar.copy(nat[:, 2, n * BANK:(n + 1) * BANK], bank[2 + n][:, :]).then_inc(set_act, 1)
                act.wait_ge(set_pe, 4)
                for n in range(2):
                    nc.scalar.copy(win_t[:, 4 * n:4 * n + 4, :].rearrange("p k m -> p (k m)"), bank[4 + n][:, :]).then_inc(set_act, 1)
                act.wait_ge(set_dve, 18)
                nc.scalar.activation(layer_par[:, :, RHO], tmp[:, 10, :], ACT.Tanh).then_inc(set_act, 1)

            @block.vector
            def _(dve):
                v = nc.vector
                n_link = [0]

                def link(ins):
                    n_link[0] += 1
                    ins.then_inc(set_dve, 1)
                    dve.wait_ge(set_dve, n_link[0])

                dve.wait_ge(const_ready, NCONST)
                link(v.tensor_scalar(center[:, :], ident[:, :], -1.0 / P, None, ALU.add))
                dve.wait_ge(set_pe, 1)
                link(v.tensor_copy(layer_par[:, :, 0:6], bank[0][:, 0:24].rearrange("p (k l) -> p l k", k=6)))
                link(v.tensor_copy(layer_par[:, :, B1:B1 + FT], bank[0][:, 40:56].rearrange("p (l t) -> p l t", l=NL)))
                link(v.tensor_copy(block_par[:, 0:3], bank[0][:, 56:59]))
                link(v.tensor_copy(ph[:, :, :], bank[0][:, 24:40].rearrange("p (k l) -> p k l", k=4)))
                re, im, lr, li = (ph[:, k, :] for k in range(4))
                t_re, t_im, t_max, t_inv, t_a, t_b, t_q, t_z, t_sq, t_rsq, t_r, c_m, s_m, t_c, t_s = (tmp[:, k, :] for k in range(15))
                link(v.scalar_tensor_tensor(t_re, re, -1.0, re, ALU.mult, ALU.max))
                link(v.scalar_tensor_tensor(t_im, im, -1.0, im, ALU.mult, ALU.max))
                link(v.tensor_tensor(t_max, t_re, t_im, ALU.max))
                link(v.tensor_scalar(t_inv, t_max, 1e-37, None, ALU.max))
                link(v.reciprocal(t_inv, t_inv))
                link(v.tensor_tensor(t_a, re, t_inv, ALU.mult))
                link(v.tensor_tensor(t_b, im, t_inv, ALU.mult))
                link(v.tensor_scalar(t_z, t_max, 0.0, None, ALU.is_equal))
                link(v.tensor_tensor(t_a, t_a, t_z, ALU.add))
                link(v.tensor_tensor(t_c, t_a, t_a, ALU.mult))
                link(v.tensor_tensor(t_s, t_b, t_b, ALU.mult))
                link(v.tensor_tensor(t_q, t_c, t_s, ALU.add))
                dve.wait_ge(set_pool, 2)
                link(v.tensor_tensor(t_r, t_max, t_sq, ALU.mult))
                assert n_link[0] == 18
                link(v.tensor_tensor(c_m, t_a, t_rsq, ALU.mult))
                link(v.tensor_tensor(s_m, t_b, t_rsq, ALU.mult))
                link(v.tensor_tensor(t_re, lr, c_m, ALU.mult))
                link(v.tensor_tensor(t_im, li, s_m, ALU.mult))
                link(v.tensor_tensor(layer_par[:, :, UR0], t_re, t_im, ALU.subtract))
                link(v.tensor_tensor(t_re, lr, s_m, ALU.mult))
                link(v.tensor_tensor(t_im, li, c_m, ALU.mult))
                link(v.tensor_tensor(t_re, t_re, t_im, ALU.add))
                link(v.tensor_scalar(layer_par[:, :, UI0], t_re, -1.0, None, ALU.mult))
                dve.wait_ge(set_pe, 3)
                link(v.tensor_copy(layer_par[:, :, B2], bank[1][:, 0:NL]))
                link(v.tensor_copy(block_par[:, 0:1], bank[1][:, NL:NL + 1]))
                dve.wait_ge(set_act, 2)
                for n in range(2):
                    link(v.tensor_scalar(wout_t[:, n * BANK:(n + 1) * BANK], bank[2 + n][:, :], block_par[:, 1:2], None, ALU.mult))
                dve.wait_ge(set_pe, 5)
                dve.wait_ge(ld_misc, 5 * 16)
                for n in range(2):
                    link(v.tensor_tensor(bout_b[:, n * BANK:(n + 1) * BANK], bank[6 + n][:, :],
                                         bout_b[:, n * BANK:(n + 1) * BANK], ALU.add))

        held = sem("held")

        def hold(eng, done, n):
            eng.wait_ge(done, n)
            eng.sem_inc(held, 1)

        r_in = [sem(f"r_in{u}") for u in range(TPC)]
        r_bias = sem("r_bias")
        AHEAD = 3

        o2_mm, x1_done = sem("o2_mm"), sem("x1_done")

        def row_of(q, u):
            return X[:, ds(q * TPC + u, 1), :].rearrange("p a d -> p (a d)")

        def load_row(sp, q, u):
            sp.dma_start(row_of(q, u), x2d[ds(q * CW + u * P, P), :]).then_inc(r_in[u], 16)

        def add_bias(pool, q, u):
            hold(pool, r_in[u], q * 16 + 16)
            nc.gpsimd.tensor_tensor(row_of(q, u), row_of(q, u), bout_b, ALU.add).then_inc(r_bias, 1)

        ln_stat = sem("ln_stat")
        ln_mean = sem("ln_mean")
        ln_var = sem("ln_var")
        ln_rstd = sem("ln_rstd")
        ln_out = sem("ln_out")

        def ln_stats(dve, src, u, n):
            v = nc.vector
            v.bn_stats(st6[:, u, 0:6], src[:, 0:BANK])
            v.bn_stats(st6[:, u, 6:12], src[:, BANK:D]).then_inc(ln_stat, 1)
            hold(dve, ln_stat, n)
            v.bn_aggr(mv[:, u, :], st6[:, u, :]).then_inc(ln_mean, 1)
            dve.wait_ge(ln_mean, n)
            v.tensor_scalar(ve[:, u, 0:1], mv[:, u, 1:2], EPS, None, ALU.add).then_inc(ln_var, 1)

        def ln_pow(pool, u, n):
            pool.wait_ge(ln_var, n)
            nc.gpsimd.tensor_tensor(rs[:, u, 0:1], ve[:, u, 0:1], neg_half[:, 0:1], ALU.pow).then_inc(ln_rstd, 1)

        def ln_apply(dve, dst, src, u, n):
            dve.wait_ge(ln_rstd, n)
            nc.vector.tensor_scalar(dst, src, mv[:, u, 0:1], rs[:, u, 0:1], ALU.subtract, ALU.mult).then_inc(ln_out, 1)

        def products(pe, q, u):
            for n in range(2):
                pe.wait_ge(x1_done, q * 8 + 2 * u + n + 5)
                cols = slice(n * BANK, (n + 1) * BANK)
                nc.tensor.matmul(bank[2 + 2 * (u % 2) + n][:, :], yn[:, q * CW + u * P:q * CW + (u + 1) * P],
                                 wout_t[:, cols], start=True, stop=False)
                pe.wait_ge(r_bias, q * TPC + u + 1)
                nc.tensor.matmul(bank[2 + 2 * (u % 2) + n][:, :], ident[:, :], X[:, q * TPC + u, cols],
                                 start=False, stop=True).then_inc(o2_mm, 1)

        def rows(act, q, u):
            for n in range(2):
                hold(act, o2_mm, q * 8 + 2 * u + n + 1)
                nc.scalar.copy(row_of(q, u)[:, n * BANK:(n + 1) * BANK], bank[2 + 2 * (u % 2) + n][:, :]).then_inc(x1_done, 1)

        x_in = [sem(f"x_in{u}") for u in range(TPC)]
        tab_pool = sem("tab_pool")
        tab_dve = sem("tab_dve")
        emb_tp = sem("emb_tp")
        emb_tpev = sem("emb_tpev")
        emb_mm = sem("emb_mm")
        emb_ev = sem("emb_ev")
        xn_t = X[:, :, :].rearrange("p t d -> p (t d)").rearrange("p (k n) -> p k n", k=KD)

        with nc.Block() as block:
            @block.sync
            def _(sp):
                with sp.Fori(0, CH) as q:
                    for u in range(TPC):
                        sp.wait_ge(emb_tp, q * 8 + 2 * u + 2)
                        sp.dma_start(nat[:, u, :], x2d[ds(q * CW + u * P, P), :]).then_inc(x_in[u], 16)

            @block.gpsimd
            def _(pool):
                g = nc.gpsimd
                c_m, s_m, t_c, t_s, t_q = tmp[:, 11, :], tmp[:, 12, :], tmp[:, 13, :], tmp[:, 14, :], tmp[:, 6, :]
                n_tab = [0]

                def step(*how):
                    if n_tab[0]:
                        pool.wait_ge(tab_pool, n_tab[0])
                    g.tensor_tensor(*how).then_inc(tab_pool, 1)
                    n_tab[0] += 1

                def angles(m):
                    cb = c_m.unsqueeze(2).to_broadcast([P, NL, m])
                    sb_ = s_m.unsqueeze(2).to_broadcast([P, NL, m])
                    step(tab[:, 0, :, 0:m], cos_t[:, :, 0:m], cb, ALU.mult)
                    step(tab[:, 1, :, 0:m], sin_t[:, :, 0:m], sb_, ALU.mult)
                    step(tab[:, 2, :, 0:m], sin_t[:, :, 0:m], cb, ALU.mult)
                    step(tab[:, 3, :, 0:m], cos_t[:, :, 0:m], sb_, ALU.mult)
                    step(cos_t[:, :, m:2 * m], tab[:, 0, :, 0:m], tab[:, 1, :, 0:m], ALU.subtract)

                def doubled(m):
                    step(sin_t[:, :, m:2 * m], tab[:, 2, :, 0:m], tab[:, 3, :, 0:m], ALU.add)
                    step(t_c, c_m, c_m, ALU.mult)
                    step(t_s, s_m, s_m, ALU.mult)
                    step(t_q, c_m, s_m, ALU.mult)
                    step(c_m, t_c, t_s, ALU.subtract)
                    step(s_m, t_q, t_q, ALU.add)

                g.memset(cos_t[:, :, 0:1], 1.0)
                g.memset(sin_t[:, :, 0:1], 0.0).then_inc(tab_pool, 1)
                n_tab[0] = 1
                assert S == 1 << (NT // 2)
                for t in range(NT):
                    ln_pow(pool, t % TPC, t + 1)
                    (angles, doubled)[t % 2](1 << (t // 2))

            @block.vector
            def _(dve):
                v = nc.vector
                with dve.Fori(0, CH) as q:
                    for u in range(TPC + 1):
                        if u < TPC:
                            dve.wait_ge(x_in[u], q * 16 + 16)
                            ln_stats(dve, nat[:, u, :], u, q * TPC + u + 1)
                        if u > 0:
                            ln_apply(dve, nat[:, u - 1, :], nat[:, u - 1, :], u - 1, q * TPC + u)
                n_link = [0]

                def link(ins):
                    n_link[0] += 1
                    ins.then_inc(tab_dve, 1)
                    dve.wait_ge(tab_dve, n_link[0])

                for c in range(2):
                    link(v.tensor_scalar(band[:, c, :], ewide[:, 0:3 * P], convw[:, c * TAPS:c * TAPS + 1], None, ALU.mult))
                    for j in range(1, TAPS):
                        w = convw[:, c * TAPS + j:c * TAPS + j + 1]
                        link(v.scalar_tensor_tensor(band[:, c, :], ewide[:, j:j + 3 * P], w, band[:, c, :], ALU.mult, ALU.add))
                link(v.tensor_copy(iota_lane[:, :], io_lane))
                link(v.tensor_copy(iota_slot[:, :], io_slot))
                link(v.tensor_copy(rev_e[:, :, :], io_rev))
                link(v.tensor_copy(step_t[:, :, :], io_step))
                link(v.tensor_copy(tok1[:, :], io_tok))
                link(v.tensor_copy(spare[:, :], io_spare))
                link(v.tensor_scalar(later_t[:, :], step_t[:, :, :].rearrange("p e t -> p (e t)"), 0.0, None, ALU.is_gt))


            @block.tensor
            def _(pe):
                pe.sem_inc(emb_tp, 8)
                with pe.Fori(0, CH) as q:
                    for u in range(TPC):
                        pe.wait_ge(ln_out, q * TPC + u + 1)
                        for h in range(2):
                            pe.wait_ge(emb_tpev, q * 8 + 2 * u + h + 1)
                            for j in range(4):
                                k = 4 * h + j
                                mm = nc.tensor.transpose(bank[2 * (u % 2) + h][:, j * P:(j + 1) * P], nat[:, u, k * P:(k + 1) * P], ident[:, :])
                            mm.then_inc(emb_tp, 1)
                    pe.wait_ge(emb_tpev, q * 8 + 12)
                    pe.wait_ge(emb_ev, q + 1)
                    for k in range(KD):
                        mm = nc.tensor.matmul(bank[4][:, :], win_t[:, k, :], xn_t[:, k, ds(q * CW, CW)], start=(k == 0), stop=(k == KD - 1))
                    mm.then_inc(emb_mm, 1)

            @block.scalar
            def _(act):
                act.sem_inc(emb_tpev, 4)
                act.sem_inc(emb_ev, 1)
                with act.Fori(0, CH) as q:
                    for u in range(TPC):
                        for h in range(2):
                            act.wait_ge(emb_tp, q * 8 + 2 * u + h + 9)
                            nc.scalar.copy(xn_t[:, 4 * h:4 * h + 4, ds(q * CW + u * P, P)],
                                           bank[2 * (u % 2) + h][:, :].rearrange("p (k n) -> p k n", k=4)).then_inc(emb_tpev, 1)
                    act.wait_ge(emb_mm, q + 1)
                    nc.scalar.activation(H[:, ds(q * CW, CW)], bank[4][:, :], ACT.Identity, bias=block_par[:, 0:1]).then_inc(emb_ev, 1)

        assert B == 2 * NL
        GT = 2 * KD
        NG = B // 2
        QUICK = 2
        WINDOW = 8 * QUICK
        WK = WINDOW + S
        LOW, HIGH = -0.5, 0.0
        AIM = KS - WINDOW / 2 + 0.5
        AIM_S = 2 * AIM - S
        cT = Xf[:, 8192:16384].rearrange("p (b k s) -> p b k s", b=4, k=KD)
        tabf = tab.rearrange("p k l s -> p (k l s)")
        cin = [[tabf[:, 0:D], tabf[:, D:2 * D]],
               [win_t.rearrange("p k m -> p (k m)"), fin[:, :, :].rearrange("p a n -> p (a n)")]]
        w = Tf[:, 0:GT * WK].rearrange("p (i s) -> p i s", i=GT)
        under = Tf[:, GT * WK:GT * WK + GT * S // 2].bitcast(BF16).rearrange("p (i s) -> p i s", i=GT)
        so = GT * WK + GT * S // 2

        def in_sel(*shape):
            nonlocal so
            n = 1
            for d in shape:
                n *= d
            so += n
            assert so <= 8192
            names = "abc"[:len(shape)]
            return Tf[:, so - n:so].rearrange(f"p ({' '.join(names)}) -> p {' '.join(names)}", **dict(zip(names, shape)))

        st_c, mv_c = in_sel(GT, 6), in_sel(GT, 2)
        dev, t_lo, t_hi, width, t_1, t_2, s_lo, s_hi, s_1, rise, inv, miss, side, step = (in_sel(GT) for _ in range(14))
        c_low, c_width, c_one, c_aim, c_inv = (in_sel(GT) for _ in range(5))
        m_cnt, off = in_sel(GT), in_sel(GT)
        top8 = in_sel(GT, 8)
        pad01 = w[:, :, 0:WINDOW]
        pad_neg = in_sel(GT, WINDOW)
        off_max, off_any, off_one = in_sel(NG), in_sel(1), in_sel(1)
        off_i = sb("off_i", [P, 1], I32)
        ctx_in = [[sem(f"ctx_in{u}{h}") for h in range(CT)] for u in range(2)]
        ctx_tp, ctx_set, c_stat, c_mean, sel_pool = (sem(n) for n in ("ctx_tp", "ctx_set", "c_stat", "c_mean", "sel_pool"))
        t0_set, s0_sum, t1_set, s1_sum, t2_set, counted, sel_small, w_set = (sem(n) for n in (
            "t0_set", "s0_sum", "t1_set", "s1_sum", "t2_set", "counted", "sel_small", "w_set"))
        round_max, round_rep, mask_done, off_set, off_mm = (sem(n) for n in ("round_max", "round_rep", "mask_done", "off_set", "off_mm"))

        CHAIN = 29
        hid = Xf[:, 0:2 * FT * CW].rearrange("p (q t n) -> p q t n", q=2, t=FT)
        a_buf = Xf[:, 4096:6144]
        b_buf = Xf[:, 6144:8192]
        yn, sq = natf[:, 0:N], natf[:, N:2 * N]
        BC, ZO, HD, VAR, SMALL, PREP = (0, 1), (2, 3), (4, 5), (6, 7), 6, 7
        w1_in, w2_in = sem("w1_in"), sem("w2_in")
        cur_set, cs_set = sem("cur_set"), sem("cs_set")
        w1_tp, w1_u, w1_s, w2_tp, w2_set, b1_mm, b1_set = (sem(n) for n in ("w1_tp", "w1_u", "w1_s", "w2_tp", "w2_set", "b1_mm", "b1_set"))
        sq1, var1, ve1, rt1, bc1, yn1 = (sem(n) for n in ("sq1", "var1", "ve1", "rt1", "bc1", "yn1"))
        sq2, var2, ve2, rt2, bc2, yn2 = (sem(n) for n in ("sq2", "var2", "ve2", "rt2", "bc2", "yn2"))
        act1, a_in, b_in, scanned, a_out, b_out, z_mm, h_mid = (sem(n) for n in ("act1", "a_in", "b_in_", "scanned", "a_out", "b_out_", "z_mm", "h_mid"))
        hid_mm, hid_act, o_mm, h_out = (sem(n) for n in ("hid_mm", "hid_act", "o_mm", "h_out"))

        def chunk(buf, q):
            return buf[:, q * CW:(q + 1) * CW]

        def by_seq(buf, q):
            return chunk(buf, q).rearrange("p (b s) -> p b s", b=BPC)

        def variance(q):
            for i in range(TPC):
                mm = nc.tensor.matmul(bank[VAR[q % 2]][:, i:i + 1], chunk(sq, q)[:, i * P:(i + 1) * P], inv_col[:, :], start=True, stop=True)
            return mm

        def spread(q):
            for i in range(TPC):
                mm = nc.tensor.matmul(bank[BC[q % 2]][:, i * P:(i + 1) * P], rs[:, q, i:i + 1].to_broadcast([P, P]), ident[:, :], start=True, stop=True)
            return mm

        with nc.Block() as block:
            @block.sync
            def _(sp):
                sp.sem_inc(w1_tp, 1)
                sp.sem_inc(w2_tp, 1)
                sp.sem_inc(ctx_tp, 8)
                sp.sem_inc(x1_done, 8)
                with sp.Fori(0, NL) as l:
                    sp.wait_ge(w1_tp, l + 1)
                    sp.dma_start(w1raw, w1[ds(l, 1), :, :].rearrange("a (t p) d -> p (a t) d", p=P)).then_inc(w1_in, 16)
                    sp.wait_ge(w2_tp, l + 1)
                    sp.dma_start(w2raw, w2[ds(l, 1), :, :].rearrange("a p f -> p (a f)")).then_inc(w2_in, 16)
                    for u in range(2):
                        sp.wait_ge(ctx_tp, l * 8 + 4 * u + 4)
                        for h in range(CT):
                            sp.dma_start(cin[u][h], ctx_map[ds(l * 2 + u, 1), h * P:(h + 1) * P, :].rearrange("a p l -> p (a l)")).then_inc(ctx_in[u][h], 16)
                sp.wait_ge(o_mm, NL * CH)
                for u in range(TPC):
                    load_row(sp, 0, u)

            @block.gpsimd
            def _(pool):
                g = nc.gpsimd

                def power(q, n, ve_done, done):
                    pool.wait_ge(ve_done, n)
                    g.tensor_tensor(rs[:, q, :], ve[:, q, :], neg_half[:, 0:TPC], ALU.pow).then_inc(done, 1)

                def chain(g_, n, *how):
                    pool.wait_ge(sel_pool, g_ * CHAIN + n + 1)
                    g.tensor_tensor(*how).then_inc(sel_pool, 1)

                def chained(g_, n, done):
                    pool.wait_ge(sel_pool, g_ * CHAIN + n + 1)
                    pool.sem_inc(done, 1)

                def first_thresholds(g_):
                    pool.wait_ge(c_mean, g_ * GT + GT)
                    for n, how in enumerate((
                            (dev, mv_c[:, :, 1], pos_half[:, 0:GT], ALU.pow),
                            (t_lo, dev, c_low, ALU.mult),
                            (t_lo, t_lo, mv_c[:, :, 0], ALU.add),
                            (width, dev, c_width, ALU.mult),
                            (t_hi, t_lo, width, ALU.add))):
                        chain(g_, n, *how)
                    chained(g_, 5, t0_set)

                def third_threshold(g_):
                    pool.wait_ge(s0_sum, g_ * (2 * GT) + 2 * GT)
                    for n, how in enumerate((
                            (rise, s_hi, s_lo, ALU.subtract),
                            (inv, rise, rise, ALU.mult),
                            (inv, inv, c_one, ALU.add),
                            (inv, inv, c_inv, ALU.pow),
                            (inv, inv, rise, ALU.mult),
                            (miss, c_aim, s_lo, ALU.subtract),
                            (miss, miss, width, ALU.mult),
                            (miss, miss, inv, ALU.mult),
                            (t_1, t_lo, miss, ALU.add))):
                        chain(g_, 5 + n, *how)
                    chained(g_, 14, t1_set)

                def last_threshold(g_):
                    pool.wait_ge(s1_sum, g_ * GT + GT)
                    hold(pool, sel_pool, g_ * CHAIN + 15)
                    g.tensor_scalar(side, s_1, AIM_S, None, ALU.is_le).then_inc(sel_pool, 1)
                    pool.wait_ge(counted, g_ * GT + 1)
                    for n, how in enumerate((
                            (rise, rise, side, ALU.mult),
                            (rise, rise, s_lo, ALU.add),
                            (rise, rise, s_1, ALU.subtract),
                            (width, width, side, ALU.mult),
                            (width, width, t_lo, ALU.add),
                            (width, width, t_1, ALU.subtract),
                            (inv, rise, rise, ALU.mult),
                            (inv, inv, c_one, ALU.add),
                            (inv, inv, c_inv, ALU.pow),
                            (rise, rise, inv, ALU.mult),
                            (rise, rise, width, ALU.mult),
                            (miss, c_aim, s_1, ALU.subtract),
                            (miss, miss, rise, ALU.mult),
                            (t_2, t_1, miss, ALU.add))):
                        chain(g_, 15 + n, *how)
                    chained(g_, CHAIN, t2_set)

                def layer(l):
                    sin_l = sin_t[:, ds(l, 1), :].to_broadcast([P, BPC, S])
                    for q in range(CH):
                        hold(pool, act1, l * CH + q + 1)
                        g.tensor_tensor(by_seq(b_buf, q), by_seq(yn, q), sin_l, ALU.mult).then_inc(b_in, 1)
                    for q in range(CH):
                        hold(pool, scanned, l * CH + q + 1)
                        g.tensor_tensor(by_seq(b_buf, q), by_seq(b_buf, q), sin_l, ALU.mult).then_inc(b_out, 1)
                    if not isinstance(l, int):
                        last_threshold(l - 1)
                    for q in range(CH):
                        power(q, l * CH + q + 1, ve2, rt2)
                        if q == 1:
                            first_thresholds(l)
                    for q in range(CH):
                        power(q, l * CH + q + CH + 1, ve1, rt1)
                        if q == 0:
                            third_threshold(l)

                for dst, val in ((c_low, LOW), (c_width, HIGH - LOW), (c_one, 1.0), (c_aim, AIM_S), (c_inv, -1.0)):
                    ins = g.memset(dst, val)
                ins.then_inc(sel_pool, 1)
                for q in range(CH):
                    power(q, q + 1, ve1, rt1)
                layer(0)
                with pool.Fori(1, NL) as l:
                    layer(l)
                last_threshold(NG - 1)
                for u in range(AHEAD):
                    add_bias(pool, 0, u)

            @block.tensor
            def _(pe):
                def var_first(q, n):
                    pe.wait_ge(sq1, n)
                    if q >= 2:
                        pe.wait_ge(ve1, n - 2)
                    variance(q).then_inc(var1, 1)

                def spread_first(q, n):
                    pe.wait_ge(rt1, n)
                    if q >= 2:
                        pe.wait_ge(yn1, n - 2)
                    spread(q).then_inc(bc1, 1)

                for q in range(CH):
                    var_first(q, q + 1)
                for q in range(CH):
                    spread_first(q, q + 1)
                with pe.Fori(0, NL) as l:
                    base = l * CH

                    def z(q):
                        pe.wait_ge(a_out, base + q + 1)
                        pe.wait_ge(b_out, base + q + 1)
                        if q >= 2:
                            pe.wait_ge(h_mid, base + q - 1)
                        nc.tensor.matmul(bank[ZO[q % 2]][:, :], cs, chunk(a_buf, q), start=True, stop=False)
                        nc.tensor.matmul(bank[ZO[q % 2]][:, :], cs, chunk(b_buf, q), start=False, stop=True).then_inc(z_mm, 1)

                    def var_second(q):
                        pe.wait_ge(sq2, base + q + 1)
                        if q >= 2:
                            pe.wait_ge(ve2, base + q - 1)
                        variance(q).then_inc(var2, 1)

                    def spread_second(q):
                        pe.wait_ge(rt2, base + q + 1)
                        if q >= 2:
                            pe.wait_ge(yn2, base + q - 1)
                        spread(q).then_inc(bc2, 1)

                    def feed_forward(q):
                        pe.wait_ge(yn2, base + q + 1)
                        if q == 0:
                            pe.wait_ge(ctx_set, l * 8 + 10)
                        for t in range(FT):
                            pe.wait_ge(hid_act, l * (CH * FT) + q * FT + t + 1)
                            nc.tensor.matmul(bank[HD[t % 2]][:, :], w1s[:, t * P:(t + 1) * P], chunk(yn, q), start=True, stop=True).then_inc(hid_mm, 1)
                        pe.wait_ge(h_mid if q < 2 else h_out, base + (q + 3 if q < 2 else q - 1))
                        for t in range(FT):
                            pe.wait_ge(hid_act, l * (CH * FT) + q * FT + t + 3)
                            mm = nc.tensor.matmul(bank[ZO[q % 2]][:, :], w2c[:, t, :], hid[:, q % 2, t, :], start=(t == 0), stop=(t == FT - 1))
                        mm.then_inc(o_mm, 1)

                    def fill(n):
                        u, j = divmod(n, 4)
                        if j == 0:
                            for h in range(CT):
                                pe.wait_ge(ctx_in[u][h], l * 16 + 16)
                        pe.wait_ge(ctx_set, l * 8 + n + 1)
                        for k in (2 * j, 2 * j + 1):
                            for h in range(CT):
                                mm = nc.tensor.transpose(bank[HD[j % 2]][:, (k % 2) * S + h * P:(k % 2) * S + (h + 1) * P],
                                                         cin[u][h][:, k * P:(k + 1) * P], ident[:, :])
                        mm.then_inc(ctx_tp, 1)

                    pe.wait_ge(w1_in, l * 16 + 16)
                    pe.wait_ge(ve1, base + CH)
                    for t in range(FT):
                        mm = nc.tensor.transpose(bank[PREP][:, t * P:(t + 1) * P], w1raw[:, t, :], ident[:, :])
                    mm.then_inc(w1_tp, 1)
                    fill(0)
                    fill(1)
                    pe.wait_ge(w1_u, l + 1)
                    pe.wait_ge(w1_s, l + 1)
                    pe.wait_ge(w2_in, l * 16 + 16)
                    for t in range(FT):
                        mm = nc.tensor.matmul(bank[PREP][:, t * P:(t + 1) * P], w2raw[:, t * P:(t + 1) * P], center[:, :], start=True, stop=True)
                    mm.then_inc(w2_tp, 1)
                    pe.wait_ge(cur_set, l + 1)
                    for t in range(FT):
                        mm = nc.tensor.matmul(bank[SMALL][:, 32 + t:33 + t], w1u[:, t * P:(t + 1) * P], cur[:, LN2B:LN2B + 1], start=True, stop=True)
                    mm.then_inc(b1_mm, 1)
                    pe.wait_ge(cs_set, l + 1)
                    for n in range(2, 6):
                        fill(n)
                    z(0)
                    fill(6)
                    fill(7)
                    z(1)
                    z(2)
                    pe.wait_ge(b1_set, l + 1)
                    pe.wait_ge(w2_set, l + 1)
                    var_second(0)
                    z(3)
                    var_second(1)
                    spread_second(0)
                    var_second(2)
                    spread_second(1)
                    feed_forward(0)
                    var_second(3)
                    spread_second(2)
                    feed_forward(1)
                    spread_second(3)
                    var_first(0, base + CH + 1)
                    feed_forward(2)
                    var_first(1, base + CH + 2)
                    spread_first(0, base + CH + 1)
                    feed_forward(3)
                    var_first(2, base + CH + 3)
                    spread_first(1, base + CH + 2)
                    var_first(3, base + CH + 4)
                    spread_first(2, base + CH + 3)
                    spread_first(3, base + CH + 4)
                pe.wait_ge(yn1, NL * CH + CH)
                for u in range(2):
                    products(pe, 0, u)
                pe.wait_ge(off_set, 1)
                nc.tensor.matmul(bank[0][:, 0:1], ones[:, :], off_any[:, 0:1], start=True, stop=True).then_inc(off_mm, 1)

            @block.scalar
            def _(act):
                a = nc.scalar

                def square(q, done):
                    a.activation(chunk(sq, q), chunk(H, q), ACT.Square).then_inc(done, 1)

                act.sem_inc(hid_act, 2)
                act.sem_inc(ctx_set, 2)
                for q in range(CH):
                    square(q, sq1)
                def masks(g):
                    hold(act, round_rep, (g + 1) * (QUICK * GT) + GT)
                    for u in range(2):
                        a.activation(M[:, :, ds((g * 2 + u) * S, S)], w[:, u * KD:(u + 1) * KD, WINDOW:WK][:, :, ::-1], ACT.Relu,
                                     scale=1e-30, bias=ones[:, 0:1]).then_inc(mask_done, 1)

                def layer(l):
                    act.wait_ge(cur_set, l + 1)
                    for q in range(CH):
                        if q == 2:
                            act.wait_ge(w1_tp, l + 2)
                            a.copy(w1u, bank[PREP][:, :]).then_inc(w1_u, 1)
                        act.wait_ge(yn1, l * CH + q + 1)
                        a.activation(chunk(yn, q), chunk(yn, q), ACT.Silu, scale=cur[:, LN1W:LN1W + 1], bias=cur[:, LN1B:LN1B + 1]).then_inc(act1, 1)
                    act.wait_ge(w2_tp, l + 2)
                    a.copy(w2c.rearrange("p t m -> p (t m)"), bank[PREP][:, :]).then_inc(w2_set, 1)
                    for n in range(8):
                        act.wait_ge(ctx_tp, l * 8 + n + 9)
                        hold(act, w_set, l * 2 + 2)
                        a.copy(cT[:, ds((l % 2) * 2 + n // 4, 1), 2 * (n % 4):2 * (n % 4) + 2, :].rearrange("p a k s -> p (a k) s"),
                               bank[HD[n % 2]][:, :].rearrange("p (k s) -> p k s", k=2)[:, :, ::-1]).then_inc(ctx_set, 1)
                    for q in range(CH):
                        act.wait_ge(h_mid, l * CH + q + 1)
                        square(q, sq2)
                    act.wait_ge(b1_set, l + 1)
                    def count_signs(thr, sums, done, i):
                        u, k = divmod(i, KD)
                        a.activation(M[:, k, ds((l * 2 + u) * S, S)], cT[:, ds((l % 2) * 2 + u, 1), k, :].rearrange("p a s -> p (a s)"), ACT.Sign,
                                     scale=-1.0, bias=thr[:, i:i + 1], accum_out=sums[:, i:i + 1]).then_inc(done, 1)

                    def search(q):
                        if q == 0 and not isinstance(l, int):
                            masks(l - 2)
                        if q == 0:
                            hold(act, t0_set, l + 2)
                        for n in range(*((0, 10), (10, 21), (21, 32), (0, 0))[q]):
                            if n == GT:
                                hold(act, s0_sum, l * (2 * GT) + GT)
                            count_signs(*((t_lo, s_lo) if n < GT else (t_hi, s_hi)), s0_sum, n % GT)
                        if q == 3:
                            hold(act, t1_set, l + 1)
                            for i in range(GT):
                                count_signs(t_1, s_1, s1_sum, i)

                    for q in range(CH):
                        for t in range(FT):
                            if q >= 2:
                                act.wait_ge(o_mm, l * CH + q - 1)
                            act.wait_ge(hid_mm, l * (CH * FT) + q * FT + t + 1)
                            a.activation(hid[:, q % 2, t, :], bank[HD[t % 2]][:, :], ACT.Silu, bias=b1f[:, t:t + 1]).then_inc(hid_act, 1)
                        if q > 0:
                            act.wait_ge(h_out, l * CH + q)
                            square(q - 1, sq1)
                        if q < CH - 1:
                            search(q)
                    act.wait_ge(h_out, l * CH + CH)
                    square(CH - 1, sq1)
                    search(CH - 1)

                layer(0)
                layer(1)
                with act.Fori(2, NL) as l:
                    layer(l)
                masks(NG - 2)
                for u in range(2):
                    rows(act, 0, u)
                masks(NG - 1)

            @block.vector
            def _(dve):
                v = nc.vector

                def tile(g, i):
                    return cT[:, ds((g % 2) * 2 + i // KD, 1), i % KD, :].rearrange("p a s -> p (a s)")

                def stats(g, first):
                    for i in range(first, first + 4):
                        if i % 2 == 0:
                            hold(dve, ctx_set, g * 8 + i // 2 + 3)
                        v.bn_stats(st_c[:, i, :], tile(g, i)).then_inc(c_stat, 1)

                def means(g):
                    hold(dve, t0_set, g + 1)
                    for i in range(GT):
                        hold(dve, c_stat, g * GT + i + 1)
                        v.bn_aggr(mv_c[:, i, :], st_c[:, i, :]).then_inc(c_mean, 1)

                def counts(g, u):
                    if u == 0:
                        hold(dve, t2_set, g + 1)
                        hold(dve, w_set, g * 2 + 4)
                    for i in range(u * KD, (u + 1) * KD):
                        v.tensor_scalar(under[:, i, :], tile(g, i), t_2[:, i:i + 1], 0.0, ALU.is_lt, ALU.add,
                                        accum_out=m_cnt[:, i:i + 1]).then_inc(counted, 1)

                def without_under(g):
                    hold(dve, mask_done, g * 2 + 2)
                    for u in range(2):
                        hold(dve, counted, g * GT + (u + 1) * KD + 1)
                        v.scalar_tensor_tensor(w[:, u * KD:(u + 1) * KD, WINDOW:WK], under[:, u * KD:(u + 1) * KD, :], -FLT_MAX,
                                               cT[:, ds((g % 2) * 2 + u, 1), :, :].rearrange("p a k s -> p (a k) s"), ALU.mult, ALU.subtract).then_inc(w_set, 1)

                def fill_pads(g):
                    fill = m_cnt[:, :].unsqueeze(2).to_broadcast([P, GT, WINDOW])
                    v.scalar_tensor_tensor(pad01, iota_lane[:, 0:WINDOW].unsqueeze(1).to_broadcast([P, GT, WINDOW]), float(KS - WINDOW), fill,
                                           ALU.add, ALU.is_lt).then_inc(sel_small, 1)
                    v.tensor_scalar(off[:, :], m_cnt[:, :], -float(KS - WINDOW // 2), None, ALU.add).then_inc(sel_small, 1)
                    hold(dve, sel_small, g * 6 + 1)
                    v.tensor_scalar(pad_neg, pad01, -1.0, FLT_MAX, ALU.add, ALU.mult).then_inc(sel_small, 1)
                    hold(dve, sel_small, g * 6 + 2)
                    v.tensor_tensor(off[:, :], off[:, :], off[:, :], ALU.mult).then_inc(sel_small, 1)
                    hold(dve, sel_small, g * 6 + 3)
                    v.scalar_tensor_tensor(pad01, pad01, FLT_MAX, pad_neg, ALU.mult, ALU.add).then_inc(sel_small, 1)
                    hold(dve, sel_small, g * 6 + 4)
                    v.tensor_reduce(off_max[:, ds(g, 1)], off[:, :], AX.X, ALU.max).then_inc(sel_small, 1)
                    hold(dve, sel_small, g * 6 + 5)
                    hold(dve, w_set, g * 2 + 6)

                def take(n_before, pads, part, tiles=range(GT)):
                    for i in tiles:
                        if i % 4 == 0:
                            hold(dve, (round_rep, round_max)[part], n_before + i + 4)
                        if part == 0:
                            v.max(top8[:, i, :], w[:, i, pads:]).then_inc(round_max, 1)
                        else:
                            v.match_replace(w[:, i, pads:], top8[:, i, :], w[:, i, pads:], -FLT_MAX).then_inc(round_rep, 1)

                def plus_eps(q, n, var_done, done):
                    dve.wait_ge(var_done, n)
                    v.tensor_scalar(ve[:, q, :], bank[VAR[q % 2]][:, 0:TPC], EPS, None, ALU.add).then_inc(done, 1)

                def scale(q, n, bc_done, done):
                    dve.wait_ge(bc_done, n)
                    v.tensor_tensor(chunk(yn, q), chunk(H, q), bank[BC[q % 2]][:, :], ALU.mult).then_inc(done, 1)

                dve.sem_inc(counted, 1)
                dve.sem_inc(mask_done, 2)
                dve.sem_inc(round_rep, GT)
                dve.sem_inc(w_set, 4)
                dve.sem_inc(t0_set, 1)
                for q in range(CH):
                    plus_eps(q, q + 1, var1, ve1)
                for q in range(CH):
                    scale(q, q + 1, bc1, yn1)
                def layer(l):
                    back = not isinstance(l, int) or l > 0
                    rounds = not isinstance(l, int)
                    base = l * CH
                    cos_l = cos_t[:, ds(l, 1), :].to_broadcast([P, BPC, S])
                    hold(dve, yn1, base + CH)
                    v.tensor_copy(cur[:, :], layer_par[:, ds(l, 1), :].rearrange("p a k -> p (a k)")).then_inc(cur_set, 1)
                    dve.wait_ge(cur_set, l + 1)
                    v.tensor_scalar(cs, center[:, :], cur[:, SCL:SCL + 1], None, ALU.mult).then_inc(cs_set, 1)
                    if rounds:
                        take(((l - 2) * QUICK + 1) * GT, 0, 0, range(8, 16))
                    rho = cur[:, RHO:RHO + 1].to_broadcast([P, S])

                    def turn_in(q):
                        hold(dve, act1, base + q + 1)
                        v.tensor_tensor(by_seq(a_buf, q), by_seq(yn, q), cos_l, ALU.mult).then_inc(a_in, 1)

                    def scan(q):
                        dve.wait_ge(a_in, base + q + 1)
                        dve.wait_ge(b_in, base + q + 1)
                        for b in range(BPC):
                            for buf, first in ((a_buf, UR0), (b_buf, UI0)):
                                part = buf[:, q * CW + b * S:q * CW + (b + 1) * S]
                                sc = v.tensor_tensor_scan(part, rho, part, cur[:, first:first + 1], ALU.mult, ALU.add)
                        sc.then_inc(scanned, 1)

                    def turn_out(q):
                        hold(dve, scanned, base + q + 1)
                        v.tensor_tensor(by_seq(a_buf, q), by_seq(a_buf, q), cos_l, ALU.mult).then_inc(a_out, 1)

                    def middle(q):
                        dve.wait_ge(z_mm, base + q + 1)
                        v.tensor_tensor(chunk(H, q), chunk(H, q), bank[ZO[q % 2]][:, :], ALU.add).then_inc(h_mid, 1)

                    def last(q):
                        dve.wait_ge(o_mm, base + q + 1)
                        v.scalar_tensor_tensor(chunk(H, q), bank[ZO[q % 2]][:, :], cur[:, B2:B2 + 1], chunk(H, q), ALU.add, ALU.add).then_inc(h_out, 1)

                    turn_in(0)
                    turn_in(1)
                    scan(0)
                    dve.wait_ge(w1_u, l + 1)
                    v.tensor_scalar(w1s, bank[PREP][:, :], cur[:, LN2W:LN2W + 1], None, ALU.mult).then_inc(w1_s, 1)
                    turn_in(2)
                    turn_out(0)
                    scan(1)
                    turn_in(3)
                    turn_out(1)
                    scan(2)
                    dve.wait_ge(b1_mm, l + 1)
                    v.tensor_tensor(b1f, bank[SMALL][:, 32:32 + FT], cur[:, B1:B1 + FT], ALU.add).then_inc(b1_set, 1)
                    scan(3)
                    turn_out(2)
                    turn_out(3)
                    middle(0)
                    stats(l, 0)
                    middle(1)
                    stats(l, 4)
                    middle(2)
                    stats(l, 8)
                    plus_eps(0, base + 1, var2, ve2)
                    middle(3)
                    stats(l, 12)
                    plus_eps(1, base + 2, var2, ve2)
                    means(l)
                    scale(0, base + 1, bc2, yn2)
                    plus_eps(2, base + 3, var2, ve2)
                    if rounds:
                        take(((l - 2) * QUICK + 1) * GT, 0, 1, range(0, 8))
                    scale(1, base + 2, bc2, yn2)
                    if rounds:
                        take(((l - 2) * QUICK + 1) * GT, 0, 1, range(8, 16))
                    if back:
                        counts(l - 1, 0)
                    last(0)
                    plus_eps(3, base + 4, var2, ve2)
                    scale(2, base + 3, bc2, yn2)
                    if back:
                        counts(l - 1, 1)
                        without_under(l - 1)
                    last(1)
                    scale(3, base + 4, bc2, yn2)
                    plus_eps(0, base + CH + 1, var1, ve1)
                    if back:
                        fill_pads(l - 1)
                        take((l - 1) * QUICK * GT, 0, 0, range(0, 12))
                    last(2)
                    plus_eps(1, base + CH + 2, var1, ve1)
                    scale(0, base + CH + 1, bc1, yn1)
                    if back:
                        take((l - 1) * QUICK * GT, 0, 0, range(12, 16))
                        take((l - 1) * QUICK * GT, 0, 1)
                    last(3)
                    plus_eps(2, base + CH + 3, var1, ve1)
                    scale(1, base + CH + 2, bc1, yn1)
                    if back:
                        take(((l - 1) * QUICK + 1) * GT, 0, 0, range(0, 4))
                    plus_eps(3, base + CH + 4, var1, ve1)
                    scale(2, base + CH + 3, bc1, yn1)
                    if back:
                        take(((l - 1) * QUICK + 1) * GT, 0, 0, range(4, 8))
                    scale(3, base + CH + 4, bc1, yn1)

                layer(0)
                layer(1)
                with dve.Fori(2, NL) as l:
                    layer(l)
                g = NG - 1
                take(((g - 1) * QUICK + 1) * GT, 0, 0, range(8, 16))
                take(((g - 1) * QUICK + 1) * GT, 0, 1)
                for u in range(2):
                    counts(g, u)
                without_under(g)
                fill_pads(g)
                for r in range(QUICK):
                    for part in range(2):
                        take((g * QUICK + r) * GT, 0, part)
                hold(dve, sel_small, NG * 6)
                v.tensor_reduce(off_one, off_max, AX.X, ALU.max).then_inc(sel_small, 1)
                hold(dve, sel_small, NG * 6 + 1)
                v.tensor_scalar(off_any, off_one, float((WINDOW // 2) ** 2), None, ALU.is_gt).then_inc(off_set, 1)
                hold(dve, off_mm, 1)
                v.tensor_copy(off_i[:, :], bank[0][:, 0:1]).then_inc(sel_small, 1)


        free = TPC * D
        cin_all = Xf[:, free:free + CT * D].rearrange("p (h l) -> p h l", h=CT)
        WA = S + PADS
        w_all = Xf[:, free + CT * D:free + CT * D + KD * WA].rearrange("p (i s) -> p i s", i=KD)
        assert free + CT * D + KD * WA <= 3 * free
        top_all = Xf[:, 3 * free:3 * free + KD * 8].rearrange("p (i s) -> p i s", i=KD)
        all_in, all_tp, all_w, all_max, all_rep, all_mask = (sem(n) for n in ("all_in", "all_tp", "all_w", "all_max", "all_rep", "all_mask"))

        with nc.Block() as block:
            @block.sync
            def _(sp):
                missed = sp.value_load(off_i[0:1, 0:1], min_val=0, max_val=P)
                with sp.If(missed > 0):
                    sp.sem_inc(all_tp, 1)
                    with sp.Fori(0, B) as b:
                        sp.wait_ge(all_tp, b + 1)
                        sp.dma_start(cin_all, ctx_map[ds(b, 1), :, :].rearrange("a (h p) l -> p (a h) l", p=P)).then_inc(all_in, 16)

            @block.tensor
            def _(pe):
                missed = pe.value_load(off_i[0:1, 0:1], min_val=0, max_val=P)
                with pe.If(missed > 0):
                    with pe.Fori(0, B) as b:
                        pe.wait_ge(all_in, b * 16 + 16)
                        pe.wait_ge(all_w, b * 5 + 1)
                        for k in range(KD):
                            for h in range(CT):
                                mm = nc.tensor.transpose(bank[k // 2][:, (k % 2) * S + h * P:(k % 2) * S + (h + 1) * P],
                                                         cin_all[:, h, k * P:(k + 1) * P], ident[:, :])
                        mm.then_inc(all_tp, 1)

            @block.vector
            def _(dve):
                v = nc.vector
                missed = dve.value_load(off_i[0:1, 0:1], min_val=0, max_val=P)
                with dve.If(missed > 0):
                    dve.sem_inc(all_w, 1)
                    dve.sem_inc(all_mask, 1)
                    dve.sem_inc(all_rep, KD)
                    with dve.Fori(0, B) as b:
                        hold(dve, all_mask, b + 1)
                        v.memset(w_all[:, :, 0:PADS], FLT_MAX).then_inc(all_w, 1)
                        hold(dve, all_tp, b + 2)
                        for j in range(4):
                            v.tensor_scalar(w_all[:, 2 * j:2 * j + 2, PADS:WA], bank[j][:, :].rearrange("p (k s) -> p k s", k=2)[:, :, ::-1],
                                            -1.0, None, ALU.mult).then_inc(all_w, 1)
                        hold(dve, all_w, b * 5 + 6)
                        with dve.Fori(0, ROUNDS) as r:
                            n = (b * ROUNDS + r) * KD
                            for i in range(KD):
                                hold(dve, all_rep, n + i + 1)
                                v.max(top_all[:, i, :], w_all[:, i, :]).then_inc(all_max, 1)
                            for i in range(KD):
                                hold(dve, all_max, n + i + 1)
                                v.match_replace(w_all[:, i, :], top_all[:, i, :], w_all[:, i, :], -FLT_MAX).then_inc(all_rep, 1)
                        hold(dve, all_rep, b * (ROUNDS * KD) + (ROUNDS + 1) * KD)
                        v.tensor_scalar(M[:, :, ds(b * S, S)], w_all[:, :, PADS:WA][:, :, ::-1], -FLT_MAX, None, ALU.is_gt).then_inc(all_mask, 1)

        UN = TPC
        KU = KD // 2
        ring = [nat[:, 2 + u, :] for u in range(2)]
        crux = [H[:, u * KU * S:(u + 1) * KU * S].rearrange("p (k s) -> p k s", k=KU) for u in range(2)]
        rest = fin[:, :, :].rearrange("p a n -> p (a n)").rearrange("p (k s) -> p k s", k=KU)
        pooled = ewide[:, 0:4 * KD * B].rearrange("p (m i k b) -> p m i k b", m=2, i=2, k=KD)
        logits = sb("logits", [P, NT, E])
        assert E == KD
        totals = logits[:, :, :].rearrange("p t e -> p (t e)").rearrange("p (k t) -> p k t", k=KD)
        spill = sb("spill", [P, KU // 2, S], BF16)
        junk = [bank[1][:, k * S:(k + 1) * S] for k in range(KU // 2)] + [spill[:, k, :] for k in range(KU // 2)]
        x1_tp, x1_tpev = (sem(n) for n in ("x1_tp", "x1_tpev"))
        cr_mul, cr_max, cr_sum, re_sub, re_max, av_set = (sem(n) for n in ("cr_mul", "cr_max", "cr_sum", "re_sub", "re_max", "av_set"))

        def unit(buf, q, j):
            return buf[:, (j % 2) * KU:(j % 2 + 1) * KU, ds(q * CW + (j // 2) * S, S)]

        def pool_at(m, i, q, j):
            return pooled[:, m, i, (j % 2) * KU:(j % 2 + 1) * KU, ds(q * BPC + j // 2, 1)].rearrange("p k b -> p (k b)")

        with nc.Block() as block:
            @block.sync
            def _(sp):
                with sp.Fori(1, CH) as q:
                    for u in range(TPC):
                        sp.wait_ge(x1_done, q * 8 + 2 * u + 2)
                        load_row(sp, q, u)

            @block.gpsimd
            def _(pool):
                def others(q, j):
                    pool.wait_ge(cr_mul, q * UN + j + 1)
                    hold(pool, re_max, q * UN + j + 1)
                    nc.gpsimd.tensor_tensor(rest, unit(T, q, j), crux[j % 2], ALU.subtract).then_inc(re_sub, 1)

                def tiles(q):
                    for u in range(TPC):
                        ln_pow(pool, u, q * TPC + u + NT + 1)
                        if not isinstance(q, int) or q > 0:
                            others(q - 1, u)
                        if not isinstance(q, int) or q < CH - 1 or u < TPC - AHEAD:
                            add_bias(pool, q + (u + AHEAD) // TPC, (u + AHEAD) % TPC)

                tiles(0)
                with pool.Fori(1, CH - 1) as q:
                    tiles(q)
                tiles(CH - 1)
                for j in range(UN):
                    others(CH - 1, j)

            @block.scalar
            def _(act):
                a = nc.scalar

                def sums(q, j):
                    hold(act, cr_mul, q * UN + j + 1)
                    hold(act, cr_sum, q * UN + j + 2)
                    for k in range(KU):
                        ins = a.activation(junk[k], crux[j % 2][:, k, :], ACT.Copy,
                                           accum_out=pooled[:, 1, 0, (j % 2) * KU + k, ds(q * BPC + j // 2, 1)])
                    ins.then_inc(cr_sum, 1)

                def tiles(q, pools):
                    for u in range(TPC):
                        if pools:
                            sums(q - 1, u)
                        for h in range(2):
                            act.wait_ge(x1_tp, q * 8 + 2 * u + h + 5)
                            for j in range(4):
                                ins = a.activation(T[:, 4 * h + j, ds(q * CW + u * P, P)], bank[6 + h][:, j * P:(j + 1) * P], ACT.Copy,
                                                   accum_out=totals[:, 4 * h + j, ds(q * TPC + u, 1)])
                            ins.then_inc(x1_tpev, 1)
                        if not isinstance(q, int) or q < CH - 1 or u < 2:
                            rows(act, q + (u + 2) // TPC, (u + 2) % TPC)

                act.sem_inc(x1_tpev, 2)
                act.sem_inc(cr_sum, 2)
                tiles(0, False)
                with act.Fori(1, CH - 1) as q:
                    tiles(q, True)
                tiles(CH - 1, True)
                for j in range(UN):
                    sums(CH - 1, j)

            @block.tensor
            def _(pe):
                def turned(q, u):
                    pe.wait_ge(ln_out, q * TPC + u + NT + 1)
                    for h in range(2):
                        pe.wait_ge(x1_tpev, q * 8 + 2 * u + h + 1)
                        for j in range(4):
                            k = 4 * h + j
                            mm = nc.tensor.transpose(bank[6 + h][:, j * P:(j + 1) * P], ring[u % 2][:, k * P:(k + 1) * P], ident[:, :])
                        mm.then_inc(x1_tp, 1)

                for t in range(NT + 2):
                    if 2 <= t < NT:
                        products(pe, *divmod(t, TPC))
                    if t >= 2:
                        turned(*divmod(t - 2, TPC))

            @block.vector
            def _(dve):
                v = nc.vector

                def largest(src, i, q, j, done):
                    v.tensor_reduce(pool_at(0, i, q, j), src, AX.X, ALU.max).then_inc(done, 1)

                def crucial(q, j):
                    hold(dve, x1_tpev, q * 8 + 10)
                    hold(dve, cr_sum, q * UN + j + 1)
                    hold(dve, cr_max, q * UN + j + 1)
                    v.tensor_tensor(crux[j % 2], unit(T, q, j), unit(M, q, j), ALU.mult).then_inc(cr_mul, 1)

                def maxima(q, j):
                    dve.wait_ge(cr_mul, q * UN + j + 1)
                    largest(crux[j % 2], 0, q, j, cr_max)
                    dve.wait_ge(re_sub, q * UN + j + 1)
                    largest(rest, 1, q, j, re_max)

                def normed(q, u):
                    hold(dve, x1_tp, q * 8 + 2 * u + 2)
                    ln_apply(dve, ring[u % 2], row_of(q, u), u, q * TPC + u + NT + 1)

                def tiles(q):
                    pools = not isinstance(q, int) or q > 0
                    late = not isinstance(q, int) or q > 1
                    for u in range(TPC):
                        if u > 0 or pools:
                            normed(q - (u == 0), (u - 1) % TPC)
                        if u == 0 and late:
                            maxima(q - 2, UN - 1)
                        if u > 0 and pools:
                            crucial(q - 1, u)
                        hold(dve, x1_done, q * 8 + 2 * u + 10)
                        ln_stats(dve, row_of(q, u), u, q * TPC + u + NT + 1)
                        if pools:
                            if u == 0:
                                crucial(q - 1, u)
                            else:
                                maxima(q - 1, u - 1)

                dve.sem_inc(x1_tp, 4)
                dve.sem_inc(cr_max, 2)
                dve.sem_inc(re_max, 1)
                tiles(0)
                tiles(1)
                with dve.Fori(2, CH) as q:
                    tiles(q)
                normed(CH - 1, TPC - 1)
                maxima(CH - 2, UN - 1)
                crucial(CH - 1, 0)
                for j in range(UN):
                    if j + 1 < UN:
                        crucial(CH - 1, j + 1)
                    maxima(CH - 1, j)
                avg = [pooled[:, 1, i, :, :] for i in range(2)]
                dve.wait_ge(x1_tpev, 2 * NT + 2)
                dve.wait_ge(cr_sum, NT + 2)
                v.tensor_reduce(avg[1].rearrange("p k b -> p b k"), totals[:, :, :].rearrange("p k (b h) -> p b k h", h=CT),
                                AX.X, ALU.add).then_inc(av_set, 1)
                dve.wait_ge(av_set, 1)
                v.tensor_tensor(avg[1], avg[1], avg[0], ALU.subtract).then_inc(av_set, 1)
                dve.wait_ge(av_set, 2)
                for i, n in enumerate((KC, KS)):
                    v.tensor_scalar(avg[i], avg[i], 1.0 / n, None, ALU.mult).then_inc(av_set, 1)

        lo = 0

        def in_late(*shape):
            nonlocal lo
            n = 1
            for s in shape:
                n *= s
            lo += n
            flat = late[:, lo - n:lo]
            names = "abcd"[:len(shape)]
            return flat.rearrange(f"p ({' '.join(names)}) -> p {' '.join(names)}", **dict(zip(names, shape)))

        z = in_late(2, KD * B)
        zz = in_late(2, KD * B)
        gsum = in_late(2)
        gmean = in_late(2)
        gvar = in_late(2)
        grs = in_late(2)
        g_dve, g_pe, g_pool, g_act = (sem(n) for n in ("g_dve", "g_pe", "g_pool", "g_act"))
        CNT = D * B

        with nc.Block() as block:
            @block.tensor
            def _(pe):
                pin = pooled[:, :, :, :, :].rearrange("p m i k b -> p m i (k b)")
                zb = bank[0][:, 0:2 * KD * B].rearrange("p (i n) -> p i n", i=2)
                edge = B
                for c in range(2):
                    nc.tensor.matmul(zb[:, :, :], band[:, c, P:2 * P], pin[:, c, :, :], start=(c == 0), stop=False, skip_group_check=True)
                for c in range(2):
                    for i in range(2):
                        nc.tensor.matmul(zb[:, i, edge:], band[:, c, 2 * P:3 * P], pin[:, c, i, 0:KD * B - edge], start=False, stop=False, skip_group_check=True)
                        mm = nc.tensor.matmul(zb[:, i, 0:KD * B - edge], band[:, c, 0:P], pin[:, c, i, edge:], start=False, stop=(c == 1 and i == 1),
                                              skip_group_check=True)
                mm.then_inc(g_pe, 1)
                pe.wait_ge(g_dve, 2)
                nc.tensor.matmul(bank[1][:, 0:2], ones[:, :], gsum[:, :], start=True, stop=True).then_inc(g_pe, 1)
                pe.wait_ge(g_dve, 6)
                nc.tensor.matmul(bank[2][:, 0:2], ones[:, :], gsum[:, :], start=True, stop=True).then_inc(g_pe, 1)

            @block.gpsimd
            def _(pool):
                pool.wait_ge(g_dve, 7)
                nc.gpsimd.tensor_tensor(grs[:, :], gvar[:, :], neg_half[:, 0:2], ALU.pow).then_inc(g_pool, 1)

            @block.scalar
            def _(act):
                act.wait_ge(g_dve, 10)
                nc.scalar.activation(z[:, :, :], z[:, :, :], ACT.Sigmoid).then_inc(g_act, 1)

            @block.vector
            def _(dve):
                v = nc.vector
                n_link = [0]

                def link(ins):
                    n_link[0] += 1
                    ins.then_inc(g_dve, 1)
                    dve.wait_ge(g_dve, n_link[0])

                dve.wait_ge(g_pe, 1)
                link(v.tensor_copy(z[:, :, :], bank[0][:, 0:2 * KD * B].rearrange("p (i n) -> p i n", i=2)))
                link(v.tensor_reduce(gsum[:, :], z[:, :, :], AX.X, ALU.add))
                dve.wait_ge(g_pe, 2)
                link(v.tensor_scalar(gmean[:, :], bank[1][:, 0:2], 1.0 / CNT, None, ALU.mult))
                link(v.tensor_tensor(z[:, :, :], z[:, :, :], gmean[:, :].unsqueeze(2).to_broadcast([P, 2, KD * B]), ALU.subtract))
                link(v.tensor_tensor(zz[:, :, :], z[:, :, :], z[:, :, :], ALU.mult))
                link(v.tensor_reduce(gsum[:, :], zz[:, :, :], AX.X, ALU.add))
                dve.wait_ge(g_pe, 3)
                link(v.tensor_scalar(gvar[:, :], bank[2][:, 0:2], 1.0 / CNT, EPS, ALU.mult, ALU.add))
                dve.wait_ge(g_pool, 1)
                link(v.tensor_tensor(z[:, :, :], z[:, :, :], grs[:, :].unsqueeze(2).to_broadcast([P, 2, KD * B]), ALU.mult))
                link(v.tensor_scalar(z[:, :, :], z[:, :, :], bn_gb[:, 0:1], bn_gb[:, 1:2], ALU.mult, ALU.add))
                link(v.tensor_scalar(z[:, :, :], z[:, :, :], 0.0, None, ALU.max))
                dve.wait_ge(g_act, 1)
                link(v.tensor_tensor(z[:, 0, :], z[:, 0, :], z[:, 1, :], ALU.subtract))

        gsel = [natf[:, u * N:(u + 1) * N].rearrange("p (k s) -> p k s", k=KD) for u in range(2)]
        nring = [H[:, u * D:(u + 1) * D] for u in range(2)]
        xt = [fin[:, :, :].rearrange("p a n -> p (a n)").rearrange("p (k n) -> p k n", k=KD),
              late[:, D:2 * D].rearrange("p (k n) -> p k n", k=KD)]
        assert lo <= D
        wslot = Tf.rearrange("p (w k n) -> p w k n", w=2, k=KD)
        out_init = sem("out_init")
        w_in_sem = [sem(f"w_in{w}") for w in range(2)]
        nrm_st = [sem(f"nrm_st{u}") for u in range(2)]
        gmul, gm_done, back_mm, x2_done = (sem(n) for n in ("gmul", "gm_done", "back_mm", "x2_done"))
        l_tp, l_tpev, l_mm, logits_out = (sem(n) for n in ("l_tp", "l_tpev", "l_mm", "logits_out"))

        def expert_src(e):
            return expert_w[e, :, :].rearrange("(k p) n -> p k n", p=P)

        def peeled(body):
            def run(eng):
                for b in range(2):
                    body(b, b)
                with eng.Fori(1, B // 2 - 1) as i:
                    for s_ in range(2):
                        body(i * 2 + s_, s_)
                for b in range(B - 2, B):
                    body(b, b % 2)
            return run

        with nc.Block() as block:
            @block.sync
            def _(sp):
                with sp.Fori(0, B) as b:
                    for h in range(CT):
                        t = b * CT + h
                        sp.wait_ge(x2_done, t * 2 + 6)
                        sp.dma_start(out[ds(t * P, P), :], X[:, ds(t, 1), :].rearrange("p a d -> p (a d)")).then_inc(out_init, 16)
                        sp.wait_ge(ln_out, t + 2 * NT + 1)
                        sp.dma_start(x_nrm[ds(t * P, P), :], nring[h]).then_inc(nrm_st[h], 16)
                sp.dma_start(out[N:N + P, :], X[:, 0, :]).then_inc(out_init, 16)
                sp.wait_ge(gm_done, 2 * B)
                for w in range(2):
                    sp.dma_start(wslot[:, w, :, :], expert_src(w)).then_inc(w_in_sem[w], 16)

            @block.gpsimd
            def _(pool):
                def gated(b, par, h):
                    hold(pool, gmul, b + 1)
                    part = gsel[par][:, h * KU:(h + 1) * KU, :]
                    nc.gpsimd.tensor_tensor(part, part, T[:, h * KU:(h + 1) * KU, ds(b * S, S)], ALU.mult).then_inc(gm_done, 1)

                def step(b, par):
                    for h in range(2):
                        if not isinstance(b, int) or b < B - 1:
                            gated(b + 1, 1 - par, h)
                        ln_pow(pool, 2 * par + h, b * CT + h + 2 * NT + 1)

                for h in range(2):
                    gated(0, 0, h)
                peeled(step)(pool)

            @block.scalar
            def _(act):
                a = nc.scalar

                def gates_of(b, par):
                    hold(act, back_mm, b * 2 + 2)
                    for k in range(KD):
                        ins = a.activation(gsel[par][:, k, :], M[:, k, ds(b * S, S)], ACT.Identity,
                                           scale=z[:, 0, ds(k * B + b, 1)], bias=z[:, 1, ds(k * B + b, 1)])
                    ins.then_inc(gmul, 1)

                def copies(b, h):
                    t = b * CT + h
                    act.wait_ge(l_mm, t + 1)
                    for n in range(2):
                        act.wait_ge(l_tp, t * 2 + n + 5)
                        a.copy(xt[h][:, 4 * n:4 * n + 4, :], bank[4 + n][:, :].rearrange("p (k n) -> p k n", k=4)).then_inc(l_tpev, 1)

                def step(b, par):
                    if not isinstance(b, int) or b > 0:
                        copies(b - 1, 0)
                    if not isinstance(b, int) or b < B - 2:
                        gates_of(b + 2, par)
                    if not isinstance(b, int) or b > 0:
                        copies(b - 1, 1)

                act.sem_inc(back_mm, 4)
                act.sem_inc(l_tpev, 2)
                gates_of(0, 0)
                gates_of(1, 1)
                peeled(step)(act)
                for h in range(CT):
                    copies(B - 1, h)

            @block.tensor
            def _(pe):
                def back(b, par):
                    pe.wait_ge(gm_done, b * 2 + 2)
                    for h in range(CT):
                        pe.wait_ge(x2_done, (b * CT + h) * 2 + 2)
                        for k in range(KD):
                            mm = nc.tensor.transpose(bank[2 * h + k // 4][:, (k % 4) * P:(k % 4 + 1) * P], gsel[par][:, k, h * P:(h + 1) * P], ident[:, :])
                        mm.then_inc(back_mm, 1)

                def forth(b, h):
                    t = b * CT + h
                    pe.wait_ge(ln_out, t + 2 * NT + 1)
                    for n in range(2):
                        pe.wait_ge(l_tpev, t * 2 + n + 1)
                        for j in range(4):
                            k = 4 * n + j
                            mm = nc.tensor.transpose(bank[4 + n][:, j * P:(j + 1) * P], nring[h][:, k * P:(k + 1) * P], ident[:, :])
                        mm.then_inc(l_tp, 1)

                def gate_logits(b, h):
                    t = b * CT + h
                    pe.wait_ge(l_tpev, t * 2 + 4)
                    for k in range(KD):
                        mm = nc.tensor.matmul(bank[6][:, ds(t * E, E)], xt[h][:, k, :], gate[:, k, :], start=(k == 0), stop=(k == KD - 1))
                    mm.then_inc(l_mm, 1)

                def step(b, par):
                    back(b, par)
                    if not isinstance(b, int) or b > 0:
                        forth(b - 1, 0)
                        if not isinstance(b, int) or b > 1:
                            gate_logits(b - 2, 1)
                        forth(b - 1, 1)
                        gate_logits(b - 1, 0)

                pe.sem_inc(l_mm, 2)
                peeled(step)(pe)
                forth(B - 1, 0)
                gate_logits(B - 2, 1)
                forth(B - 1, 1)
                for h in range(CT):
                    gate_logits(B - 1, h)

            @block.vector
            def _(dve):
                v = nc.vector

                def row_at(t):
                    return X[:, ds(t, 1), :].rearrange("p a d -> p (a d)")

                def residual(b, par, h):
                    t = b * CT + h
                    hold(dve, back_mm, t + 5)
                    for n in range(2):
                        part = row_at(t)[:, n * BANK:(n + 1) * BANK]
                        v.tensor_tensor(part, part, bank[2 * h + n][:, :], ALU.add).then_inc(x2_done, 1)
                    hold(dve, x2_done, t * 2 + 6)
                    ln_stats(dve, row_at(t), 2 * par + h, t + 2 * NT + 1)

                def normed(b, par, h):
                    t = b * CT + h
                    dve.wait_ge(nrm_st[h], b * 16 + 16)
                    hold(dve, l_tp, t * 2 + 2)
                    ln_apply(dve, nring[h], row_at(t), 2 * par + h, t + 2 * NT + 1)

                def step(b, par):
                    residual(b, par, 0)
                    if not isinstance(b, int) or b > 0:
                        normed(b - 1, 1 - par, 1)
                    residual(b, par, 1)
                    normed(b, par, 0)

                for u in range(2):
                    dve.sem_inc(nrm_st[u], 16)
                dve.sem_inc(l_tp, 4)
                dve.sem_inc(x2_done, 4)
                peeled(step)(dve)
                normed(B - 1, 1, 1)
                dve.wait_ge(l_mm, NT + 2)
                v.tensor_copy(logits[:, :, :].rearrange("p t e -> p (t e)"), bank[6][:, 0:NT * E]).then_inc(logits_out, 1)

        Mf = M[:, :, :].rearrange("p k n -> p (k n)").bitcast(F32)
        xo = 0

        def small(*shape, dt=F32):
            nonlocal xo
            n = 1
            for s in shape:
                n *= s
            xo += n
            assert xo <= KD * N // 2
            flat = Mf[:, xo - n:xo]
            names = "abc"[:len(shape)]
            return (flat if dt == F32 else flat.bitcast(dt)).rearrange(f"p ({' '.join(names)}) -> p {' '.join(names)}", **dict(zip(names, shape)))

        best = small(2, NT)
        hot = small(2, NT, E)
        eq = small(NT, E)
        first = small(NT)
        masked = small(NT, E)
        either = small(NT, E)
        e2 = small(NT)
        prob = small(2, NT)
        tot = small(E, NT)
        upto = small(E, NT)
        full = small(E, NT)
        need = small(E)
        end = small(E)
        begin = small(E)
        place = small(NT, E)
        pos = small(2, NT)
        pos_i = small(2, NT, dt=I32)
        lane_i = small(2, NT, dt=I32)
        lane = small(2, NT)
        slot = small(2, NT)
        past = small(E, SLOTS)
        who = small(SLOTS)
        who_i = small(SLOTS, dt=I32)
        odd_i = small(SLOTS, dt=I32)
        ready_i = small(SLOTS, dt=I32)
        end_i = small(E, dt=I32)
        hot_lane = natf[:, 0:2 * NT * P].rearrange("p (k t l) -> p k t l", k=2, t=NT)
        hot_slot = [small(NT, 2, SLOTS) for _ in range(2)]
        at_slot = small(NT, SLOTS)
        tokp1 = small(SLOTS)
        pair_p = small(SLOTS)
        unused = small(SLOTS)
        tok_f = small(SLOTS)
        src_i = small(SLOTS, dt=U32)
        dst_i = small(SLOTS, dt=U32)
        r_dve, r_act, r_pe, hot_set = (sem(n) for n in ("r_dve", "r_act", "r_pe", "hot_set"))

        with nc.Block() as block:
            @block.scalar
            def _(act):
                act.wait_ge(r_dve, 13)
                nc.scalar.activation(e2[:, :], e2[:, :], ACT.Exp).then_inc(r_act, 1)

            @block.tensor
            def _(pe):
                pe.wait_ge(r_dve, 12)
                nc.tensor.matmul(bank[0][:, 0:NT * E], utri[:, :], either[:, :, :].rearrange("p t e -> p (t e)"), start=True, stop=True)
                nc.tensor.matmul(bank[1][:, 0:NT * E], ones[:, :], either[:, :, :].rearrange("p t e -> p (t e)"), start=True, stop=True).then_inc(r_pe, 1)
                for k in range(2):
                    pe.wait_ge(hot_set, k + 1)
                    for t in range(NT):
                        mm = nc.tensor.matmul(bank[2][:, 0:2 * SLOTS], hot_lane[:, k, t, :], hot_slot[k][:, t, :, :].rearrange("p a s -> p (a s)"),
                                              start=(k == 0 and t == 0), stop=(k == 1 and t == NT - 1))
                mm.then_inc(r_pe, 1)

            @block.vector
            def _(dve):
                v = nc.vector
                n_link = [0]

                def link(ins):
                    n_link[0] += 1
                    ins.then_inc(r_dve, 1)
                    dve.wait_ge(r_dve, n_link[0])

                def over_e(ap):
                    return ap.unsqueeze(2).to_broadcast([P, NT, E])

                link(v.tensor_reduce(best[:, 0, :], logits[:, :, :], AX.X, ALU.max))
                link(v.tensor_tensor(eq[:, :, :], logits[:, :, :], over_e(best[:, 0, :]), ALU.is_equal))
                link(v.tensor_tensor(eq[:, :, :], eq[:, :, :], rev_e[:, :, :], ALU.mult))
                link(v.tensor_reduce(first[:, :], eq[:, :, :], AX.X, ALU.max))
                link(v.tensor_tensor(hot[:, 0, :, :], eq[:, :, :], over_e(first[:, :]), ALU.is_equal))
                link(v.scalar_tensor_tensor(masked[:, :, :], hot[:, 0, :, :], -FLT_MAX, logits[:, :, :], ALU.mult, ALU.add))
                link(v.tensor_reduce(best[:, 1, :], masked[:, :, :], AX.X, ALU.max))
                link(v.tensor_tensor(eq[:, :, :], masked[:, :, :], over_e(best[:, 1, :]), ALU.is_equal))
                link(v.tensor_tensor(eq[:, :, :], eq[:, :, :], rev_e[:, :, :], ALU.mult))
                link(v.tensor_reduce(first[:, :], eq[:, :, :], AX.X, ALU.max))
                link(v.tensor_tensor(hot[:, 1, :, :], eq[:, :, :], over_e(first[:, :]), ALU.is_equal))
                link(v.tensor_tensor(either[:, :, :], hot[:, 0, :, :], hot[:, 1, :, :], ALU.add))
                assert n_link[0] == 12
                link(v.tensor_tensor(e2[:, :], best[:, 1, :], best[:, 0, :], ALU.subtract))
                dve.wait_ge(r_act, 1)
                link(v.tensor_scalar(prob[:, 0, :], e2[:, :], 1.0, None, ALU.add))
                link(v.reciprocal(prob[:, 0, :], prob[:, 0, :]))
                link(v.tensor_tensor(prob[:, 1, :], e2[:, :], prob[:, 0, :], ALU.mult))
                dve.wait_ge(r_pe, 1)
                link(v.tensor_copy(tot[:, :, :], bank[1][:, 0:NT * E].rearrange("p (t e) -> p e t", e=E)))
                link(v.tensor_tensor_scan(upto[:, :, :].rearrange("p e t -> p (e t)"), later_t[:, :], tot[:, :, :].rearrange("p e t -> p (e t)"),
                                          0.0, ALU.mult, ALU.add))
                link(v.tensor_tensor(full[:, :, :], step_t[:, :, :], upto[:, :, NT - 1:NT].to_broadcast([P, E, NT]), ALU.is_lt))
                link(v.tensor_reduce(need[:, :], full[:, :, :], AX.X, ALU.add))
                link(v.tensor_tensor_scan(end[:, :], ones[:, 0:E], need[:, :], 0.0, ALU.mult, ALU.add))
                link(v.tensor_tensor(begin[:, :], end[:, :], need[:, :], ALU.subtract))
                link(v.tensor_tensor(upto[:, :, :], upto[:, :, :], tot[:, :, :], ALU.subtract))
                link(v.scalar_tensor_tensor(upto[:, :, :], begin[:, :].unsqueeze(2).to_broadcast([P, E, NT]), float(P), upto[:, :, :], ALU.mult, ALU.add))
                link(v.tensor_tensor(place[:, :, :], bank[0][:, 0:NT * E].rearrange("p (t e) -> p t e", e=E),
                                     upto[:, :, :].rearrange("p e t -> p t e"), ALU.add))
                for k in range(2):
                    link(v.tensor_tensor(eq[:, :, :], hot[:, k, :, :], place[:, :, :], ALU.mult))
                    link(v.tensor_reduce(pos[:, k, :], eq[:, :, :], AX.X, ALU.add))
                link(v.tensor_copy(pos_i[:, :, :], pos[:, :, :]))
                link(v.tensor_scalar(lane_i[:, :, :], pos_i[:, :, :], P - 1, None, ALU.bitwise_and))
                link(v.tensor_copy(lane[:, :, :], lane_i[:, :, :]))
                link(v.tensor_scalar(pos_i[:, :, :], pos_i[:, :, :], 7, None, ALU.logical_shift_right))
                link(v.tensor_copy(slot[:, :, :], pos_i[:, :, :]))
                link(v.tensor_tensor(past[:, :, :], iota_slot[:, :].unsqueeze(1).to_broadcast([P, E, SLOTS]),
                                     end[:, :].unsqueeze(2).to_broadcast([P, E, SLOTS]), ALU.is_ge))
                link(v.tensor_reduce(who[:, :], past[:, :, :].rearrange("p e s -> p s e"), AX.X, ALU.add))
                link(v.tensor_scalar(who[:, :], who[:, :], float(E - 1), None, ALU.min))
                link(v.tensor_copy(who_i[:, :], who[:, :]))
                link(v.tensor_scalar(odd_i[:, :], who_i[:, :], 1, None, ALU.bitwise_and))
                link(v.tensor_scalar(ready_i[:, :], who[:, :], 1.0, None, ALU.add))
                link(v.tensor_scalar(end_i[:, :], end[:, :], 1.0, None, ALU.add))
                for k in range(2):
                    v.tensor_tensor(hot_lane[:, k, :, :], iota_lane[:, :].unsqueeze(1).to_broadcast([P, NT, P]),
                                    lane[:, k, :].unsqueeze(2).to_broadcast([P, NT, P]), ALU.is_equal)
                    link(v.tensor_tensor(at_slot[:, :, :], iota_slot[:, :].unsqueeze(1).to_broadcast([P, NT, SLOTS]),
                                         slot[:, k, :].unsqueeze(2).to_broadcast([P, NT, SLOTS]), ALU.is_equal))
                    v.tensor_tensor(hot_slot[k][:, :, 0, :], at_slot[:, :, :], tok1[:, :].unsqueeze(2).to_broadcast([P, NT, SLOTS]), ALU.mult)
                    link(v.tensor_tensor(hot_slot[k][:, :, 1, :], at_slot[:, :, :], prob[:, k, :].unsqueeze(2).to_broadcast([P, NT, SLOTS]), ALU.mult))
                    dve.sem_inc(hot_set, 1)
                dve.wait_ge(r_pe, 2)
                link(v.tensor_copy(tokp1[:, :], bank[2][:, 0:SLOTS]))
                link(v.tensor_copy(pair_p[:, :], bank[2][:, SLOTS:2 * SLOTS]))
                link(v.tensor_scalar(unused[:, :], tokp1[:, :], 0.0, spare[:, 0:1], ALU.is_equal, ALU.mult))
                link(v.tensor_scalar(tok_f[:, :], tokp1[:, :], -1.0, 0.0, ALU.add, ALU.max))
                link(v.tensor_copy(src_i[:, :], tok_f[:, :]))
                link(v.tensor_tensor(tok_f[:, :], tokp1[:, :], unused[:, :], ALU.add))
                link(v.tensor_scalar(dst_i[:, :], tok_f[:, :], -1.0, None, ALU.add))

        ITER = SLOTS // IN_FLIGHT - 1
        LAST = range(ITER * IN_FLIGHT, SLOTS)
        xg = [Xf[:, u * D:(u + 1) * D] for u in range(IN_FLIGHT)]
        xgt = [Xf[:, (3 + u) * D:(4 + u) * D].rearrange("p (k n) -> p k n", k=KD) for u in range(IN_FLIGHT)]
        yv = [Xf[:, (6 + u) * D:(7 + u) * D] for u in range(IN_FLIGHT)]
        col_s = [sb(f"col_s{u}", [P, 1], U32) for u in range(IN_FLIGHT)]
        col_d = [sb(f"col_d{u}", [P, 1], U32) for u in range(IN_FLIGHT)]
        col_p = [sb(f"col_p{u}", [P, 1]) for u in range(IN_FLIGHT)]
        xg_in = [sem(f"xg_in{u}") for u in range(IN_FLIGHT)]
        src_set, cols_set, xg_tp, xg_tpev, y_mm, y_act, y_dve, y_out, w_ready, tile_mm = (sem(n) for n in (
            "src_set", "cols_set", "xg_tp", "xg_tpev", "y_mm", "y_act", "y_dve", "y_out", "w_ready", "tile_mm"))

        with nc.Block() as block:
            @block.sync
            def _(sp):
                for w in range(2):
                    sp.wait_ge(w_in_sem[w], 16)
                    sp.sem_inc(w_ready, 1)
                with sp.Fori(0, E // 2 - 1) as i:
                    for w in range(2):
                        used = sp.value_load(end_i[0:1, ds(i * 2 + w, 1)], min_val=1, max_val=SLOTS + 1)
                        sp.wait_ge(tile_mm, used)
                        sp.dma_start(wslot[:, w, :, :], expert_w[ds(i * 2 + w + 2, 1), :, :].rearrange("a (k p) n -> p (a k) n", p=P)).then_inc(w_in_sem[w], 16)
                    for w in range(2):
                        sp.wait_ge(w_in_sem[w], i * 16 + 32)
                        sp.sem_inc(w_ready, 1)

            @block.gpsimd
            def _(pool):
                g = nc.gpsimd

                def gather(j, u):
                    pool.wait_ge(src_set, j + 1)
                    hold(pool, xg_tp, j * 2 + 2)
                    g.indirect_dma_start(out=xg[u], out_offset=None, in_=x_nrm[:, :],
                                         in_offset=bass.IndirectOffsetOnAxis(ap=col_s[u][:, 0:1], axis=0)).then_inc(xg_in[u], 16)

                def scatter(j, u, first=False):
                    pool.wait_ge(y_act, j + IN_FLIGHT + 1)
                    pool.wait_ge(y_dve, j + IN_FLIGHT + 1)
                    if not first:
                        pool.wait_ge(y_out, j * 16)
                    pool.sem_inc(held, 1)
                    g.indirect_dma_start(out=out[:, :], out_offset=bass.IndirectOffsetOnAxis(ap=col_d[u][:, 0:1], axis=0),
                                         in_=yv[u], in_offset=None, compute_op=ALU.add).then_inc(y_out, 16)

                for u in range(2):
                    pool.wait_ge(nrm_st[u], B * 16 + 16)
                pool.wait_ge(out_init, NT * 16 + 16)
                for u in range(IN_FLIGHT):
                    gather(u, u)
                for u in range(IN_FLIGHT):
                    gather(IN_FLIGHT + u, u)
                    scatter(u, u, first=u == 0)
                with pool.Fori(2, ITER) as i:
                    for u in range(IN_FLIGHT):
                        gather(i * IN_FLIGHT + u, u)
                        scatter(i * IN_FLIGHT + u - IN_FLIGHT, u)
                used = pool.value_load(end_i[0:1, E - 1:E], min_val=1, max_val=SLOTS + 1)
                for u, j in enumerate(LAST):
                    with pool.If(used > j + 1):
                        gather(j, u)
                    scatter(j - IN_FLIGHT, u)
                pool.wait_ge(y_out, LAST[0] * 16)
                for u, j in enumerate(LAST):
                    with pool.If(used > j + 1):
                        scatter(j, u)
                        pool.wait_ge(y_out, j * 16 + 16)

            @block.tensor
            def _(pe):
                def turned(i, u):
                    j = i * IN_FLIGHT + u
                    pe.wait_ge(xg_in[u], i * 16 + 16)
                    for h in range(2):
                        pe.wait_ge(xg_tpev, j * 2 + h + 1)
                        for c in range(4):
                            k = 4 * h + c
                            mm = nc.tensor.transpose(bank[6 + h][:, c * P:(c + 1) * P], xg[u][:, k * P:(k + 1) * P], ident[:, :])
                        mm.then_inc(xg_tp, 1)

                def products(i, u):
                    j = i * IN_FLIGHT + u
                    ready = pe.value_load(ready_i[0:1, ds(j, 1)], min_val=1, max_val=E)
                    odd = pe.value_load(odd_i[0:1, ds(j, 1)], min_val=0, max_val=1)
                    pe.wait_ge(w_ready, ready)
                    pe.wait_ge(xg_tpev, j * 2 + 4)
                    pe.wait_ge(y_act, j + 1)
                    pe.wait_ge(y_dve, j + 1)
                    for n in range(2):
                        for k in range(KD):
                            mm = nc.tensor.matmul(bank[2 * u + n][:, :], xgt[u][:, k, :],
                                                  Tf[:, ds(odd * (KD * D) + (k * D + n * BANK), BANK)], start=(k == 0), stop=(k == KD - 1))
                        mm.then_inc(y_mm if n == 0 else tile_mm, 1)

                pe.sem_inc(xg_tp, 6)
                pe.sem_inc(tile_mm, 1)
                turned(0, 0)
                with pe.Fori(0, ITER - 1) as i:
                    for u in range(IN_FLIGHT):
                        turned(i + (u + 1) // IN_FLIGHT, (u + 1) % IN_FLIGHT)
                        products(i, u)
                used = pe.value_load(end_i[0:1, E - 1:E], min_val=1, max_val=SLOTS + 1)
                for u in range(IN_FLIGHT):
                    if u + 1 < IN_FLIGHT:
                        turned(ITER - 1, u + 1)
                    products(ITER - 1, u)
                for u, j in enumerate(LAST):
                    with pe.If(used > j + 1):
                        turned(ITER, u)
                        products(ITER, u)

            @block.scalar
            def _(act):
                def copies(j, u):
                    for h in range(2):
                        act.wait_ge(xg_tp, j * 2 + h + 7)
                        nc.scalar.copy(xgt[u][:, 4 * h:4 * h + 4, :].rearrange("p k n -> p (k n)"), bank[6 + h][:, :]).then_inc(xg_tpev, 1)

                def first_half(j, u):
                    act.wait_ge(y_mm, j + 1)
                    act.wait_ge(cols_set, j + 1)
                    nc.scalar.activation(yv[u][:, 0:BANK], bank[2 * u][:, :], ACT.Copy, scale=col_p[u][:, 0:1]).then_inc(y_act, 1)

                act.sem_inc(xg_tpev, 2)
                act.sem_inc(y_act, IN_FLIGHT)
                copies(0, 0)
                with act.Fori(0, ITER - 1) as i:
                    for u in range(IN_FLIGHT):
                        copies(i * IN_FLIGHT + u + 1, (u + 1) % IN_FLIGHT)
                        first_half(i * IN_FLIGHT + u, u)
                used = act.value_load(end_i[0:1, E - 1:E], min_val=1, max_val=SLOTS + 1)
                for u in range(IN_FLIGHT):
                    j = LAST[0] - IN_FLIGHT + u
                    if u + 1 < IN_FLIGHT:
                        copies(j + 1, u + 1)
                    first_half(j, u)
                for u, j in enumerate(LAST):
                    with act.If(used > j + 1):
                        copies(j, u)
                        first_half(j, u)

            @block.vector
            def _(dve):
                v = nc.vector

                def sources(j, u):
                    v.tensor_copy(col_s[u][:, :], src_i[:, ds(j, 1)]).then_inc(src_set, 1)

                def columns(j, u):
                    v.tensor_copy(col_d[u][:, :], dst_i[:, ds(j, 1)])
                    v.tensor_copy(col_p[u][:, :], pair_p[:, ds(j, 1)]).then_inc(cols_set, 1)

                def second_half(j, u):
                    dve.wait_ge(cols_set, j + 1)
                    dve.wait_ge(tile_mm, j + 2)
                    v.tensor_scalar(yv[u][:, BANK:D], bank[2 * u + 1][:, :], col_p[u][:, 0:1], None, ALU.mult).then_inc(y_dve, 1)

                dve.sem_inc(y_dve, IN_FLIGHT)
                for u in range(IN_FLIGHT):
                    sources(u, u)
                    columns(u, u)
                with dve.Fori(0, ITER) as i:
                    for u in range(IN_FLIGHT):
                        j = i * IN_FLIGHT + u
                        dve.wait_ge(xg_tp, j * 2 + 8)
                        sources(j + IN_FLIGHT, u)
                        second_half(j, u)
                        dve.wait_ge(y_out, j * 16 + 16)
                        columns(j + IN_FLIGHT, u)
                used = dve.value_load(end_i[0:1, E - 1:E], min_val=1, max_val=SLOTS + 1)
                for u, j in enumerate(LAST):
                    with dve.If(used > j + 1):
                        second_half(j, u)


_INS = ['x', 'ctx_4096', 'L0_attn_Win', 'L0_attn_bin', 'L0_attn_ln1_w', 'L0_attn_ln1_b', 'L0_attn_phz_re', 'L0_attn_phz_im',
        'L0_attn_lc_re', 'L0_attn_lc_im', 'L0_attn_sc_lin', 'L0_attn_ln2_w', 'L0_attn_ln2_b', 'L0_attn_W1', 'L0_attn_b1',
        'L0_attn_W2', 'L0_attn_b2', 'L0_attn_lnl_w', 'L0_attn_lnl_b', 'L0_attn_Wout', 'L0_attn_bout', 'L0_xattn_conv_w',
        'L0_xattn_bn_gamma', 'L0_xattn_bn_beta', 'L0_ffn_gate_w', 'L0_ffn_expert_w']


def kernel(**inputs):
    import numpy as _np
    import concourse.bacc as _bacc
    from concourse import mybir as _mybir
    from concourse.bass_utils import run_bass_kernel_spmd as _run

    nc = _bacc.Bacc("TRN2", target_bir_lowering=False, num_devices=1)
    arrays, args = {}, []
    for name in _INS:
        a = _np.ascontiguousarray(inputs[name])
        arrays[f"in_{name}_dram"] = a
        args.append(nc.dram_tensor(f"in_{name}_dram", a.shape, _mybir.dt.from_np(a.dtype), kind="ExternalInput").ap())
    b, s, d = inputs["x"].shape
    res = nc.dram_tensor("out_0_dram", (b * s + 128, d), _mybir.dt.float32, kind="ExternalOutput").ap()
    decoder_kernel(nc, *args, res)
    r = _run(nc, [arrays], core_ids=[0])
    return r.results[0]["out_0_dram"][:b * s].reshape(b, s, d)
```
